# Optimizing a Trainium2 kernel written in Bass

```python
import numpy as np
import jax
import jax.numpy as jnp

def _softmax(x, axis=-1):
    return jax.nn.softmax(x, axis=axis)

def _gelu(x):
    return jax.nn.gelu(x, approximate=True)

def _silu(x):
    return jax.nn.silu(x)

def _sigmoid(x):
    return jax.nn.sigmoid(x)

def _layernorm(x, axis=-1, eps=1e-05):
    m = jnp.mean(x, axis=axis, keepdims=True)
    v = jnp.var(x, axis=axis, keepdims=True)
    return (x - m) / jnp.sqrt(v + eps)

def _scatter_add(tgt, idx, src, axis=0):
    return tgt.at[idx].add(src)

def _segment_sum(src, seg, n):
    return jax.ops.segment_sum(src, seg, n)
kernel_name = 'mk_gnn_ffn_d1_gnn_r8_b69f6c'

def setup_inputs(seed: int=0):
    np.random.seed(seed)
    _w = jnp.asarray

    def _rec_inputs():
        import jax
        import jax.numpy as jnp
        _gk = jax.random.key(seed)
        x = 3.789e-05 + 1 * jax.random.normal(jax.random.fold_in(_gk, 1), (6250, 256), jnp.float32)
        _s = jax.random.randint(jax.random.fold_in(_gk, 2), (50000,), 0, 6250, jnp.int32)
        _d = jax.random.randint(jax.random.fold_in(_gk, 3), (50000,), 0, 6250, jnp.int32)
        _loop = jnp.arange(6250, dtype=jnp.int32)
        src = jnp.concatenate([_s, _d, _loop])
        dst = jnp.concatenate([_d, _s, _loop])
        _o = jnp.argsort(dst, stable=True)
        src = src[_o]
        dst = dst[_o]
        edge_attr3_1x1 = jax.random.uniform(jax.random.fold_in(_gk, 12), (106250, 1, 1), jnp.float32, 0.0, 0.999998)
        return (x, src, dst, edge_attr3_1x1)
    x, src, dst, edge_attr3_1x1 = _rec_inputs()

    def _L0_gnn_setup():
        import jax, jax.numpy as jnp
        import numpy as np
        N, F_IN, H, OUT, E = (4000, 256, 4, 64, 64000)
        NEG_SLOPE = 0.2
        key = jax.random.key(seed)
        ks = jax.random.split(key, 7)
        return {'feat': jax.random.normal(ks[0], (N, F_IN), dtype=jnp.float32), 'dist': jax.random.uniform(ks[1], (E, 1, 1), dtype=jnp.float32), 'W': jax.random.normal(ks[2], (F_IN, H * OUT), dtype=jnp.float32) * (1.0 / np.sqrt(F_IN)), 'w_att_src': jax.random.normal(ks[3], (1, H, OUT), dtype=jnp.float32) * 0.1, 'w_att_dst': jax.random.normal(ks[4], (1, H, OUT), dtype=jnp.float32) * 0.1, 'src': jax.random.randint(ks[5], (E,), 0, N, dtype=jnp.int32), 'dst': jax.random.randint(ks[6], (E,), 0, N, dtype=jnp.int32)}
    _L0_gnn_all = _L0_gnn_setup()
    _L0_gnn_in = {k: v for k, v in _L0_gnn_all.items() if k in ('W', 'w_att_src', 'w_att_dst')}
    del _L0_gnn_all

    def _L0_ffn_setup():
        import jax, jax.numpy as jnp
        import numpy as np
        BN_EPS = 0.001

        def _bn(h, g, b, m, v):
            return g * (h - m) * jax.lax.rsqrt(v + BN_EPS) + b
        key = jax.random.key(seed)
        ks = jax.random.split(key, 8)
        B, F, Df = (256, 64, 256)
        E, H, D = (8, 256, 256)
        s1 = 1.0 / np.sqrt(Df)
        s2 = 1.0 / np.sqrt(H)
        return {'x': jax.random.normal(ks[0], (B, F, Df), jnp.float32), 'Wr': jax.random.normal(ks[1], (Df, E), jnp.float32) * s1, 'br': jnp.zeros((E,), jnp.float32), 'W1': jax.random.normal(ks[2], (E, Df, H), jnp.float32) * s1, 'b1': jnp.zeros((E, H), jnp.float32), 'g1': jnp.ones((E, H), jnp.float32), 'be1': jnp.zeros((E, H), jnp.float32), 'm1': jnp.zeros((E, H), jnp.float32), 'v1': jnp.ones((E, H), jnp.float32), 'W2': jax.random.normal(ks[3], (E, H, H), jnp.float32) * s2, 'b2': jnp.zeros((E, H), jnp.float32), 'g2': jnp.ones((E, H), jnp.float32), 'be2': jnp.zeros((E, H), jnp.float32), 'm2': jnp.zeros((E, H), jnp.float32), 'v2': jnp.ones((E, H), jnp.float32), 'Wo': jax.random.normal(ks[4], (E, H, D), jnp.float32) * s2, 'bo': jnp.zeros((E, D), jnp.float32)}
    _L0_ffn_all = _L0_ffn_setup()
    _L0_ffn_in = {k: v for k, v in _L0_ffn_all.items() if k in ('Wr', 'br', 'W1', 'b1', 'g1', 'be1', 'm1', 'v1', 'W2', 'b2', 'g2', 'be2', 'm2', 'v2', 'Wo', 'bo')}
    del _L0_ffn_all
    return {'x': x, 'src': src, 'dst': dst, 'edge_attr3_1x1': edge_attr3_1x1, 'L0_gnn_W': _L0_gnn_in['W'], 'L0_gnn_w_att_src': _L0_gnn_in['w_att_src'], 'L0_gnn_w_att_dst': _L0_gnn_in['w_att_dst'], 'L0_ffn_Wr': _L0_ffn_in['Wr'], 'L0_ffn_br': _L0_ffn_in['br'], 'L0_ffn_W1': _L0_ffn_in['W1'], 'L0_ffn_b1': _L0_ffn_in['b1'], 'L0_ffn_g1': _L0_ffn_in['g1'], 'L0_ffn_be1': _L0_ffn_in['be1'], 'L0_ffn_m1': _L0_ffn_in['m1'], 'L0_ffn_v1': _L0_ffn_in['v1'], 'L0_ffn_W2': _L0_ffn_in['W2'], 'L0_ffn_b2': _L0_ffn_in['b2'], 'L0_ffn_g2': _L0_ffn_in['g2'], 'L0_ffn_be2': _L0_ffn_in['be2'], 'L0_ffn_m2': _L0_ffn_in['m2'], 'L0_ffn_v2': _L0_ffn_in['v2'], 'L0_ffn_Wo': _L0_ffn_in['Wo'], 'L0_ffn_bo': _L0_ffn_in['bo']}

def reference(x, src, dst, edge_attr3_1x1, L0_gnn_W, L0_gnn_w_att_src, L0_gnn_w_att_dst, L0_ffn_Wr, L0_ffn_br, L0_ffn_W1, L0_ffn_b1, L0_ffn_g1, L0_ffn_be1, L0_ffn_m1, L0_ffn_v1, L0_ffn_W2, L0_ffn_b2, L0_ffn_g2, L0_ffn_be2, L0_ffn_m2, L0_ffn_v2, L0_ffn_Wo, L0_ffn_bo):
    import jax
    import jax.numpy as jnp

    def _L0_gnn_ref(feat, dist, W, w_att_src, w_att_dst, src, dst):
        import jax, jax.numpy as jnp
        import numpy as np
        N, F_IN, H, OUT, E = (4000, 256, 4, 64, 64000)
        NEG_SLOPE = 0.2
        n = feat.shape[0]
        ft = (feat @ W).reshape(n, H, OUT)
        e_src = jnp.sum(ft * w_att_src, axis=-1, keepdims=True)
        e_dst = jnp.sum(ft * w_att_dst, axis=-1, keepdims=True)
        e = e_src[src] + e_dst[dst]
        e = jnp.where(e >= 0, e, NEG_SLOPE * e)
        emax = jax.ops.segment_max(e, dst, num_segments=n)
        ex = jnp.exp(e - emax[dst])
        denom = jax.ops.segment_sum(ex, dst, num_segments=n)
        a = ex / denom[dst] * dist
        m = ft[src] * a
        out = jax.ops.segment_sum(m, dst, num_segments=n)
        return out.reshape(n, H * OUT)

    def _L0_ffn_ref(x, Wr, br, W1, b1, g1, be1, m1, v1, W2, b2, g2, be2, m2, v2, Wo, bo):
        import jax, jax.numpy as jnp
        import numpy as np
        BN_EPS = 0.001

        def _bn(h, g, b, m, v):
            return g * (h - m) * jax.lax.rsqrt(v + BN_EPS) + b
        feat = jnp.mean(x, axis=0)
        w = jax.nn.softmax(feat @ Wr + br, axis=-1)
        h = jnp.einsum('bfd,edh->bfeh', x, W1) + b1
        h = jax.nn.relu(_bn(h, g1, be1, m1, v1))
        h = jnp.einsum('bfeh,ehk->bfek', h, W2) + b2
        h = jax.nn.relu(_bn(h, g2, be2, m2, v2))
        y = jnp.einsum('bfeh,ehd->bfed', h, Wo) + bo
        return jnp.einsum('bfed,fe->bfd', y, w)
    x = x + _L0_gnn_ref(_layernorm(x, axis=-1), edge_attr3_1x1, L0_gnn_W, L0_gnn_w_att_src, L0_gnn_w_att_dst, src, dst)
    x = x + _L0_ffn_ref(_layernorm(x, axis=-1)[None], L0_ffn_Wr, L0_ffn_br, L0_ffn_W1, L0_ffn_b1, L0_ffn_g1, L0_ffn_be1, L0_ffn_m1, L0_ffn_v1, L0_ffn_W2, L0_ffn_b2, L0_ffn_g2, L0_ffn_be2, L0_ffn_m2, L0_ffn_v2, L0_ffn_Wo, L0_ffn_bo)[0]
    return x

_drawn_inputs = setup_inputs


def setup_inputs(seed=0):
    import zlib

    import numpy as np

    out = dict(_drawn_inputs(seed))
    spreads = {'L0_ffn_br': (0.0, 0.1),
     'L0_ffn_b1': (0.0, 0.325),
     'L0_ffn_g1': (1.0, 0.2),
     'L0_ffn_be1': (0.0, 0.331),
     'L0_ffn_m1': (0.0, 0.322),
     'L0_ffn_v1': (1.0, 0.6),
     'L0_ffn_b2': (0.0, 0.1),
     'L0_ffn_g2': (1.0, 0.2),
     'L0_ffn_be2': (0.0, 0.1),
     'L0_ffn_m2': (0.0, 0.1),
     'L0_ffn_v2': (1.0, 0.569),
     'L0_ffn_bo': (0.0, 0.1)}
    factors = {}
    for name, (base, spread) in spreads.items():
        noise = np.random.default_rng([zlib.crc32(name.encode()), seed]).standard_normal(out[name].shape)
        drawn = base * np.exp(spread * noise) if base else spread * noise
        out[name] = jnp.asarray(drawn.astype(out[name].dtype))
    for name, factor in factors.items():
        out[name] = (out[name] * factor).astype(out[name].dtype)
    return out
```

```python
from contextlib import ExitStack

import concourse.bass as bass
from concourse import mybir

ALU = mybir.AluOpType
ACT = mybir.ActivationFunctionType
AX = mybir.AxisListType
F32 = mybir.dt.float32
I32 = mybir.dt.int32
U32 = mybir.dt.uint32

P = 128
NT = 125
D = 256
KC = D // P
H = 4
DH = D // H
ROW = D + H
ROWX = ROW + H
TE = 18
WIN = P * TE
TH = TE * H
EX = 8
SLOPE = 0.2
LN_EPS = 1e-5
BN_EPS = 1e-3
BIG = 1e37
TINY = 1e-30
RING = 2
ROUTE = 2 * TE * 2 * H
YS = EX + 1
GNN_STEPS = 23
FFN_STEPS = 3


class Pair:

    def __init__(self, k, off):
        self.k, self.off = k, off

    @property
    def n(self):
        return self.off if isinstance(self.k, int) else self.k * 2 + self.off

    @property
    def half(self):
        return self.off // 2 if isinstance(self.k, int) else self.k + self.off // 2

    @property
    def par(self):
        return self.off % 2

    def begins(self, d):
        return isinstance(self.k, int) and self.off < d

    def __add__(self, d):
        return Pair(self.k, self.off + d)


def over_pairs(eng, lo, hi, body, peel=0):
    first = lo
    for n in range(peel):
        if first < hi:
            body(Pair(0, first))
            first += 1
    turns = (hi - first) // 2
    if turns > 0:
        with eng.Fori(0, turns) as k:
            body(Pair(k, first))
            body(Pair(k, first + 1))
    if (hi - first) % 2:
        body(Pair(0, hi - 1))


class Chain:

    def __init__(self, eng, sem):
        self.eng, self.sem, self.base, self.count = eng, sem, 0, 0

    def start(self, base):
        self.base, self.count = base, 0

    def did(self, ins):
        ins.then_inc(self.sem, 1)
        self.count += 1

    def settle(self, alone=None):
        self.eng.wait_ge(self.sem, self.base + self.count)
        if alone is not None:
            self.eng.sem_inc(alone, 1)


def gnn_ffn_kernel(nc, x, src, dst, dist, W, att_src, att_dst, Wr, br, W1, b1, g1, be1, m1, v1, W2, b2, g2, be2,
                   m2, v2, Wo, bo, out):
    N = x.shape[0]
    E = src.shape[0]
    TILES = N // NT
    NP = TILES // 2
    EB = E // NT
    assert NP * 2 * NT == N and EB * NT == E and TILES + 1 <= P and NP >= 4
    EPAD = (-(E + WIN)) % P
    PADDED = E + WIN + EPAD

    with ExitStack() as ctx:
        def sb(name, shape, dt=F32):
            return ctx.enter_context(nc.sbuf_tensor(name, shape, dt))

        def bank(name):
            return ctx.enter_context(nc.psum_tensor(name, [P, 512], F32))

        def sem(name):
            return ctx.enter_context(nc.semaphore(name))

        table = nc.dram_tensor("table", [N, ROW], F32, kind="Internal").ap()
        src_pad = nc.dram_tensor("src_pad", [PADDED], I32, kind="Internal").ap()
        dst_pad = nc.dram_tensor("dst_pad", [PADDED + P], I32, kind="Internal").ap()
        dist_pad = nc.dram_tensor("dist_pad", [PADDED], F32, kind="Internal").ap()

        ident = sb("ident", [P, P])
        iota_i = sb("iota_i", [P, NT], I32)
        iota = sb("iota", [P, NT])
        base_i = sb("base_i", [P, TILES], I32)
        base = sb("base", [P, TILES])
        node_i = sb("node_i", [P, TILES], I32)
        node = sb("node", [P, TILES])
        ids_i = sb("ids_i", [P, TILES], I32)
        bound_i = sb("bound_i", [P, 1], I32)
        bound = sb("bound", [P, 1])
        ones = sb("ones", [P, P])
        eps_ln = sb("eps_ln", [P, 1])
        pad_fill = sb("pad_fill", [P, TE], I32)
        neg_fill = sb("neg_fill", [P, TE], I32)

        w1 = sb("w1", [P, EX * KC, D])
        w2 = sb("w2", [P, EX * KC, D])
        wo = sb("wo", [P, EX * KC, D])
        wr = sb("wr", [P, KC, EX])
        br_row = sb("br_row", [1, EX])
        bo_rows = sb("bo_rows", [EX, D])
        bn_rows = sb("bn_rows", [5 * EX * KC, 2, P])
        bn_cols = sb("bn_cols", [P, 2, 5, EX * KC])
        bn_scale = sb("bn_scale", [P, 2, EX * KC])
        bn_shift = sb("bn_shift", [P, 2, EX * KC])
        wx = sb("wx", [P, KC, ROWX])

        edst = sb("edst", [P, TILES, H])
        plan_i = sb("plan_i", [1, P + 1], I32)

        gath = sb("gath", [P, RING, 2, TE, ROW])
        onehot = sb("onehot", [P, 2, TE, NT])
        onehot_t = sb("onehot_t", [P, 2, WIN])
        src_win = sb("src_win", [P, RING, 2, TE], U32)
        dst_win = sb("dst_win", [P, RING, 2, TE], I32)
        dist_win = sb("dist_win", [P, RING, 2, TE])
        x_res = sb("x_res", [P, RING, 2, D])
        rel = sb("rel", [P, 2, TE, H])
        esrc = sb("esrc", [P, 2, TH])
        turned = sb("turned", [TH, 2, 2, P])
        change = sb("change", [TH, 2, P + 1])
        reset = sb("reset", [TH, 2, P])
        scan = sb("scan", [TH, 2, P])
        scan_end = sb("scan_end", [TH, 2, P])
        ends = sb("ends", [P, 2, 2, TH])
        nmask = sb("nmask", [P, 2, TH])
        nval = sb("nval", [P, 2, TH])
        nmax = sb("nmax", [P, 2, H])
        zmax = sb("zmax", [P, 2, H])
        edm = sb("edm", [P, 2, 2 * H])
        z = sb("z", [P, 2 * TE, H])
        lz = sb("lz", [P, 2 * TE, H])
        wgt = sb("wgt", [P, 2 * TE, H])
        rden = sb("rden", [P, 2, H])
        aggn = sb("aggn", [P, 2, D])
        stats = sb("stats", [P, 2, 6])
        mv = sb("mv", [P, 2, 2])
        std = sb("std", [P, 2])
        rstd = sb("rstd", [P, 2])
        xn = sb("xn", [P, 2, D])
        x1 = sb("x1", [P, RING, 2, D])
        xT = sb("xT", [P, RING, KC, 2, NT])
        rsub = sb("rsub", [P, 2, EX])
        rexp = sb("rexp", [P, 2, EX])
        rmax = sb("rmax", [P, 2])
        rsum = sb("rsum", [P, 2])
        rinv = sb("rinv", [P, 2])
        gate = sb("gate", [P, 2, EX])
        gate_t = sb("gate_t", [EX, 2, NT])
        h1 = sb("h1", [P, KC, 2, NT])
        h2 = sb("h2", [P, KC, 2, NT])

        bankA, bankB, bankC = bank("bankA"), bank("bankB"), bank("bankC")
        bankE = [bank("bankE0"), bank("bankE1")]
        bankH1, bankH2, bankY = bank("bankH1"), bank("bankH2"), bank("bankY")

        attn_in, small_in, pads_src = sem("attn_in"), sem("small_in"), sem("pads_src")
        weights_in = sem("weights_in")
        consts = sem("consts")
        dve_step = sem("dve_step")
        act_step = sem("act_step")
        fills = sem("fills")
        wx_ready, bn_turned, bn_sum, bn_root, bn_ready = (
            sem("wx_ready"), sem("bn_turned"), sem("bn_sum"), sem("bn_root"), sem("bn_ready"))
        t_x = [sem("t_x0"), sem("t_x1")]
        t_var, t_std, t_norm, t_turned, t_xT, t_ft, t_rows = (
            sem("t_var"), sem("t_std"), sem("t_norm"), sem("t_turned"), sem("t_xT"), sem("t_ft"), sem("t_rows"))
        t_stored = [sem("t_stored0"), sem("t_stored1")]
        p_in, p_first, p_coarse, p_block, p_fetched, p_row, p_flag, p_ready = (
            sem("p_in"), sem("p_first"), sem("p_coarse"), sem("p_block"), sem("p_fetched"), sem("p_row"),
            sem("p_flag"), sem("p_ready"))
        setup_done = sem("setup_done")
        passed = sem("passed")
        win_in = [sem("win_in0"), sem("win_in1")]
        dstT_in = sem("dstT_in")
        rows_in = [sem("rows_in0"), sem("rows_in1")]
        esrc_kept = sem("esrc_kept")
        rel_ready, turn_done, turn_kept, seg_done, back_done, back_kept = (
            sem("rel_ready"), sem("turn_done"), sem("turn_kept"), sem("seg_done"), sem("back_done"), sem("back_kept"))
        onehot_ready, onehotT_ready, nodes_done, edm_ready, edge_done = (
            sem("onehot_ready"), sem("onehotT_ready"), sem("nodes_done"), sem("edm_ready"), sem("edge_done"))
        logit_ready, ex_ready, msg_ready, agg_done = (
            sem("logit_ready"), sem("ex_ready"), sem("msg_ready"), sem("agg_done"))
        var_ready, std_ready, xn_ready, xT_done, xT_ready = (
            sem("var_ready"), sem("std_ready"), sem("xn_ready"), sem("xT_done"), sem("xT_ready"))
        route_done, rsub_ready, rexp_ready, gate_ready, gateT_done, gateT_kept = (
            sem("route_done"), sem("rsub_ready"), sem("rexp_ready"), sem("gate_ready"), sem("gateT_done"),
            sem("gateT_kept"))
        h1_done, h1_kept, h2_done, h2_kept, y_done, y_added = (
            sem("h1_done"), sem("h1_kept"), sem("h2_done"), sem("h2_kept"), sem("y_done"), sem("y_added"))
        out_stored = [sem("out_stored0"), sem("out_stored1")]

        table2 = nc.dram_tensor("table2", [N, ROW], F32, kind="Internal").ap()
        CH = -(-E // P)
        gp_rows = gath[:, 0, 0, 0, :]
        gp_acc = gath[:, 0, 0, 1, :]
        gp_res = gath[:, 0, 0, 2, :]
        gp_dst_row = gath[:, 0, 1, 0, 0:P].bitcast(I32)
        gp_away = gath[:, 0, 1, 1, 0:P]
        gp_val = gath[:, 0, 1, 2:4, :].rearrange("p a c -> p (a c)")[:, 0:H * P].rearrange("p (h e) -> p h e", h=H)
        gp_onehot = gath[:, 0, 1, 4, 0:NT]
        gp_onehot_t = gath[:, 0, 1, 5, 0:P]
        gp_nmax, gp_cmax, gp_zmax = (gath[:, 0, 1, 6, i * H:(i + 1) * H] for i in range(3))
        gp_edm = gath[:, 0, 1, 7, 0:2 * H]
        gp_z, gp_l, gp_w, gp_den = (gath[:, 0, 1, 8, i * H:(i + 1) * H] for i in range(4))
        gp_src = sb("gp_src", [P, 1], U32)
        gp_dst = sb("gp_dst", [P, 1], I32)
        gp_dist = sb("gp_dist", [P, 1])
        gp_rel = sb("gp_rel", [P, 1])
        table_ready = sem("table_ready")
        gp_dve = sem("gp_dve")
        max_in, max_rows, sum_in, sum_rows = sem("max_in"), sem("max_rows"), sem("sum_in"), sem("sum_rows")
        max_spread = sem("max_spread")
        max_free, sum_free, tile_go, res_free = sem("max_free"), sem("sum_free"), sem("tile_go"), sem("res_free")
        sum_masks, sum_edge, sum_logit, sum_ex, sum_msg, sum_agg = (
            sem("sum_masks"), sem("sum_edge"), sem("sum_logit"), sem("sum_ex"),
            sem("sum_msg"), sem("sum_agg"))
        res_ready, res_stored, gp_tables, gp_plan = sem("res_ready"), sem("res_stored"), sem("gp_tables"), sem("gp_plan")
        MAX_STEPS, SUM_STEPS, TILE_STEPS = 3, 5, 5

        def general(eng, path):
            eng.wait_ge(p_ready, 1)
            flag = eng.value_load(plan_i[0:1, P:P + 1], min_val=0, max_val=2 * P)
            with eng.If(flag > 0):
                path()

        xin = x_res
        xnt = x1
        ft_rows = gath[:, 0, 0, 0:4, :].rearrange("p (r u) c -> p r u c", r=2)
        dst_all = gath[:, 1, 0, :, :].rearrange("p t c -> p (t c)")[:, 0:EB].bitcast(I32)
        dst_prev = gath[:, 1, 1, :, :].rearrange("p t c -> p (t c)")[:, 0:EB].bitcast(I32)
        blk = onehot[:, 0, :, :].rearrange("p t c -> p (t c)")[:, 0:EB].bitcast(I32)
        scr = onehot[:, 1, :, :].rearrange("p t c -> p (t c)")[:, 0:EB]
        scr2 = onehot_t[:, 0, 0:EB]
        att = onehot_t[:, 1, 0:2 * D].rearrange("p (k c) -> p k c", k=2)
        att_prod = onehot_t[:, 1, 2 * D:2 * D + D]
        J = TILES + 1
        blk_i = sb("blk_i", [P, 1], I32)
        plan_cols = sb("plan_cols", [P, 5])
        coarse, fine, startf, blkf, bad1 = (plan_cols[:, i:i + 1] for i in range(5))
        plan_f = sb("plan_f", [1, 3 * P + 1])
        first_dst = sb("first_dst", [P, J])

        x_pairs = x.rearrange("(g u p) d -> g p u d", u=2, p=NT)
        out_pairs = out.rearrange("(g u p) d -> g p u d", u=2, p=NT)
        table_pairs = table.rearrange("(g u p) d -> g p u d", u=2, p=NT)

        block = ctx.enter_context(nc.Block())

        PER_WIN = 16 * 7
        PER_ROWS = 16 * 2 * TE

        @block.sync
        def _(sp):
            sp.dma_start(wx[:, :, 0:D], W.rearrange("(c k) n -> k c n", k=P)).then_inc(attn_in, 16)
            sp.dma_start(att[:, 0, :], att_src.rearrange("a h c -> a (h c)").broadcast_to([P, D])).then_inc(attn_in, 16)
            sp.dma_start(att[:, 1, :], att_dst.rearrange("a h c -> a (h c)").broadcast_to([P, D])).then_inc(attn_in, 16)

            def load_x(g):
                if not g.begins(2):
                    sp.wait_ge(t_norm, g.n * 2 - 2)
                sp.dma_start(xin[0:NT, g.par, :, :], x_pairs[g.n]).then_inc(t_x[g.par], 16)

            load_x(Pair(0, 0))
            load_x(Pair(0, 1))
            sp.wait_ge(fills, 1)
            sp.dma_start(dst_pad[1:1 + E].rearrange("(a b) -> a b", a=NT), dst.rearrange("(a b) -> a b", a=NT)).then_inc(pads_src, 16)
            sp.dma_start(src_pad[0:E].rearrange("(a b) -> a b", a=NT), src.rearrange("(a b) -> a b", a=NT)).then_inc(pads_src, 16)
            sp.dma_start(dist_pad[0:E].rearrange("(a b) -> a b", a=NT),
                         dist.rearrange("(a b) c d -> a (b c d)", a=NT)).then_inc(pads_src, 16)
            sp.dma_start(src_pad[E:E + WIN].rearrange("(a b) -> a b", a=P), pad_fill[:, 0:TE]).then_inc(pads_src, 16)
            sp.dma_start(dist_pad[E:E + WIN].rearrange("(a b) -> a b", a=P).bitcast(I32), pad_fill[:, 0:TE]).then_inc(pads_src, 16)
            sp.dma_start(dst_all[0:NT, :], dst.rearrange("(a b) -> a b", a=NT)).then_inc(p_in, 16)
            sp.wait_ge(fills, 2)
            sp.dma_start(dst_pad[1 + E:1 + E + WIN].rearrange("(a b) -> a b", a=P), neg_fill[:, 0:TE]).then_inc(pads_src, 16)
            sp.dma_start(dst_pad[0:1].rearrange("(a b) -> a b", a=1), neg_fill[0:1, 0:1]).then_inc(pads_src, 16)
            sp.wait_ge(pads_src, 16 * 7)
            sp.dma_start(dst_prev[0:NT, :], dst_pad[0:E].rearrange("(a b) -> a b", a=NT)).then_inc(p_in, 16)
            over_pairs(sp, 2, NP, load_x)

            sp.wait_ge(t_stored[0], 16 * ((NP + 1) // 2))
            sp.wait_ge(t_stored[1], 16 * (NP // 2))
            sp.nop().then_inc(table_ready, 1)

            def path():
                sp.sem_inc(res_free, 1)
                with sp.Fori(0, TILES) as j:
                    sp.wait_ge(res_ready, j + 1)
                    sp.dma_start(table2[bass.ds(j * NT, NT), :], gp_res[0:NT, :]).then_inc(res_stored, 16)
                    sp.wait_ge(res_stored, j * 16 + 16)
                    sp.sem_inc(res_free, 1)
                sp.wait_ge(sum_free, TILES * CH + 1)
                sp.dma_start(table.rearrange("(a b) c -> a (b c)", a=NT), table2.rearrange("(a b) c -> a (b c)", a=NT)).then_inc(gp_tables, 16)
                sp.dma_start(src_pad[0:N].rearrange("(p j) -> p j", p=NT), ids_i[0:NT, :]).then_inc(gp_tables, 16)
                sp.dma_start(dst_pad[1:1 + N].rearrange("(p j) -> p j", p=NT), ids_i[0:NT, :]).then_inc(gp_tables, 16)
                sp.dma_start(dst_pad[1 + N:1 + N + WIN].rearrange("(a b) -> a b", a=P), neg_fill[:, 0:TE]).then_inc(gp_tables, 16)
                sp.dma_start(dist_pad[0:N].rearrange("(p j) -> p j", p=NT), ones[0:NT, 0:TILES]).then_inc(gp_tables, 16)
                sp.wait_ge(gp_tables, 16 * 5)
                sp.wait_ge(gp_plan, 1)

            general(sp, path)
            sp.nop().then_inc(setup_done, 1)

            def load_windows(g):
                for u in range(2):
                    first = sp.value_load(plan_i[0:1, bass.ds(g.n * 2 + u, 1)], min_val=0, max_val=E)
                    for buf, dram, off in ((src_win, src_pad.bitcast(U32), 0), (dst_win, dst_pad, 1), (dist_win, dist_pad, 0)):
                        sp.dma_start(buf[:, g.par, u, :], dram[bass.ds(first + off, WIN)].rearrange("(p t) -> p t", t=TE)).then_inc(win_in[g.par], 16)
                sp.dma_start(x_res[0:NT, g.par, :, :], x_pairs[g.n]).then_inc(win_in[g.par], 16)

            def load_dstT(g):
                for u in range(2):
                    first = sp.value_load(plan_i[0:1, bass.ds(g.n * 2 + u, 1)], min_val=0, max_val=E)
                    sp.dma_start(onehot_t[:, u, :].bitcast(I32),
                                 dst_pad[bass.ds(first + 1, WIN)].rearrange("(a t) -> a t", a=1).broadcast_to([P, WIN])).then_inc(dstT_in, 16)

            def store(f):
                sp.wait_ge(y_added, f.n * YS + YS)
                sp.sem_inc(passed, 1)
                sp.dma_start(out_pairs[f.n], x1[0:NT, f.par, :, :]).then_inc(out_stored[f.par], 16)

            load_windows(Pair(0, 0))
            load_dstT(Pair(0, 0))
            load_windows(Pair(0, 1))
            sp.wait_ge(edge_done, 1)
            load_dstT(Pair(0, 1))

            def turn(f):
                sp.wait_ge(agg_done, f.n * 2 + 2)
                sp.wait_ge(xn_ready, f.n * 2 + 2)
                sp.sem_inc(passed, 1)
                load_windows(f + 2)
                sp.wait_ge(edge_done, f.n + 2)
                sp.sem_inc(passed, 1)
                load_dstT(f + 2)
                store(f)

            over_pairs(sp, 0, NP - 2, turn)
            store(Pair(0, NP - 2))
            store(Pair(0, NP - 1))
            sp.wait_ge(out_stored[0], 16 * ((NP + 1) // 2))
            sp.wait_ge(out_stored[1], 16 * (NP // 2))

        @block.gpsimd
        def _(pool):
            pool.memset(ident[:], 1.0).then_inc(consts, 1)
            pool.memset(pad_fill[:], 0).then_inc(fills, 1)
            pool.memset(neg_fill[:], -1).then_inc(fills, 1)
            pool.memset(ones[:], 1.0).then_inc(consts, 1)
            pool.memset(eps_ln[:], LN_EPS).then_inc(consts, 1)
            pool.wait_ge(consts, 3)
            pool.affine_select(out=ident[:], in_=ident[:], compare_op=ALU.is_equal, fill=0.0, base=0,
                               pattern=[[1, P]], channel_multiplier=-1).then_inc(consts, 1)
            pool.iota(iota_i[:], [[1, NT]], base=0, channel_multiplier=0).then_inc(consts, 1)
            pool.iota(base_i[:], [[NT, TILES]], base=0, channel_multiplier=0).then_inc(consts, 1)
            pool.iota(node_i[:], [[NT, TILES]], base=0, channel_multiplier=1).then_inc(consts, 1)
            pool.iota(ids_i[:], [[1, TILES]], base=0, channel_multiplier=TILES).then_inc(consts, 1)
            pool.iota(bound_i[:], [[1, 1]], base=0, channel_multiplier=NT).then_inc(consts, 1)
            pool.wait_ge(p_block, 1)
            pool.indirect_dma_start(blk[0:J, :], None, dst.rearrange("(a b) -> a b", a=NT),
                                    bass.IndirectOffsetOnAxis(blk_i[0:J, 0:1].bitcast(U32), 0)).then_inc(p_fetched, 16)
            def path():
                pool.wait_ge(table_ready, 1)
                pool.sem_inc(tile_go, 1)
                with pool.Fori(0, TILES) as j:
                    with pool.Fori(0, CH) as i:
                        pool.wait_ge(max_free, j * CH + i + 1)
                        pool.dma_start(gp_src[:], src_pad[bass.ds(i * P, P)].rearrange("(p a) -> p a", a=1).bitcast(U32)).then_inc(max_in, 16)
                        pool.dma_start(gp_dst_row, dst_pad[bass.ds(i * P + 1, P)].rearrange("(a e) -> a e", a=1).broadcast_to([P, P])).then_inc(max_in, 16)
                        pool.wait_ge(max_in, i * 32 + 32)
                        pool.sem_inc(passed, 1)
                        pool.indirect_dma_start(gp_rows, None, table, bass.IndirectOffsetOnAxis(gp_src[:, 0:1], 0)).then_inc(max_rows, 16)
                    pool.wait_ge(max_free, j * CH + CH + 1)
                    pool.sem_inc(passed, 1)
                    with pool.Fori(0, CH) as i:
                        pool.wait_ge(sum_free, j * CH + i + 1)
                        pool.dma_start(gp_src[:], src_pad[bass.ds(i * P, P)].rearrange("(p a) -> p a", a=1).bitcast(U32)).then_inc(sum_in, 16)
                        pool.dma_start(gp_dst[:], dst_pad[bass.ds(i * P + 1, P)].rearrange("(p a) -> p a", a=1)).then_inc(sum_in, 16)
                        pool.dma_start(gp_dist[:], dist_pad[bass.ds(i * P, P)].rearrange("(p a) -> p a", a=1)).then_inc(sum_in, 16)
                        pool.dma_start(gp_dst_row, dst_pad[bass.ds(i * P + 1, P)].rearrange("(a e) -> a e", a=1).broadcast_to([P, P])).then_inc(sum_in, 16)
                        pool.wait_ge(sum_in, i * 64 + 64)
                        pool.sem_inc(passed, 1)
                        pool.indirect_dma_start(gp_rows, None, table, bass.IndirectOffsetOnAxis(gp_src[:, 0:1], 0)).then_inc(sum_rows, 16)
                    pool.wait_ge(sum_free, j * CH + CH + 1)
                    pool.sem_inc(passed, 1)
                    pool.inc_swdge_sem([max_in, max_rows, sum_in, sum_rows], [32 * CH, 16 * CH, 64 * CH, 16 * CH], mode="sub")
                    pool.nop().then_inc(tile_go, 1)

            general(pool, path)
            pool.wait_ge(setup_done, 1)

            def gather(g):
                pool.wait_ge(win_in[g.par], (g.half + 1) * PER_WIN)
                if not g.begins(2):
                    pool.wait_ge(agg_done, g.n * 2 - 2)
                pool.sem_inc(passed, 1)
                for u in range(2):
                    for t in range(TE):
                        pool.indirect_dma_start(gath[:, g.par, u, t, :], None, table,
                                                bass.IndirectOffsetOnAxis(src_win[:, g.par, u, t:t + 1], 0)
                                                ).then_inc(rows_in[g.par], 16)

            over_pairs(pool, 0, NP, gather, peel=2)

        @block.tensor
        def _(pe):
            pe.wait_ge(consts, 9)
            pe.wait_ge(small_in, 16 * 13)
            for l in range(2):
                mm = pe.transpose(bankC[:, l * 80:l * 80 + 80], bn_rows[0:80, l, :], ident[0:80, 0:80])
            mm.then_inc(bn_turned, 1)

            def turn_x(g):
                pe.wait_ge(t_norm, g.n * 2 + 2)
                if not g.begins(1):
                    pe.wait_ge(t_xT, g.n)
                for u in range(2):
                    for c in range(KC):
                        mm = pe.transpose(bankA[:, (u * KC + c) * NT:(u * KC + c + 1) * NT],
                                          xnt[0:NT, g.par, u, c * P:(c + 1) * P], ident[0:NT, 0:NT])
                mm.then_inc(t_turned, 1)

            def project(g):
                pe.wait_ge(t_xT, g.n + 1)
                if not g.begins(1):
                    pe.wait_ge(t_rows, g.n * 2)
                for u in range(2):
                    for c in range(KC):
                        mm = pe.matmul(bankE[u][0:NT, 0:ROWX], xT[:, g.par, c, u, :], wx[:, c, :],
                                       start=(c == 0), stop=(c == KC - 1))
                    mm.then_inc(t_ft, 1)

            pe.wait_ge(wx_ready, 1)
            turn_x(Pair(0, 0))
            pe.wait_ge(p_first, 1)
            pe.matmul(bankH1[0:J, 0:NT], first_dst[0:NT, :], ident[0:NT, 0:NT], start=True, stop=True).then_inc(p_coarse, 1)

            def table_turn(g):
                turn_x(g)
                project(g + -1)

            over_pairs(pe, 1, NP, table_turn, peel=1)
            project(Pair(0, NP - 1))
            pe.wait_ge(p_row, 1)
            pe.matmul(bankH2[0:1, 0:J], startf[0:J, :], ident[0:J, 0:J], start=True, stop=True)
            pe.matmul(bankH2[0:1, P:P + 1], bad1[0:NT, :], ones[0:NT, 0:1], start=True, stop=True).then_inc(p_flag, 1)

            def turn_logits(g):
                pe.wait_ge(rel_ready, g.n + 1)
                pe.wait_ge(esrc_kept, g.n + 1)
                for u in range(2):
                    pe.matmul(bankA[0:TH, u * 2 * P:u * 2 * P + P], esrc[:, u, :], ident[:, :],
                              start=True, stop=True)
                    mm = pe.matmul(bankA[0:TH, u * 2 * P + P:(u + 1) * 2 * P],
                                   rel[:, u, :, :].rearrange("p t h -> p (t h)"), ident[:, :],
                                   start=True, stop=True)
                mm.then_inc(turn_done, 1)

            def turn_back(g):
                pe.wait_ge(seg_done, g.n + 1)
                for u in range(2):
                    pe.matmul(bankB[:, (u * 2) * TH:(u * 2 + 1) * TH], scan_end[:, u, :], ident[0:TH, 0:TH],
                              start=True, stop=True)
                    mm = pe.matmul(bankB[:, (u * 2 + 1) * TH:(u * 2 + 2) * TH], change[:, u, 1:P + 1],
                                   ident[0:TH, 0:TH], start=True, stop=True)
                mm.then_inc(back_done, 1)

            def to_nodes(g):
                pe.wait_ge(onehot_ready, g.n + 1)
                pe.wait_ge(back_kept, g.n + 1)
                for u in range(2):
                    for t in range(TE):
                        col = (u * TE + t) * 2 * H
                        mm = pe.matmul(bankC[0:NT, col:col + 2 * H], onehot[:, u, t, :],
                                       ends[:, u, :, t * H:(t + 1) * H], start=True, stop=True)
                mm.then_inc(nodes_done, 1)

            def to_edges(g):
                pe.wait_ge(onehotT_ready, g.n + 1)
                pe.wait_ge(edm_ready, g.n + 1)
                for u in range(2):
                    for t in range(TE):
                        col = (u * TE + t) * 2 * H
                        mm = pe.matmul(bankB[:, col:col + 2 * H], onehot_t[0:NT, u, t:WIN:TE], edm[0:NT, u, :],
                                       start=True, stop=True)
                mm.then_inc(edge_done, 1)

            def aggregate(g, u):
                pe.wait_ge(msg_ready, g.n * 2 + u + 1)
                for t in range(TE):
                    mm = pe.matmul(bankE[u][0:NT, 0:ROW], onehot[:, u, t, :], gath[:, g.par, u, t, :],
                                   start=(t == 0), stop=(t == TE - 1))
                mm.then_inc(agg_done, 1)

            def turn_x1(g):
                pe.wait_ge(xn_ready, g.n * 2 + 2)
                for u in range(2):
                    for c in range(KC):
                        mm = pe.transpose(bankA[:, (c * 2 + u) * NT:(c * 2 + u + 1) * NT],
                                          xn[0:NT, u, c * P:(c + 1) * P], ident[0:NT, 0:NT])
                mm.then_inc(xT_done, 1)

            def route(g):
                pe.wait_ge(xT_ready, g.n + 1)
                for u in range(2):
                    o = bankC[0:NT, ROUTE + u * EX:ROUTE + (u + 1) * EX]
                    for c in range(KC):
                        pe.matmul(o, xT[:, g.par, c, u, :], wr[:, c, :], start=(c == 0), stop=False)
                    mm = pe.matmul(o, ones[0:1, 0:NT], br_row[0:1, :], start=False, stop=True)
                mm.then_inc(route_done, 1)

            def turn_gate(f):
                pe.wait_ge(gate_ready, f.n + 1)
                for u in range(2):
                    mm = pe.transpose(bankC[0:EX, u * NT:(u + 1) * NT], gate[0:NT, u, :], ident[0:NT, 0:NT])
                mm.then_inc(gateT_done, 1)

            def out_bias(f):
                pe.wait_ge(gateT_kept, f.n + 1)
                if not f.begins(1):
                    pe.wait_ge(y_added, f.n * YS)
                for u in range(2):
                    mm = pe.matmul(bankY[0:NT, u * D:(u + 1) * D], gate_t[:, u, :], bo_rows[:, :], start=True, stop=True)
                mm.then_inc(y_done, 1)

            def layer(weights, e, operand, target):
                for hc in range(KC):
                    for c in range(KC):
                        mm = pe.matmul(target[:, hc * 2 * NT:(hc + 1) * 2 * NT],
                                       weights[:, e * KC + c, hc * P:(hc + 1) * P], operand(c),
                                       start=(c == 0), stop=(c == KC - 1))
                return mm

            def layer1(f, e):
                if e or not f.begins(1):
                    pe.wait_ge(h1_kept, f.n * EX + e)
                layer(w1, e, lambda c: xT[:, f.par, c, :, :].rearrange("p u n -> p (u n)"), bankH1).then_inc(h1_done, 1)

            def layer2(f, e):
                pe.wait_ge(h1_kept, f.n * EX + e + 1)
                if e or not f.begins(1):
                    pe.wait_ge(h2_kept, f.n * EX + e)
                layer(w2, e, lambda c: h1[:, c, :, :].rearrange("p u n -> p (u n)"), bankH2).then_inc(h2_done, 1)

            def layer3(f, e):
                pe.wait_ge(h2_kept, f.n * EX + e + 1)
                pe.wait_ge(y_added, f.n * YS + e + 1)
                for u in range(2):
                    for c in range(KC):
                        mm = pe.matmul(bankY[0:NT, u * D:(u + 1) * D], h2[:, c, u, :], wo[:, e * KC + c, :],
                                       start=(c == 0), stop=(c == KC - 1))
                mm.then_inc(y_done, 1)

            def body(f, g):
                attention = {0: lambda: turn_logits(g), 1: lambda: turn_back(g), 2: lambda: to_nodes(g),
                             3: lambda: to_edges(g), 5: lambda: aggregate(g, 0), 6: lambda: aggregate(g, 1),
                             8: lambda: turn_x1(g), 9: lambda: route(g)}
                for s in range(EX + 2):
                    if f is not None:
                        if s < EX:
                            layer1(f, s)
                        if s == 0:
                            turn_gate(f)
                        if s == 1:
                            out_bias(f)
                        if 1 <= s <= EX:
                            layer2(f, s - 1)
                        if s >= 2:
                            layer3(f, s - 2)
                    if g is not None and s in attention:
                        attention[s]()

            def path():
                with pe.Fori(0, TILES) as j:
                    pe.wait_ge(tile_go, j + 1)
                    pe.sem_inc(passed, 1)
                    with pe.Fori(0, CH) as i:
                        pe.wait_ge(max_rows, i * 16 + 16)
                        for h in range(H):
                            mm = pe.matmul(bankA[0:NT, h * P:(h + 1) * P], gp_rows[:, D + h:D + h + 1].broadcast_to([P, NT]),
                                           ident[:, :], start=True, stop=True)
                        mm.then_inc(max_spread, 1)
                    with pe.Fori(0, CH) as i:
                        pe.wait_ge(sum_masks, j * CH + i + 1)
                        pe.matmul(bankB[:, 0:2 * H], gp_onehot_t[0:NT, :], gp_edm[0:NT, :], start=True, stop=True).then_inc(sum_edge, 1)
                        pe.wait_ge(sum_msg, j * CH + i + 1)
                        pe.matmul(bankE[0][0:NT, 0:ROW], gp_onehot[:, :], gp_rows[:, :], start=True, stop=True).then_inc(sum_agg, 1)

            general(pe, path)
            pe.wait_ge(weights_in, 16 * 3)
            body(None, Pair(0, 0))
            over_pairs(pe, 0, NP - 1, lambda f: body(f, f + 1), peel=1)
            body(Pair(0, NP - 1), None)

        @block.scalar
        def _(act):
            act.dma_start(wr[:], Wr.rearrange("(c k) e -> k c e", k=P)).then_inc(small_in, 16)
            act.dma_start(br_row[:], br.rearrange("(a e) -> a e", a=1)).then_inc(small_in, 16)
            act.dma_start(bo_rows[:], bo).then_inc(small_in, 16)
            for l, params in enumerate(((b1, g1, be1, m1, v1), (b2, g2, be2, m2, v2))):
                for i, prm in enumerate(params):
                    act.dma_start(bn_rows[16 * i:16 * i + 16, l, :], prm.rearrange("e (c k) -> (e c) k", k=P)).then_inc(small_in, 16)
            for buf, dram in ((w1, W1), (w2, W2), (wo, Wo)):
                act.dma_start(buf[:], dram.rearrange("e (c k) n -> k (e c) n", k=P)).then_inc(weights_in, 16)

            act.wait_ge(consts, 3)

            def root(g):
                act.wait_ge(t_var, g.n + 1)
                act.activation(std[0:NT, :], mv[0:NT, :, 1], ACT.Sqrt, bias=eps_ln[0:NT, :]).then_inc(t_std, 1)

            def keep_xT(g):
                act.wait_ge(t_turned, g.n + 1)
                if not g.begins(2):
                    act.wait_ge(t_ft, g.n * 2 - 2)
                act.activation(xT[:, g.par, :, :, :].rearrange("p c u n -> p u c n"),
                               bankA[:, 0:2 * KC * NT].rearrange("p (u c n) -> p u c n", u=2, c=KC),
                               ACT.Copy).then_inc(t_xT, 1)

            def keep_rows(g):
                act.wait_ge(t_ft, g.n * 2 + 2)
                if not g.begins(2):
                    act.wait_ge(t_stored[g.par], g.half * 16)
                for u in range(2):
                    act.activation(ft_rows[0:NT, g.par, u, :], bankE[u][0:NT, 0:ROW], ACT.Copy).then_inc(act_step, 1)
                    act.activation(edst[0:NT, bass.ds(g.n * 2 + u, 1), :].rearrange("p a h -> p (a h)"),
                                   bankE[u][0:NT, ROW:ROWX], ACT.Copy).then_inc(t_rows, 1)
                act.wait_ge(act_step, g.n * 2 + 2)
                act.wait_ge(t_rows, g.n * 2 + 2)
                act.dma_start(table_pairs[g.n], ft_rows[0:NT, g.par, :, :]).then_inc(t_stored[g.par], 16)

            root(Pair(0, 0))
            root(Pair(0, 1))
            keep_xT(Pair(0, 0))

            def turn(g):
                root(g)
                keep_xT(g + -1)
                keep_rows(g + -2)

            over_pairs(act, 2, NP, turn, peel=2)
            keep_xT(Pair(0, NP - 1))
            keep_rows(Pair(0, NP - 2))
            keep_rows(Pair(0, NP - 1))
            act.wait_ge(bn_sum, 1)
            act.activation(bn_cols[:, :, 4, :], bn_cols[:, :, 4, :], ACT.Sqrt).then_inc(bn_root, 1)

            def keep_esrc(g):
                act.wait_ge(rows_in[g.par], (g.half + 1) * PER_ROWS)
                act.activation(esrc[:].rearrange("p u (t h) -> p (u t) h", h=H),
                               gath[:, g.par, :, :, D:ROW].rearrange("p u t h -> p (u t) h"), ACT.Copy).then_inc(esrc_kept, 1)

            def keep_turned(g):
                act.wait_ge(turn_done, g.n + 1)
                act.activation(turned[:].rearrange("r u k e -> r (u k e)"), bankA[0:TH, 0:4 * P], ACT.Copy).then_inc(turn_kept, 1)

            def keep_back(g):
                act.wait_ge(back_done, g.n + 1)
                act.activation(ends[:].rearrange("p u k c -> p (u k c)"), bankB[:, 0:4 * TH], ACT.Copy).then_inc(back_kept, 1)

            def exp_logits(g):
                act.wait_ge(logit_ready, g.n + 1)
                act.activation(gath[:, g.par, :, :, D:ROW].rearrange("p u t h -> p (u t) h"), lz[:, :, :], ACT.Exp).then_inc(ex_ready, 1)

            def root1(g, u):
                act.wait_ge(var_ready, g.n * 2 + u + 1)
                act.activation(std[0:NT, u:u + 1], mv[0:NT, u, 1:2], ACT.Sqrt, bias=eps_ln[0:NT, :]).then_inc(std_ready, 1)

            def keep_x1T(g):
                act.wait_ge(xT_done, g.n + 1)
                act.activation(xT[:, g.par, :, :, :].rearrange("p c u n -> p (c u n)"), bankA[:, 0:2 * KC * NT], ACT.Copy).then_inc(xT_ready, 1)

            def exp_route(f):
                act.wait_ge(rsub_ready, f.n + 1)
                act.activation(rexp[0:NT, :, :], rsub[0:NT, :, :], ACT.Exp).then_inc(rexp_ready, 1)

            def keep_gate(f):
                act.wait_ge(gateT_done, f.n + 1)
                act.activation(gate_t[:].rearrange("e u n -> e (u n)"), bankC[0:EX, 0:2 * NT], ACT.Copy).then_inc(gateT_kept, 1)

            def relu(f, e, l, done, target, source):
                act.wait_ge(done, f.n * EX + e + 1)
                kept = h1_kept if l == 0 else h2_kept
                for hc in range(KC):
                    ins = act.activation(target[:, hc, :, :].rearrange("p u n -> p (u n)"),
                                         source[:, hc * 2 * NT:(hc + 1) * 2 * NT], ACT.Relu,
                                         bias=bn_shift[:, l, e * KC + hc:e * KC + hc + 1],
                                         scale=bn_scale[:, l, e * KC + hc:e * KC + hc + 1])
                ins.then_inc(kept, 1)

            def relu1(f, e):
                if e or not f.begins(1):
                    act.wait_ge(h2_done, f.n * EX + e)
                relu(f, e, 0, h1_done, h1, bankH1)

            def relu2(f, e):
                if e or not f.begins(1):
                    act.wait_ge(y_done, f.n * YS + e + (1 if e else 0))
                relu(f, e, 1, h2_done, h2, bankH2)

            def body(f, g):
                attention = {0: lambda: keep_turned(g), 1: lambda: keep_back(g), 4: lambda: exp_logits(g),
                             6: lambda: root1(g, 0), 7: lambda: root1(g, 1), 8: lambda: keep_x1T(g)}
                if f is not None:
                    exp_route(f)
                if g is not None:
                    keep_esrc(g)
                for s in range(EX + 2):
                    if f is not None:
                        if s == 1:
                            keep_gate(f)
                        if s < EX:
                            relu1(f, s)
                        if 1 <= s <= EX:
                            relu2(f, s - 1)
                    if g is not None and s in attention:
                        attention[s]()

            def path():
                with act.Fori(0, TILES) as j:
                    with act.Fori(0, CH) as i:
                        act.wait_ge(sum_logit, j * CH + i + 1)
                        act.activation(gp_rows[:, D:ROW], gp_l, ACT.Exp).then_inc(sum_ex, 1)

            general(act, path)
            act.wait_ge(bn_ready, 1)
            body(None, Pair(0, 0))
            over_pairs(act, 0, NP - 1, lambda f: body(f, f + 1), peel=1)
            body(Pair(0, NP - 1), None)

        @block.vector
        def _(dve):
            own = Chain(dve, dve_step)
            dve.wait_ge(consts, 9)
            own.did(dve.tensor_copy(iota[:], iota_i[:]))
            own.did(dve.tensor_copy(base[:], base_i[:]))
            own.did(dve.tensor_copy(node[:], node_i[:]))
            own.did(dve.tensor_copy(bound[:], bound_i[:]))
            own.did(dve.memset(change[:], 1.0))
            dve.wait_ge(attn_in, 48)
            for c in range(KC):
                for k in range(2):
                    own.did(dve.tensor_tensor(att_prod, wx[:, c, 0:D], att[:, k, :], ALU.mult))
                    own.settle()
                    ins = dve.tensor_reduce(wx[:, c, D + k * H:D + (k + 1) * H],
                                            att_prod.rearrange("p (h c) -> p h c", h=H), AX.X, ALU.add)
                    if c == KC - 1 and k == 1:
                        ins.then_inc(wx_ready, 1)
                    else:
                        own.did(ins)
                        own.settle()
            dve.wait_ge(p_in, 32)
            dve.tensor_copy(first_dst[0:NT, :], dst_all[0:NT, 0:1].broadcast_to([NT, J])).then_inc(p_first, 1)
            fixed = own.count

            def norm(g):
                own.start(fixed + g.n * 2)
                dve.wait_ge(t_x[g.par], (g.half + 1) * 16)
                for u in range(2):
                    ins = dve.bn_stats(stats[0:NT, u, :], xin[0:NT, g.par, u, :])
                own.did(ins)
                own.settle(alone=passed)
                for u in range(2):
                    ins = dve.bn_aggr(mv[0:NT, u, :], stats[0:NT, u, :])
                ins.then_inc(t_var, 1)
                dve.wait_ge(t_std, g.n + 1)
                own.did(dve.reciprocal(rstd[0:NT, :], std[0:NT, :]))
                own.settle()
                if not g.begins(2):
                    dve.wait_ge(t_turned, g.n - 1)
                for u in range(2):
                    dve.tensor_scalar(xnt[0:NT, g.par, u, :], xin[0:NT, g.par, u, :], mv[0:NT, u, 0:1],
                                      rstd[0:NT, u:u + 1], ALU.subtract, ALU.mult).then_inc(t_norm, 1)

            norm(Pair(0, 0))
            norm(Pair(0, 1))

            own.start(fixed + 4)
            dve.wait_ge(p_coarse, 1)
            own.did(dve.tensor_scalar(scr[0:J, 0:NT], bankH1[0:J, 0:NT], bound[0:J, :], None, ALU.is_lt, ALU.add,
                                      accum_out=coarse[0:J, :]))
            own.settle()
            own.did(dve.tensor_scalar(blkf[0:J, :], coarse[0:J, :], -1.0, 0.0, ALU.add, ALU.max))
            own.settle()
            dve.tensor_copy(blk_i[0:J, :], blkf[0:J, :]).then_inc(p_block, 1)
            fixed += own.count

            over_pairs(dve, 2, NP, norm)

            own.start(fixed + 2 * NP)
            dve.wait_ge(p_fetched, 16)
            own.did(dve.tensor_scalar(scr[0:J, :], blk[0:J, :], bound[0:J, :], None, ALU.is_lt))
            own.settle()
            own.did(dve.tensor_reduce(fine[0:J, :], scr[0:J, :], AX.X, ALU.add))
            own.did(dve.tensor_tensor(scr2[0:NT, :], dst_prev[0:NT, :], dst_all[0:NT, :], ALU.is_gt))
            own.settle()
            own.did(dve.scalar_tensor_tensor(startf[0:J, :], blkf[0:J, :], float(EB), fine[0:J, :], ALU.mult, ALU.add))
            own.did(dve.tensor_reduce(bad1[0:NT, :], scr2[0:NT, :], AX.X, ALU.max))
            own.settle()
            dve.nop().then_inc(p_row, 1)

            dve.wait_ge(bn_turned, 1)
            own.did(dve.tensor_copy(bn_cols[:].rearrange("p l k c -> p (l k c)"), bankC[:, 0:2 * 5 * EX * KC]))
            own.settle()
            dve.tensor_scalar(bn_cols[:, :, 4, :], bn_cols[:, :, 4, :], BN_EPS, None, ALU.add).then_inc(bn_sum, 1)
            dve.wait_ge(p_flag, 1)
            own.did(dve.tensor_copy(plan_f[:, 0:J], bankH2[0:1, 0:J]))
            own.did(dve.tensor_copy(plan_f[:, P:P + 1], bankH2[0:1, P:P + 1]))
            own.settle()
            own.did(dve.tensor_tensor(plan_f[:, 2 * P:2 * P + TILES], plan_f[:, 1:J], plan_f[:, 0:TILES], ALU.subtract))
            own.settle()
            own.did(dve.tensor_scalar(plan_f[:, 2 * P:2 * P + TILES], plan_f[:, 2 * P:2 * P + TILES], float(WIN), None,
                                      ALU.is_gt))
            own.settle()
            own.did(dve.tensor_reduce(plan_f[:, 3 * P:3 * P + 1], plan_f[:, 2 * P:2 * P + TILES], AX.X, ALU.add))
            own.settle()
            own.did(dve.tensor_tensor(plan_f[:, P:P + 1], plan_f[:, P:P + 1], plan_f[:, 3 * P:3 * P + 1], ALU.add))
            own.settle()
            own.did(dve.tensor_copy(plan_i[:, 0:J], plan_f[:, 0:J]))
            own.did(dve.tensor_copy(plan_i[:, P:P + 1], plan_f[:, P:P + 1]))
            own.settle()
            dve.nop().then_inc(p_ready, 1)

            dve.wait_ge(bn_root, 1)
            own.did(dve.reciprocal(bn_cols[:, :, 4, :], bn_cols[:, :, 4, :]))
            own.did(dve.tensor_tensor(bn_shift[:], bn_cols[:, :, 0, :], bn_cols[:, :, 3, :], ALU.subtract))
            own.settle()
            own.did(dve.tensor_tensor(bn_scale[:], bn_cols[:, :, 1, :], bn_cols[:, :, 4, :], ALU.mult))
            own.settle()
            own.did(dve.tensor_tensor(bn_shift[:], bn_shift[:], bn_scale[:], ALU.mult))
            own.settle()
            own.did(dve.tensor_tensor(bn_shift[:], bn_shift[:], bn_cols[:, :, 2, :], ALU.add))
            own.settle()
            dve.nop().then_inc(bn_ready, 1)

            def path():
                mine = Chain(dve, gp_dve)
                dve.sem_inc(max_free, 1)
                dve.sem_inc(sum_free, 1)
                with dve.Fori(0, TILES) as j:
                    dve.wait_ge(tile_go, j + 1)
                    tile_base = j * (CH * (MAX_STEPS + SUM_STEPS) + TILE_STEPS)
                    here = node[0:NT, bass.ds(j, 1)]
                    ed = edst[0:NT, bass.ds(j, 1), :].rearrange("n a h -> n (a h)")
                    mine.start(tile_base)
                    mine.did(dve.memset(gp_nmax[0:NT], -BIG))
                    mine.settle(alone=passed)
                    with dve.Fori(0, CH) as i:
                        mine.start(tile_base + i * MAX_STEPS + 1)
                        dve.wait_ge(max_in, i * 32 + 32)
                        mine.did(dve.tensor_scalar(gp_away[0:NT], gp_dst_row[0:NT], here, -BIG, ALU.not_equal, ALU.mult))
                        dve.wait_ge(max_spread, j * CH + i + 1)
                        mine.settle()
                        mine.did(dve.tensor_tensor(gp_val[0:NT], bankA[0:NT, 0:H * P].rearrange("n (h e) -> n h e", h=H),
                                                   gp_away[0:NT].unsqueeze(1).broadcast_to([NT, H, P]), ALU.add))
                        mine.settle()
                        mine.did(dve.tensor_reduce(gp_cmax[0:NT], gp_val[0:NT], AX.X, ALU.max))
                        mine.settle()
                        dve.tensor_tensor(gp_nmax[0:NT], gp_nmax[0:NT], gp_cmax[0:NT], ALU.max).then_inc(max_free, 1)
                        dve.wait_ge(max_free, j * CH + i + 2)
                    mine.start(tile_base + CH * MAX_STEPS + 1)
                    mine.did(dve.tensor_tensor(gp_zmax[0:NT], gp_nmax[0:NT], ed, ALU.add))
                    dve.tensor_copy(gp_edm[0:NT, 0:H], ed)
                    dve.memset(gp_acc[0:NT], 0.0)
                    mine.settle()
                    mine.did(dve.scalar_tensor_tensor(gp_edm[0:NT, H:2 * H], gp_zmax[0:NT], SLOPE, gp_zmax[0:NT], ALU.mult, ALU.max))
                    mine.settle(alone=passed)
                    with dve.Fori(0, CH) as i:
                        mine.start(tile_base + CH * MAX_STEPS + 3 + i * SUM_STEPS)
                        dve.wait_ge(sum_in, i * 64 + 64)
                        mine.did(dve.tensor_scalar(gp_rel[:], gp_dst[:], base[:, bass.ds(j, 1)], None, ALU.subtract))
                        mine.settle()
                        dve.tensor_scalar(gp_onehot[:], iota[:], gp_rel[:], None, ALU.is_equal)
                        dve.tensor_scalar(gp_onehot_t[0:NT], gp_dst_row[0:NT], here, None, ALU.is_equal).then_inc(sum_masks, 1)
                        dve.wait_ge(sum_edge, j * CH + i + 1)
                        dve.wait_ge(sum_rows, i * 16 + 16)
                        mine.did(dve.tensor_tensor(gp_z, gp_rows[:, D:ROW], bankB[:, 0:H], ALU.add))
                        mine.settle()
                        mine.did(dve.scalar_tensor_tensor(gp_l, gp_z, SLOPE, gp_z, ALU.mult, ALU.max))
                        mine.settle()
                        mine.did(dve.tensor_tensor(gp_l, gp_l, bankB[:, H:2 * H], ALU.subtract))
                        mine.settle()
                        dve.tensor_scalar(gp_l, gp_l, 0.0, None, ALU.min).then_inc(sum_logit, 1)
                        dve.wait_ge(sum_ex, j * CH + i + 1)
                        mine.did(dve.tensor_scalar(gp_w, gp_rows[:, D:ROW], gp_dist[:], None, ALU.mult))
                        mine.settle()
                        rows = gp_rows[:, 0:D].rearrange("e (h c) -> e h c", h=H)
                        dve.tensor_tensor(rows, rows, gp_w.unsqueeze(2).broadcast_to([P, H, DH]), ALU.mult).then_inc(sum_msg, 1)
                        dve.wait_ge(sum_agg, j * CH + i + 1)
                        dve.tensor_tensor(gp_acc[0:NT], gp_acc[0:NT], bankE[0][0:NT, 0:ROW], ALU.add).then_inc(sum_free, 1)
                        dve.wait_ge(sum_free, j * CH + i + 2)
                    mine.start(tile_base + CH * (MAX_STEPS + SUM_STEPS) + 3)
                    mine.did(dve.tensor_scalar(gp_den[0:NT], gp_acc[0:NT, D:ROW], TINY, None, ALU.max))
                    mine.settle()
                    mine.did(dve.reciprocal(gp_den[0:NT], gp_den[0:NT]))
                    mine.settle()
                    dve.wait_ge(res_free, j + 1)
                    dve.memset(gp_res[0:NT, D:ROW], 0.0)
                    dve.tensor_tensor(gp_res[0:NT, 0:D].rearrange("n (h c) -> n h c", h=H),
                                      gp_acc[0:NT, 0:D].rearrange("n (h c) -> n h c", h=H),
                                      gp_den[0:NT].unsqueeze(2).broadcast_to([NT, H, DH]), ALU.mult).then_inc(res_ready, 1)
                    dve.wait_ge(res_ready, j + 1)
                dve.tensor_copy(plan_i[:, 0:TILES], base_i[0:1, :]).then_inc(gp_plan, 1)

            general(dve, path)

            def shift_dst(g):
                dve.wait_ge(win_in[g.par], (g.half + 1) * PER_WIN)
                for u in range(2):
                    ins = dve.tensor_scalar(rel[:, u, :, :], dst_win[:, g.par, u, :].unsqueeze(2).broadcast_to([P, TE, H]),
                                            base[:, bass.ds(g.n * 2 + u, 1)], None,
                                            ALU.subtract)
                ins.then_inc(rel_ready, 1)

            def segments(g):
                dve.wait_ge(turn_kept, g.n + 1)
                own.did(dve.tensor_tensor(change[:, :, 1:P], turned[:, :, 1, 1:P], turned[:, :, 1, 0:P - 1], ALU.not_equal))
                own.settle()
                own.did(dve.tensor_scalar(reset[:], change[:, :, 0:P], -BIG, None, ALU.mult))
                own.settle()
                for u in range(2):
                    ins = dve.tensor_tensor_scan(scan[:, u, :], reset[:, u, :], turned[:, u, 0, :], -BIG, ALU.add, ALU.max)
                own.did(ins)
                own.settle()
                dve.tensor_tensor(scan_end[:], scan[:], change[:, :, 1:P + 1], ALU.mult).then_inc(seg_done, 1)

            def make_onehot(g):
                if not g.begins(1):
                    dve.wait_ge(agg_done, g.n * 2)
                for u in range(2):
                    ins = dve.tensor_tensor(onehot[:, u, :, :], iota[:].unsqueeze(1).broadcast_to([P, TE, NT]),
                                            rel[:, u, :, 0:1].broadcast_to([P, TE, NT]), ALU.is_equal)
                ins.then_inc(onehot_ready, 1)

            def make_onehot_t(g):
                dve.wait_ge(dstT_in, g.n * 32 + 32)
                for u in range(2):
                    ins = dve.tensor_scalar(onehot_t[0:NT, u, :], onehot_t[0:NT, u, :].bitcast(I32),
                                            node[0:NT, bass.ds(g.n * 2 + u, 1)], None, ALU.is_equal)
                ins.then_inc(onehotT_ready, 1)

            def node_maxima(g):
                dve.wait_ge(nodes_done, g.n + 1)
                cols = bankC[0:NT, 0:2 * TE * 2 * H].rearrange("n (c k h) -> n c k h", k=2, h=H)
                flat = [a[0:NT].rearrange("n u (t h) -> n (u t) h", h=H) for a in (nmask, nval)]
                own.did(dve.tensor_scalar(flat[0], cols[:, :, 1, :], -1.0, BIG, ALU.add, ALU.mult))
                own.settle()
                own.did(dve.tensor_tensor(flat[1], cols[:, :, 0, :], flat[0], ALU.add))
                own.settle()
                own.did(dve.tensor_reduce(nmax[0:NT], nval[0:NT].rearrange("n u (t h) -> n u h t", h=H), AX.X, ALU.max))
                own.settle()
                pair_dst = edst[0:NT, bass.ds(g.n * 2, 2), :]
                own.did(dve.tensor_tensor(zmax[0:NT], pair_dst, nmax[0:NT], ALU.add))
                dve.tensor_copy(edm[0:NT, :, 0:H], pair_dst)
                own.settle()
                dve.scalar_tensor_tensor(edm[0:NT, :, H:2 * H], zmax[0:NT], SLOPE, zmax[0:NT], ALU.mult, ALU.max
                                         ).then_inc(edm_ready, 1)

            def logits(g):
                dve.wait_ge(edge_done, g.n + 1)
                cols = bankB[:, 0:2 * TE * 2 * H].rearrange("p (c k h) -> p c k h", k=2, h=H)
                own.did(dve.tensor_tensor(z[:], esrc[:].rearrange("p u (t h) -> p (u t) h", h=H),
                                          cols[:, :, 0, :], ALU.add))
                own.settle()
                own.did(dve.scalar_tensor_tensor(lz[:], z[:], SLOPE, z[:], ALU.mult, ALU.max))
                own.settle()
                own.did(dve.tensor_tensor(lz[:], lz[:], cols[:, :, 1, :], ALU.subtract))
                own.settle()
                dve.tensor_scalar(lz[:], lz[:], 0.0, None, ALU.min).then_inc(logit_ready, 1)

            def weigh(g):
                dve.wait_ge(ex_ready, g.n + 1)
                own.did(dve.tensor_tensor(wgt[:], gath[:, g.par, :, :, D:ROW].rearrange("p u t h -> p (u t) h"),
                                          dist_win[:, g.par, :, :].rearrange("p u t -> p (u t)").unsqueeze(2).broadcast_to([P, 2 * TE, H]), ALU.mult))
                own.settle()

            def messages(g, u):
                rows = gath[:, g.par, u, :, 0:D].rearrange("p t (h c) -> p t h c", h=H)
                dve.tensor_tensor(rows, rows, wgt[:, u * TE:(u + 1) * TE, :].unsqueeze(3).broadcast_to([P, TE, H, DH]),
                                  ALU.mult).then_inc(msg_ready, 1)

            def residual(g, u):
                dve.wait_ge(agg_done, g.n * 2 + u + 1)
                own.did(dve.tensor_scalar(rden[0:NT, u, :], bankE[u][0:NT, D:ROW], TINY, None, ALU.max))
                own.settle()
                own.did(dve.reciprocal(rden[0:NT, u, :], rden[0:NT, u, :]))
                own.settle()
                own.did(dve.tensor_tensor(aggn[0:NT, u, :].rearrange("n (h c) -> n h c", h=H),
                                          bankE[u][0:NT, 0:D].rearrange("n (h c) -> n h c", h=H),
                                          rden[0:NT, u, :].unsqueeze(2).broadcast_to([NT, H, DH]), ALU.mult))
                if not g.begins(2):
                    dve.wait_ge(out_stored[g.par], g.half * 16)
                own.settle()
                own.did(dve.tensor_tensor(x1[0:NT, g.par, u, :], aggn[0:NT, u, :], x_res[0:NT, g.par, u, :], ALU.add))
                own.settle()
                own.did(dve.bn_stats(stats[0:NT, u, :], x1[0:NT, g.par, u, :]))
                own.settle(alone=passed)
                dve.bn_aggr(mv[0:NT, u, :], stats[0:NT, u, :]).then_inc(var_ready, 1)

            def norm1(g, u):
                dve.wait_ge(std_ready, g.n * 2 + u + 1)
                own.did(dve.reciprocal(rstd[0:NT, u:u + 1], std[0:NT, u:u + 1]))
                own.settle()
                dve.tensor_scalar(xn[0:NT, u, :], x1[0:NT, g.par, u, :], mv[0:NT, u, 0:1], rstd[0:NT, u:u + 1],
                                  ALU.subtract, ALU.mult).then_inc(xn_ready, 1)

            def gates(f):
                dve.wait_ge(route_done, f.n + 1)
                r = bankC[0:NT, ROUTE:ROUTE + 2 * EX].rearrange("n (u e) -> n u e", u=2)
                own.did(dve.tensor_reduce(rmax[0:NT, :], r, AX.X, ALU.max))
                own.settle()
                dve.tensor_tensor(rsub[0:NT], r, rmax[0:NT, :].unsqueeze(2).broadcast_to([NT, 2, EX]), ALU.subtract
                                  ).then_inc(rsub_ready, 1)
                dve.wait_ge(rexp_ready, f.n + 1)
                own.did(dve.tensor_reduce(rsum[0:NT, :], rexp[0:NT], AX.X, ALU.add))
                own.settle()
                own.did(dve.reciprocal(rinv[0:NT, :], rsum[0:NT, :]))
                own.settle()
                dve.tensor_tensor(gate[0:NT], rexp[0:NT], rinv[0:NT, :].unsqueeze(2).broadcast_to([NT, 2, EX]), ALU.mult
                                  ).then_inc(gate_ready, 1)

            def add_y(f, k):
                dve.wait_ge(y_done, f.n * YS + k + 1)
                if k:
                    dve.wait_ge(y_added, f.n * YS + k)
                acc = x1[0:NT, f.par, :, :]
                if k == 0:
                    dve.wait_ge(gate_ready, f.n + 1)
                    dve.tensor_tensor(acc.rearrange("n u c -> n (u c)"), bankY[0:NT, :], acc.rearrange("n u c -> n (u c)"),
                                      ALU.add).then_inc(y_added, 1)
                    return
                for u in range(2):
                    ins = dve.scalar_tensor_tensor(acc[:, u, :], bankY[0:NT, u * D:(u + 1) * D], gate[0:NT, u, k - 1:k],
                                                   acc[:, u, :], ALU.mult, ALU.add)
                ins.then_inc(y_added, 1)

            before = own.base + own.count

            def body(f, g, first=0):
                own.start(before if f is None else before + GNN_STEPS + f.n * (GNN_STEPS + FFN_STEPS))

                def a(stage, *more):
                    if g is not None:
                        stage(g, *more)

                def b(stage, *more):
                    if f is not None:
                        stage(f, *more)

                b(gates)
                a(shift_dst)
                a(segments)
                a(make_onehot)
                b(add_y, 0)
                a(make_onehot_t)
                b(add_y, 1)
                a(node_maxima)
                b(add_y, 2)
                a(logits)
                b(add_y, 3)
                a(weigh)
                a(messages, 0)
                b(add_y, 4)
                a(messages, 1)
                b(add_y, 5)
                a(residual, 0)
                a(norm1, 0)
                a(residual, 1)
                a(norm1, 1)
                b(add_y, 6)
                b(add_y, 7)
                b(add_y, 8)
                assert own.count == GNN_STEPS * (g is not None) + FFN_STEPS * (f is not None), own.count

            body(None, Pair(0, 0))
            over_pairs(dve, 0, NP - 1, lambda f: body(f, f + 1), peel=1)
            body(Pair(0, NP - 1), None)


INS = ["x", "src", "dst", "edge_attr3_1x1", "L0_gnn_W", "L0_gnn_w_att_src", "L0_gnn_w_att_dst", "L0_ffn_Wr", "L0_ffn_br",
       "L0_ffn_W1", "L0_ffn_b1", "L0_ffn_g1", "L0_ffn_be1", "L0_ffn_m1", "L0_ffn_v1", "L0_ffn_W2", "L0_ffn_b2",
       "L0_ffn_g2", "L0_ffn_be2", "L0_ffn_m2", "L0_ffn_v2", "L0_ffn_Wo", "L0_ffn_bo"]


def kernel(**inputs):
    import numpy as np
    import concourse.bacc as bacc
    from concourse.bass_utils import run_bass_kernel_spmd

    nc = bacc.Bacc("TRN2", target_bir_lowering=False, num_devices=1)
    arrays, args = {}, []
    for name in INS:
        a = np.ascontiguousarray(inputs[name])
        arrays[f"in_{name}"] = a
        args.append(nc.dram_tensor(f"in_{name}", a.shape, mybir.dt.from_np(a.dtype), kind="ExternalInput").ap())
    out = nc.dram_tensor("out", arrays["in_x"].shape, F32, kind="ExternalOutput").ap()
    gnn_ffn_kernel(nc, *args, out)
    return run_bass_kernel_spmd(nc, [arrays], core_ids=[0]).results[0]["out"]
```

```python
from contextlib import ExitStack

import concourse.bass as bass
from concourse import mybir

ALU = mybir.AluOpType
ACT = mybir.ActivationFunctionType
AX = mybir.AxisListType
F32 = mybir.dt.float32
I32 = mybir.dt.int32
U32 = mybir.dt.uint32
BF16 = mybir.dt.bfloat16

P = 128
NT = 125
D = 256
KC = D // P
H = 4
DH = D // H
ROW = D + H
ROWX = ROW + H
TE = 18
WIN = P * TE
TH = TE * H
EX = 8
SLOPE = 0.2
LN_EPS = 1e-5
BN_EPS = 1e-3
BIG = 1e37
TINY = 1e-30
RING = 2
PARTS = 3
NCOL = PARTS * H + 1
YS = EX + 1
SMALL_RUN = 6
MAXIMA_STEPS = 16
SUMS_STEPS = 19


class Pair:

    def __init__(self, k, off):
        self.k, self.off = k, off

    @property
    def n(self):
        return self.off if isinstance(self.k, int) else self.k * 2 + self.off

    @property
    def half(self):
        return self.off // 2 if isinstance(self.k, int) else self.k + self.off // 2

    @property
    def par(self):
        return self.off % 2

    def begins(self, d):
        return isinstance(self.k, int) and self.off < d

    def within(self, count):
        return not isinstance(self.k, int) or self.off < count

    def __add__(self, d):
        return Pair(self.k, self.off + d)


def over_pairs(eng, lo, hi, body, peel=0, tail=0):
    first, hi = lo, hi - tail
    for n in range(peel):
        if first < hi:
            body(Pair(0, first))
            first += 1
    turns = (hi - first) // 2
    if turns > 0:
        with eng.Fori(0, turns) as k:
            body(Pair(k, first))
            body(Pair(k, first + 1))
    for n in range(hi - (hi - first) % 2, hi + tail):
        body(Pair(0, n))


def over_stages(eng, pairs, body, tail=0):
    body(None, None, Pair(0, 0))
    body(None, Pair(0, 0), Pair(0, 1))
    over_pairs(eng, 0, pairs - 2, lambda f: body(f, f + 1, f + 2), peel=1, tail=tail)
    body(Pair(0, pairs - 2), Pair(0, pairs - 1), None)
    body(Pair(0, pairs - 1), None, None)


def before(f, s, steps):
    return (f, s - steps) if s >= steps else (f + -1, s - steps + EX)


class Chain:

    def __init__(self, eng, sem):
        self.eng, self.sem, self.base, self.count = eng, sem, 0, 0

    def start(self, base):
        self.base, self.count = base, 0

    def did(self, ins):
        ins.then_inc(self.sem, 1)
        self.count += 1

    def settle(self, alone=None):
        self.eng.wait_ge(self.sem, self.base + self.count)
        if alone is not None:
            self.eng.sem_inc(alone, 1)


def gnn_ffn_kernel(nc, x, src, dst, dist, W, att_src, att_dst, Wr, br, W1, b1, g1, be1, m1, v1, W2, b2, g2, be2,
                   m2, v2, Wo, bo, out):
    N = x.shape[0]
    E = src.shape[0]
    TILES = N // NT
    NP = TILES // 2
    EB = E // NT
    assert NP * 2 * NT == N and EB * NT == E and TILES + 1 <= P and NP >= 4
    EPAD = (-(E + WIN)) % P
    PADDED = E + WIN + EPAD

    with ExitStack() as ctx:
        def sb(name, shape, dt=F32):
            return ctx.enter_context(nc.sbuf_tensor(name, shape, dt))

        def bank(name):
            return ctx.enter_context(nc.psum_tensor(name, [P, 512], F32))

        def sem(name):
            return ctx.enter_context(nc.semaphore(name))

        table = nc.dram_tensor("table", [N, ROW], F32, kind="Internal").ap()
        src_pad = nc.dram_tensor("src_pad", [PADDED], I32, kind="Internal").ap()
        dst_pad = nc.dram_tensor("dst_pad", [PADDED + P], I32, kind="Internal").ap()
        dist_pad = nc.dram_tensor("dist_pad", [PADDED], F32, kind="Internal").ap()

        ident = sb("ident", [P, P])
        iota_i = sb("iota_i", [P, NT], I32)
        iota = sb("iota", [P, NT])
        base_i = sb("base_i", [P, TILES], I32)
        base = sb("base", [P, TILES])
        node_i = sb("node_i", [P, TILES], I32)
        node = sb("node", [P, TILES])
        ids_i = sb("ids_i", [P, TILES], I32)
        bound_i = sb("bound_i", [P, 1], I32)
        bound = sb("bound", [P, 1])
        ones = sb("ones", [P, P])
        eps_ln = sb("eps_ln", [P, 1])
        pad_fill = sb("pad_fill", [P, TE], I32)
        neg_fill = sb("neg_fill", [P, TE], I32)

        w1 = sb("w1", [P, EX * KC, D])
        w2 = sb("w2", [P, EX * KC, D])
        wo = sb("wo", [P, EX * KC, D])
        wr = sb("wr", [P, KC, EX])
        br_row = sb("br_row", [1, EX])
        bo_rows = sb("bo_rows", [EX, D])
        bn_cols = sb("bn_cols", [P, 2, 5, EX * KC])
        bn_scale = sb("bn_scale", [P, 2, EX * KC])
        bn_shift = sb("bn_shift", [P, 2, EX * KC])
        wx = sb("wx", [P, KC, ROWX])

        edst = sb("edst", [P, TILES, H])
        plan_i = sb("plan_i", [1, P + 1], I32)

        gath = sb("gath", [P, RING, 2, TE, ROW])
        onehot = sb("onehot", [P, 2, TE, NT])
        onehot_b = sb("onehot_b", [P, 2, TE, NT], BF16)
        onehot_t = sb("onehot_t", [P, 2, WIN], BF16)
        dst_row = sb("dst_row", [P, WIN], I32)
        src_win = sb("src_win", [P, RING, 2, TE], U32)
        dst_win = sb("dst_win", [P, RING, 2, TE], I32)
        dist_win = sb("dist_win", [P, RING, 2, TE])
        x_res = sb("x_res", [P, RING, 2, D])
        rel = sb("rel", [P, 2, TE, H])
        esrc = sb("esrc", [P, 2, TH])
        turned = sb("turned", [TH, 2, 2, P])
        change = sb("change", [TH, 2, P + 1])
        reset = sb("reset", [TH, 2, P])
        scan = sb("scan", [TH, 2, P])
        scan_end = sb("scan_end", [TH, 2, P])
        ends = sb("ends", [P, 2, TE, NCOL], BF16)
        ends_rest = sb("ends_rest", [P, 2, TE, H])
        nmask = sb("nmask", [P, 2 * TE, 1])
        nval = sb("nval", [P, 2, TH])
        nmax = sb("nmax", [P, 2, H])
        zmax = sb("zmax", [P, 2, H])
        edm = sb("edm", [P, 2, 2 * H])
        edm_rest = sb("edm_rest", [P, 2, 2 * H])
        edm_parts = sb("edm_parts", [P, PARTS, 2, 2 * H], BF16)
        z = sb("z", [P, 2 * TE, H])
        lz = sb("lz", [P, 2 * TE, H])
        wgt = sb("wgt", [P, 2 * TE, H])
        rden = sb("rden", [P, 2, H])
        stats = sb("stats", [P, 2, 6])
        mv = sb("mv", [P, 2, 2])
        std = sb("std", [P, 2])
        rstd = sb("rstd", [P, 2])
        xn = sb("xn", [P, 2, D])
        x1 = sb("x1", [P, RING, 2, D])
        xT = sb("xT", [P, RING, KC, 2, NT])
        rsub = sb("rsub", [P, 2, EX])
        rexp = sb("rexp", [P, 2, EX])
        rmax = sb("rmax", [P, 2])
        rsum = sb("rsum", [P, 2])
        rinv = sb("rinv", [P, 2])
        gate = sb("gate", [P, RING, 2, EX])
        gate_t = sb("gate_t", [EX, 2, NT])
        h1 = sb("h1", [P, KC, 2, NT])
        h2 = sb("h2", [P, KC, 2, NT])

        bankA, bankB, bankC = bank("bankA"), bank("bankB"), bank("bankC")
        bankE = [bank("bankE0"), bank("bankE1")]
        bankH1, bankH2, bankY = bank("bankH1"), bank("bankH2"), bank("bankY")

        attn_in, small_in, pads_src = sem("attn_in"), sem("small_in"), sem("pads_src")
        weights_in = sem("weights_in")
        consts = sem("consts")
        dve_step = sem("dve_step")
        act_step = sem("act_step")
        fills = sem("fills")
        wx_ready, bn_turned, bn_sum, bn_root, bn_ready = (
            sem("wx_ready"), sem("bn_turned"), sem("bn_sum"), sem("bn_root"), sem("bn_ready"))
        t_x = [sem("t_x0"), sem("t_x1")]
        t_var, t_std, t_norm, t_turned, t_xT, t_ft, t_rows = (
            sem("t_var"), sem("t_std"), sem("t_norm"), sem("t_turned"), sem("t_xT"), sem("t_ft"), sem("t_rows"))
        t_stored = [sem("t_stored0"), sem("t_stored1")]
        p_in, p_first, p_coarse, p_block, p_fetched, p_row, p_flag, p_ready = (
            sem("p_in"), sem("p_first"), sem("p_coarse"), sem("p_block"), sem("p_fetched"), sem("p_row"),
            sem("p_flag"), sem("p_ready"))
        setup_done = sem("setup_done")
        passed = sem("passed")
        win_in = [sem("win_in0"), sem("win_in1")]
        x_in = [sem("x_in0"), sem("x_in1")]
        dst_row_in = sem("dst_row_in")
        rows_in = [sem("rows_in0"), sem("rows_in1")]
        esrc_kept = sem("esrc_kept")
        ends_ready, onehot_kept = sem("ends_ready"), sem("onehot_kept")
        rel_ready, turn_done, turn_kept, seg_done, back_done = (
            sem("rel_ready"), sem("turn_done"), sem("turn_kept"), sem("seg_done"), sem("back_done"))
        onehot_ready, onehotT_ready, nodes_done, edm_ready, edge_done = (
            sem("onehot_ready"), sem("onehotT_ready"), sem("nodes_done"), sem("edm_ready"), sem("edge_done"))
        logit_ready, ex_ready, msg_ready, agg_done = (
            sem("logit_ready"), sem("ex_ready"), sem("msg_ready"), sem("agg_done"))
        var_ready, std_ready, xn_ready, xT_done, xT_ready = (
            sem("var_ready"), sem("std_ready"), sem("xn_ready"), sem("xT_done"), sem("xT_ready"))
        route_done, rsub_ready, rexp_ready, gate_ready, gateT_done, gateT_kept = (
            sem("route_done"), sem("rsub_ready"), sem("rexp_ready"), sem("gate_ready"), sem("gateT_done"),
            sem("gateT_kept"))
        h1_done, h1_kept, h2_done, h2_kept, y_done, y_added = (
            sem("h1_done"), sem("h1_kept"), sem("h2_done"), sem("h2_kept"), sem("y_done"), sem("y_added"))
        out_stored = [sem("out_stored0"), sem("out_stored1")]

        table2 = nc.dram_tensor("table2", [N, ROW], F32, kind="Internal").ap()
        CH = -(-E // P)
        gp_rows = gath[:, 0, 0, 0, :]
        gp_acc = gath[:, 0, 0, 1, :]
        gp_res = gath[:, 0, 0, 2, :]
        gp_dst_row = gath[:, 0, 1, 0, 0:P].bitcast(I32)
        gp_away = gath[:, 0, 1, 1, 0:P]
        gp_val = gath[:, 0, 1, 2:4, :].rearrange("p a c -> p (a c)")[:, 0:H * P].rearrange("p (h e) -> p h e", h=H)
        gp_onehot = gath[:, 0, 1, 4, 0:NT]
        gp_onehot_t = gath[:, 0, 1, 5, 0:P]
        gp_nmax, gp_cmax, gp_zmax = (gath[:, 0, 1, 6, i * H:(i + 1) * H] for i in range(3))
        gp_edm = gath[:, 0, 1, 7, 0:2 * H]
        gp_z, gp_l, gp_w, gp_den = (gath[:, 0, 1, 8, i * H:(i + 1) * H] for i in range(4))
        gp_src = sb("gp_src", [P, 1], U32)
        gp_dst = sb("gp_dst", [P, 1], I32)
        gp_dist = sb("gp_dist", [P, 1])
        gp_rel = sb("gp_rel", [P, 1])
        table_ready = sem("table_ready")
        gp_dve = sem("gp_dve")
        max_in, max_rows, sum_in, sum_rows = sem("max_in"), sem("max_rows"), sem("sum_in"), sem("sum_rows")
        max_spread = sem("max_spread")
        max_free, sum_free, tile_go, res_free = sem("max_free"), sem("sum_free"), sem("tile_go"), sem("res_free")
        sum_masks, sum_edge, sum_logit, sum_ex, sum_msg, sum_agg = (
            sem("sum_masks"), sem("sum_edge"), sem("sum_logit"), sem("sum_ex"),
            sem("sum_msg"), sem("sum_agg"))
        res_ready, res_stored, gp_tables, gp_plan = sem("res_ready"), sem("res_stored"), sem("gp_tables"), sem("gp_plan")
        MAX_STEPS, SUM_STEPS, TILE_STEPS = 3, 5, 5

        def general(eng, path):
            eng.wait_ge(p_ready, 1)
            flag = eng.value_load(plan_i[0:1, P:P + 1], min_val=0, max_val=2 * P)
            with eng.If(flag > 0):
                path()

        xin = x_res
        xnt = x1
        ft_rows = gath[:, 0, 0, 0:4, :].rearrange("p (r u) c -> p r u c", r=2)
        dst_all = gath[:, 1, 0, :, :].rearrange("p t c -> p (t c)")[:, 0:EB].bitcast(I32)
        dst_prev = gath[:, 1, 1, :, :].rearrange("p t c -> p (t c)")[:, 0:EB].bitcast(I32)
        bn_rows = gath[:, 1, 0, :, :].rearrange("p t c -> p (t c)")[:, EB:EB + 2 * P].rearrange("p (l c) -> p l c", l=2)
        spare = gath[:, 0, 1, :, :].rearrange("p t c -> p (t c)")
        blk = spare[:, 0:EB].bitcast(I32)
        scr = spare[:, EB:2 * EB]
        scr2 = spare[:, 2 * EB:3 * EB]
        att = spare[:, 3 * EB:3 * EB + 2 * D].rearrange("p (k c) -> p k c", k=2)
        att_prod = spare[:, 3 * EB + 2 * D:3 * EB + 3 * D]
        J = TILES + 1
        blk_i = sb("blk_i", [P, 1], I32)
        plan_cols = sb("plan_cols", [P, 5])
        coarse, fine, startf, blkf, bad1 = (plan_cols[:, i:i + 1] for i in range(5))
        plan_f = sb("plan_f", [1, 3 * P + 1])
        first_dst = sb("first_dst", [P, J])

        x_pairs = x.rearrange("(g u p) d -> g p u d", u=2, p=NT)
        out_pairs = out.rearrange("(g u p) d -> g p u d", u=2, p=NT)
        table_pairs = table.rearrange("(g u p) d -> g p u d", u=2, p=NT)

        block = ctx.enter_context(nc.Block())

        PER_WIN = 16 * 6
        PER_ROWS = 16 * 2 * TE

        @block.sync
        def _(sp):
            sp.dma_start(wx[:, :, 0:D], W.rearrange("(c k) n -> k c n", k=P)).then_inc(attn_in, 16)
            sp.dma_start(att[:, 0, :], att_src.rearrange("a h c -> a (h c)").broadcast_to([P, D])).then_inc(attn_in, 16)
            sp.dma_start(att[:, 1, :], att_dst.rearrange("a h c -> a (h c)").broadcast_to([P, D])).then_inc(attn_in, 16)

            def load_x(g):
                if not g.begins(2):
                    sp.wait_ge(t_norm, g.n * 2 - 2)
                sp.dma_start(xin[0:NT, g.par, :, :], x_pairs[g.n]).then_inc(t_x[g.par], 16)

            load_x(Pair(0, 0))
            load_x(Pair(0, 1))
            sp.wait_ge(fills, 1)
            sp.dma_start(dst_pad[1:1 + E].rearrange("(a b) -> a b", a=NT), dst.rearrange("(a b) -> a b", a=NT)).then_inc(pads_src, 16)
            sp.dma_start(src_pad[0:E].rearrange("(a b) -> a b", a=NT), src.rearrange("(a b) -> a b", a=NT)).then_inc(pads_src, 16)
            sp.dma_start(dist_pad[0:E].rearrange("(a b) -> a b", a=NT),
                         dist.rearrange("(a b) c d -> a (b c d)", a=NT)).then_inc(pads_src, 16)
            sp.dma_start(src_pad[E:E + WIN].rearrange("(a b) -> a b", a=P), pad_fill[:, 0:TE]).then_inc(pads_src, 16)
            sp.dma_start(dist_pad[E:E + WIN].rearrange("(a b) -> a b", a=P).bitcast(I32), pad_fill[:, 0:TE]).then_inc(pads_src, 16)
            sp.dma_start(dst_all[0:NT, :], dst.rearrange("(a b) -> a b", a=NT)).then_inc(p_in, 16)
            sp.wait_ge(fills, 2)
            sp.dma_start(dst_pad[1 + E:1 + E + WIN].rearrange("(a b) -> a b", a=P), neg_fill[:, 0:TE]).then_inc(pads_src, 16)
            sp.dma_start(dst_pad[0:1].rearrange("(a b) -> a b", a=1), neg_fill[0:1, 0:1]).then_inc(pads_src, 16)
            sp.wait_ge(pads_src, 16 * 7)
            sp.dma_start(dst_prev[0:NT, :], dst_pad[0:E].rearrange("(a b) -> a b", a=NT)).then_inc(p_in, 16)
            over_pairs(sp, 2, NP, load_x)

            sp.wait_ge(t_stored[0], 16 * ((NP + 1) // 2))
            sp.wait_ge(t_stored[1], 16 * (NP // 2))
            sp.nop().then_inc(table_ready, 1)

            def path():
                sp.sem_inc(res_free, 1)
                with sp.Fori(0, TILES) as j:
                    sp.wait_ge(res_ready, j + 1)
                    sp.dma_start(table2[bass.ds(j * NT, NT), :], gp_res[0:NT, :]).then_inc(res_stored, 16)
                    sp.wait_ge(res_stored, j * 16 + 16)
                    sp.sem_inc(res_free, 1)
                sp.wait_ge(sum_free, TILES * CH + 1)
                sp.dma_start(table.rearrange("(a b) c -> a (b c)", a=NT), table2.rearrange("(a b) c -> a (b c)", a=NT)).then_inc(gp_tables, 16)
                sp.dma_start(src_pad[0:N].rearrange("(p j) -> p j", p=NT), ids_i[0:NT, :]).then_inc(gp_tables, 16)
                sp.dma_start(dst_pad[1:1 + N].rearrange("(p j) -> p j", p=NT), ids_i[0:NT, :]).then_inc(gp_tables, 16)
                sp.dma_start(dst_pad[1 + N:1 + N + WIN].rearrange("(a b) -> a b", a=P), neg_fill[:, 0:TE]).then_inc(gp_tables, 16)
                sp.dma_start(dist_pad[0:N].rearrange("(p j) -> p j", p=NT), ones[0:NT, 0:TILES]).then_inc(gp_tables, 16)
                sp.wait_ge(gp_tables, 16 * 5)
                sp.wait_ge(gp_plan, 1)

            general(sp, path)
            sp.nop().then_inc(setup_done, 1)

            def load_windows(g):
                for u in range(2):
                    first = sp.value_load(plan_i[0:1, bass.ds(g.n * 2 + u, 1)], min_val=0, max_val=E)
                    for buf, dram, off in ((src_win, src_pad.bitcast(U32), 0), (dst_win, dst_pad, 1), (dist_win, dist_pad, 0)):
                        sp.dma_start(buf[:, g.par, u, :], dram[bass.ds(first + off, WIN)].rearrange("(p t) -> p t", t=TE)).then_inc(win_in[g.par], 16)

            def load_res(g):
                sp.dma_start(x_res[0:NT, g.par, :, :], x_pairs[g.n]).then_inc(x_in[g.par], 16)

            def load_dst_row(g, u):
                if not g.begins(1) or u:
                    sp.wait_ge(onehotT_ready, g.n * 2 + u)
                    sp.sem_inc(passed, 1)
                first = sp.value_load(plan_i[0:1, bass.ds(g.n * 2 + u, 1)], min_val=0, max_val=E)
                sp.dma_start(dst_row[:], dst_pad[bass.ds(first + 1, WIN)].rearrange("(a t) -> a t", a=1).broadcast_to([P, WIN])
                             ).then_inc(dst_row_in, 16)

            def store(f):
                sp.wait_ge(y_added, f.n * YS + YS)
                sp.sem_inc(passed, 1)
                sp.dma_start(out_pairs[f.n], x1[0:NT, f.par, :, :]).then_inc(out_stored[f.par], 16)

            load_windows(Pair(0, 0))
            load_dst_row(Pair(0, 0), 0)
            load_windows(Pair(0, 1))
            load_res(Pair(0, 0))
            load_res(Pair(0, 1))

            def body(f, g, a):
                reload = g is not None and (g + 2).within(NP)
                if reload:
                    sp.wait_ge(msg_ready, g.n * 2 + 1)
                    sp.sem_inc(passed, 1)
                    load_windows(g + 2)
                if f is not None and not f.begins(1):
                    store(f + -1)
                if a is not None:
                    load_dst_row(a, 1)
                if reload:
                    sp.wait_ge(xn_ready, g.n * 2 + 2)
                    sp.sem_inc(passed, 1)
                    load_res(g + 2)
                if a is not None and (a + 1).within(NP):
                    load_dst_row(a + 1, 0)

            over_stages(sp, NP, body, tail=1)
            store(Pair(0, NP - 1))
            sp.wait_ge(out_stored[0], 16 * ((NP + 1) // 2))
            sp.wait_ge(out_stored[1], 16 * (NP // 2))

        @block.gpsimd
        def _(pool):
            pool.memset(ident[:], 1.0).then_inc(consts, 1)
            pool.memset(pad_fill[:], 0).then_inc(fills, 1)
            pool.memset(neg_fill[:], -1).then_inc(fills, 1)
            pool.memset(ones[:], 1.0).then_inc(consts, 1)
            pool.memset(eps_ln[:], LN_EPS).then_inc(consts, 1)
            pool.wait_ge(consts, 3)
            pool.affine_select(out=ident[:], in_=ident[:], compare_op=ALU.is_equal, fill=0.0, base=0,
                               pattern=[[1, P]], channel_multiplier=-1).then_inc(consts, 1)
            pool.iota(iota_i[:], [[1, NT]], base=0, channel_multiplier=0).then_inc(consts, 1)
            pool.iota(base_i[:], [[NT, TILES]], base=0, channel_multiplier=0).then_inc(consts, 1)
            pool.iota(node_i[:], [[NT, TILES]], base=0, channel_multiplier=1).then_inc(consts, 1)
            pool.iota(ids_i[:], [[1, TILES]], base=0, channel_multiplier=TILES).then_inc(consts, 1)
            pool.iota(bound_i[:], [[1, 1]], base=0, channel_multiplier=NT).then_inc(consts, 1)
            pool.wait_ge(p_block, 1)
            pool.indirect_dma_start(blk[0:J, :], None, dst.rearrange("(a b) -> a b", a=NT),
                                    bass.IndirectOffsetOnAxis(blk_i[0:J, 0:1].bitcast(U32), 0)).then_inc(p_fetched, 16)
            def path():
                pool.wait_ge(table_ready, 1)
                pool.sem_inc(tile_go, 1)
                with pool.Fori(0, TILES) as j:
                    with pool.Fori(0, CH) as i:
                        pool.wait_ge(max_free, j * CH + i + 1)
                        pool.dma_start(gp_src[:], src_pad[bass.ds(i * P, P)].rearrange("(p a) -> p a", a=1).bitcast(U32)).then_inc(max_in, 16)
                        pool.dma_start(gp_dst_row, dst_pad[bass.ds(i * P + 1, P)].rearrange("(a e) -> a e", a=1).broadcast_to([P, P])).then_inc(max_in, 16)
                        pool.wait_ge(max_in, i * 32 + 32)
                        pool.sem_inc(passed, 1)
                        pool.indirect_dma_start(gp_rows, None, table, bass.IndirectOffsetOnAxis(gp_src[:, 0:1], 0)).then_inc(max_rows, 16)
                    pool.wait_ge(max_free, j * CH + CH + 1)
                    pool.sem_inc(passed, 1)
                    with pool.Fori(0, CH) as i:
                        pool.wait_ge(sum_free, j * CH + i + 1)
                        pool.dma_start(gp_src[:], src_pad[bass.ds(i * P, P)].rearrange("(p a) -> p a", a=1).bitcast(U32)).then_inc(sum_in, 16)
                        pool.dma_start(gp_dst[:], dst_pad[bass.ds(i * P + 1, P)].rearrange("(p a) -> p a", a=1)).then_inc(sum_in, 16)
                        pool.dma_start(gp_dist[:], dist_pad[bass.ds(i * P, P)].rearrange("(p a) -> p a", a=1)).then_inc(sum_in, 16)
                        pool.dma_start(gp_dst_row, dst_pad[bass.ds(i * P + 1, P)].rearrange("(a e) -> a e", a=1).broadcast_to([P, P])).then_inc(sum_in, 16)
                        pool.wait_ge(sum_in, i * 64 + 64)
                        pool.sem_inc(passed, 1)
                        pool.indirect_dma_start(gp_rows, None, table, bass.IndirectOffsetOnAxis(gp_src[:, 0:1], 0)).then_inc(sum_rows, 16)
                    pool.wait_ge(sum_free, j * CH + CH + 1)
                    pool.sem_inc(passed, 1)
                    pool.inc_swdge_sem([max_in, max_rows, sum_in, sum_rows], [32 * CH, 16 * CH, 64 * CH, 16 * CH], mode="sub")
                    pool.nop().then_inc(tile_go, 1)

            general(pool, path)
            pool.wait_ge(setup_done, 1)

            def gather(g):
                pool.wait_ge(win_in[g.par], (g.half + 1) * PER_WIN)
                pool.sem_inc(passed, 1)
                for u in range(2):
                    if not g.begins(2):
                        pool.wait_ge(agg_done, g.n * 2 - 3 + u)
                        pool.sem_inc(passed, 1)
                    for t in range(TE):
                        pool.indirect_dma_start(gath[:, g.par, u, t, :], None, table,
                                                bass.IndirectOffsetOnAxis(src_win[:, g.par, u, t:t + 1], 0)
                                                ).then_inc(rows_in[g.par], 16)

            over_pairs(pool, 0, NP, gather, peel=2)

        @block.tensor
        def _(pe):
            pe.wait_ge(consts, 9)
            pe.wait_ge(small_in, 16 * 13)
            for l in range(2):
                mm = pe.transpose(bankC[:, l * 80:l * 80 + 80], bn_rows[0:80, l, :], ident[0:80, 0:80])
            mm.then_inc(bn_turned, 1)

            def turn_x(g):
                pe.wait_ge(t_norm, g.n * 2 + 2)
                if not g.begins(1):
                    pe.wait_ge(t_xT, g.n)
                for u in range(2):
                    for c in range(KC):
                        mm = pe.transpose(bankA[:, (u * KC + c) * NT:(u * KC + c + 1) * NT],
                                          xnt[0:NT, g.par, u, c * P:(c + 1) * P], ident[0:NT, 0:NT])
                mm.then_inc(t_turned, 1)

            def project(g):
                pe.wait_ge(t_xT, g.n + 1)
                if not g.begins(1):
                    pe.wait_ge(t_rows, g.n * 2)
                for u in range(2):
                    for c in range(KC):
                        mm = pe.matmul(bankE[u][0:NT, 0:ROWX], xT[:, g.par, c, u, :], wx[:, c, :],
                                       start=(c == 0), stop=(c == KC - 1))
                    mm.then_inc(t_ft, 1)

            pe.wait_ge(wx_ready, 1)
            turn_x(Pair(0, 0))
            pe.wait_ge(p_first, 1)
            pe.matmul(bankH1[0:J, 0:NT], first_dst[0:NT, :], ident[0:NT, 0:NT], start=True, stop=True).then_inc(p_coarse, 1)

            def table_turn(g):
                turn_x(g)
                project(g + -1)

            over_pairs(pe, 1, NP, table_turn, peel=1)
            project(Pair(0, NP - 1))
            pe.wait_ge(p_row, 1)
            pe.matmul(bankH2[0:1, 0:J], startf[0:J, :], ident[0:J, 0:J], start=True, stop=True)
            pe.matmul(bankH2[0:1, P:P + 1], bad1[0:NT, :], ones[0:NT, 0:1], start=True, stop=True).then_inc(p_flag, 1)

            def turn_logits(g):
                pe.wait_ge(rel_ready, g.n + 1)
                pe.wait_ge(esrc_kept, g.n + 1)
                for u in range(2):
                    pe.transpose(bankA[0:TH, u * 2 * P:u * 2 * P + P], esrc[:, u, :], ident[:, :])
                    mm = pe.transpose(bankA[0:TH, u * 2 * P + P:(u + 1) * 2 * P],
                                      rel[:, u, :, :].rearrange("p t h -> p (t h)"), ident[:, :])
                mm.then_inc(turn_done, 1)

            def turn_back(g):
                pe.wait_ge(seg_done, g.n + 1)
                for u in range(2):
                    pe.transpose(bankB[:, (u * 2) * TH:(u * 2 + 1) * TH], scan_end[:, u, :], ident[0:TH, 0:TH])
                    mm = pe.transpose(bankB[:, (u * 2 + 1) * TH:(u * 2 + 2) * TH], change[:, u, 1:P + 1],
                                      ident[0:TH, 0:TH])
                mm.then_inc(back_done, 1)

            def to_nodes(g):
                pe.wait_ge(onehot_ready, g.n * 2 + 2)
                pe.wait_ge(ends_ready, g.n + 1)
                for u in range(2):
                    for t in range(TE):
                        col = (u * TE + t) * NCOL
                        mm = pe.matmul(bankC[0:NT, col:col + NCOL], onehot_b[:, u, t, :], ends[:, u, t, :],
                                       start=True, stop=True)
                        if u * TE + t == 2 * TE - 1:
                            mm.then_inc(nodes_done, 1)
                        yield

            def to_edges(g):
                pe.wait_ge(onehotT_ready, g.n * 2 + 2)
                pe.wait_ge(edm_ready, g.n + 1)
                for u in range(2):
                    for t in range(TE):
                        col = (u * TE + t) * 2 * H
                        for part in range(PARTS):
                            mm = pe.matmul(bankB[:, col:col + 2 * H], onehot_t[0:NT, u, t:WIN:TE], edm_parts[0:NT, part, u, :],
                                           start=(part == 0), stop=(part == PARTS - 1))
                        if u * TE + t == 2 * TE - 1:
                            mm.then_inc(edge_done, 1)
                        yield

            def aggregate(g, u):
                pe.wait_ge(onehot_kept, g.n * 2 + u + 1)
                pe.wait_ge(msg_ready, g.n * 2 + u + 1)
                for t in range(TE):
                    mm = pe.matmul(bankE[u][0:NT, 0:ROW], onehot[:, u, t, :], gath[:, g.par, u, t, :],
                                   start=(t == 0), stop=(t == TE - 1))
                mm.then_inc(agg_done, 1)

            def turn_x1(g):
                pe.wait_ge(xn_ready, g.n * 2 + 2)
                for u in range(2):
                    for c in range(KC):
                        mm = pe.transpose(bankA[:, (c * 2 + u) * NT:(c * 2 + u + 1) * NT],
                                          xn[0:NT, u, c * P:(c + 1) * P], ident[0:NT, 0:NT])
                mm.then_inc(xT_done, 1)

            def route(g):
                pe.wait_ge(xT_ready, g.n + 1)
                for u in range(2):
                    o = bankE[1][0:NT, u * EX:(u + 1) * EX]
                    for c in range(KC):
                        pe.matmul(o, xT[:, g.par, c, u, :], wr[:, c, :], start=(c == 0), stop=False)
                    mm = pe.matmul(o, ones[0:1, 0:NT], br_row[0:1, :], start=False, stop=True)
                mm.then_inc(route_done, 1)

            def turn_gate(f):
                pe.wait_ge(gate_ready, f.n + 1)
                for u in range(2):
                    mm = pe.transpose(bankC[0:EX, u * NT:(u + 1) * NT], gate[0:NT, f.par, u, :], ident[0:NT, 0:NT])
                mm.then_inc(gateT_done, 1)

            def out_bias(f):
                pe.wait_ge(gateT_kept, f.n + 1)
                if not f.begins(1):
                    pe.wait_ge(y_added, f.n * YS)
                for u in range(2):
                    mm = pe.matmul(bankY[0:NT, u * D:(u + 1) * D], gate_t[:, u, :], bo_rows[:, :], start=True, stop=True)
                mm.then_inc(y_done, 1)

            def layer(weights, e, operand, target, between):
                for hc in range(KC):
                    for c in range(KC):
                        mm = pe.matmul(target[:, hc * 2 * NT:(hc + 1) * 2 * NT],
                                       weights[:, e * KC + c, hc * P:(hc + 1) * P], operand(c),
                                       start=(c == 0), stop=(c == KC - 1))
                        if hc * KC + c < KC * KC - 1:
                            between()
                return mm

            def layer1(f, e, between):
                if e or not f.begins(1):
                    pe.wait_ge(h1_kept, f.n * EX + e)
                if e == 0:
                    pe.wait_ge(xT_ready, f.n + 1)
                layer(w1, e, lambda c: xT[:, f.par, c, :, :].rearrange("p u n -> p (u n)"), bankH1, between).then_inc(h1_done, 1)

            def layer2(f, e, between):
                pe.wait_ge(h1_kept, f.n * EX + e + 1)
                if e or not f.begins(1):
                    pe.wait_ge(h2_kept, f.n * EX + e)
                layer(w2, e, lambda c: h1[:, c, :, :].rearrange("p u n -> p (u n)"), bankH2, between).then_inc(h2_done, 1)

            def layer3(f, e, between):
                pe.wait_ge(h2_kept, f.n * EX + e + 1)
                pe.wait_ge(y_added, f.n * YS + e + 1)
                for u in range(2):
                    for c in range(KC):
                        mm = pe.matmul(bankY[0:NT, u * D:(u + 1) * D], h2[:, c, u, :], wo[:, e * KC + c, :],
                                       start=(c == 0), stop=(c == KC - 1))
                        if u * KC + c < 2 * KC - 1:
                            between()
                mm.then_inc(y_done, 1)

            def nothing():
                pass

            def body(f, g, a):
                for s in range(EX):
                    small = to_nodes(a) if a is not None and s == 5 else to_edges(a) if a is not None and s == 7 else iter(())

                    def between():
                        for _ in range(SMALL_RUN):
                            next(small, None)

                    if f is not None:
                        if s == 2:
                            out_bias(f)
                        layer1(f, s, nothing)
                        if s == 0:
                            turn_gate(f)
                    if a is not None:
                        if s == 1:
                            turn_logits(a)
                        if s == 4:
                            turn_back(a)
                    if g is not None:
                        if s == 5:
                            turn_x1(g)
                        if s == 6:
                            route(g)
                    if f is not None:
                        if s >= 1 or not f.begins(1):
                            layer2(*before(f, s, 1), between)
                        if s >= 2 or not f.begins(1):
                            layer3(*before(f, s, 2), between)
                    for _ in small:
                        pass
                    if g is not None and s in (1, 2):
                        aggregate(g, s - 1)

            def path():
                with pe.Fori(0, TILES) as j:
                    pe.wait_ge(tile_go, j + 1)
                    pe.sem_inc(passed, 1)
                    with pe.Fori(0, CH) as i:
                        pe.wait_ge(max_rows, i * 16 + 16)
                        for h in range(H):
                            mm = pe.matmul(bankA[0:NT, h * P:(h + 1) * P], gp_rows[:, D + h:D + h + 1].broadcast_to([P, NT]),
                                           ident[:, :], start=True, stop=True)
                        mm.then_inc(max_spread, 1)
                    with pe.Fori(0, CH) as i:
                        pe.wait_ge(sum_masks, j * CH + i + 1)
                        pe.matmul(bankB[:, 0:2 * H], gp_onehot_t[0:NT, :], gp_edm[0:NT, :], start=True, stop=True).then_inc(sum_edge, 1)
                        pe.wait_ge(sum_msg, j * CH + i + 1)
                        pe.matmul(bankE[0][0:NT, 0:ROW], gp_onehot[:, :], gp_rows[:, :], start=True, stop=True).then_inc(sum_agg, 1)

            general(pe, path)

            pe.wait_ge(weights_in, 16 * 3)
            over_stages(pe, NP, body)
            last = Pair(0, NP - 1)
            layer2(last, EX - 1, nothing)
            layer3(last, EX - 2, nothing)
            layer3(last, EX - 1, nothing)

        @block.scalar
        def _(act):
            act.dma_start(wr[:], Wr.rearrange("(c k) e -> k c e", k=P)).then_inc(small_in, 16)
            act.dma_start(br_row[:], br.rearrange("(a e) -> a e", a=1)).then_inc(small_in, 16)
            act.dma_start(bo_rows[:], bo).then_inc(small_in, 16)
            for l, params in enumerate(((b1, g1, be1, m1, v1), (b2, g2, be2, m2, v2))):
                for i, prm in enumerate(params):
                    act.dma_start(bn_rows[16 * i:16 * i + 16, l, :], prm.rearrange("e (c k) -> (e c) k", k=P)).then_inc(small_in, 16)
            for buf, dram in ((w1, W1), (w2, W2), (wo, Wo)):
                act.dma_start(buf[:], dram.rearrange("e (c k) n -> k (e c) n", k=P)).then_inc(weights_in, 16)

            act.wait_ge(consts, 3)

            def root(g):
                act.wait_ge(t_var, g.n + 1)
                act.activation(std[0:NT, :], mv[0:NT, :, 1], ACT.Sqrt, bias=eps_ln[0:NT, :]).then_inc(t_std, 1)

            def keep_xT(g):
                act.wait_ge(t_turned, g.n + 1)
                if not g.begins(2):
                    act.wait_ge(t_ft, g.n * 2 - 2)
                act.activation(xT[:, g.par, :, :, :].rearrange("p c u n -> p u c n"),
                               bankA[:, 0:2 * KC * NT].rearrange("p (u c n) -> p u c n", u=2, c=KC),
                               ACT.Copy).then_inc(t_xT, 1)

            def keep_rows(g):
                act.wait_ge(t_ft, g.n * 2 + 2)
                if not g.begins(2):
                    act.wait_ge(t_stored[g.par], g.half * 16)
                for u in range(2):
                    act.activation(ft_rows[0:NT, g.par, u, :], bankE[u][0:NT, 0:ROW], ACT.Copy).then_inc(act_step, 1)
                    act.activation(edst[0:NT, bass.ds(g.n * 2 + u, 1), :].rearrange("p a h -> p (a h)"),
                                   bankE[u][0:NT, ROW:ROWX], ACT.Copy).then_inc(t_rows, 1)
                act.wait_ge(act_step, g.n * 2 + 2)
                act.wait_ge(t_rows, g.n * 2 + 2)
                act.dma_start(table_pairs[g.n], ft_rows[0:NT, g.par, :, :]).then_inc(t_stored[g.par], 16)

            root(Pair(0, 0))
            root(Pair(0, 1))
            keep_xT(Pair(0, 0))

            def turn(g):
                root(g)
                keep_xT(g + -1)
                keep_rows(g + -2)

            over_pairs(act, 2, NP, turn, peel=2)
            keep_xT(Pair(0, NP - 1))
            keep_rows(Pair(0, NP - 2))
            keep_rows(Pair(0, NP - 1))
            act.wait_ge(bn_sum, 1)
            act.activation(bn_cols[:, :, 4, :], bn_cols[:, :, 4, :], ACT.Sqrt).then_inc(bn_root, 1)

            def keep_esrc(g):
                act.wait_ge(rows_in[g.par], (g.half + 1) * PER_ROWS)
                act.activation(esrc[:].rearrange("p u (t h) -> p (u t) h", h=H),
                               gath[:, g.par, :, :, D:ROW].rearrange("p u t h -> p (u t) h"), ACT.Copy).then_inc(esrc_kept, 1)

            def keep_turned(g):
                act.wait_ge(turn_done, g.n + 1)
                act.activation(turned[:].rearrange("r u k e -> r (u k e)"), bankA[0:TH, 0:4 * P], ACT.Copy).then_inc(turn_kept, 1)

            def keep_onehot(g, u):
                act.wait_ge(onehot_ready, g.n * 2 + 2)
                if not g.begins(1):
                    act.wait_ge(agg_done, g.n * 2)
                act.activation(onehot[:, u, :, :], onehot_b[:, u, :, :], ACT.Copy).then_inc(onehot_kept, 1)

            def exp_logits(g):
                act.wait_ge(logit_ready, g.n + 1)
                act.activation(gath[:, g.par, :, :, D:ROW].rearrange("p u t h -> p (u t) h"), lz[:, :, :], ACT.Exp).then_inc(ex_ready, 1)

            def root1(g, u):
                act.wait_ge(var_ready, g.n * 2 + u + 1)
                act.activation(std[0:NT, u:u + 1], mv[0:NT, u, 1:2], ACT.Sqrt, bias=eps_ln[0:NT, :]).then_inc(std_ready, 1)

            def keep_x1T(g):
                act.wait_ge(xT_done, g.n + 1)
                act.activation(xT[:, g.par, :, :, :].rearrange("p c u n -> p (c u n)"), bankA[:, 0:2 * KC * NT], ACT.Copy).then_inc(xT_ready, 1)

            def exp_route(f):
                act.wait_ge(rsub_ready, f.n + 1)
                act.activation(rexp[0:NT, :, :], rsub[0:NT, :, :], ACT.Exp).then_inc(rexp_ready, 1)

            def keep_gate(f):
                act.wait_ge(gateT_done, f.n + 1)
                act.activation(gate_t[:].rearrange("e u n -> e (u n)"), bankC[0:EX, 0:2 * NT], ACT.Copy).then_inc(gateT_kept, 1)

            def relu(f, e, l, done, target, source):
                act.wait_ge(done, f.n * EX + e + 1)
                kept = h1_kept if l == 0 else h2_kept
                for hc in range(KC):
                    ins = act.activation(target[:, hc, :, :].rearrange("p u n -> p (u n)"),
                                         source[:, hc * 2 * NT:(hc + 1) * 2 * NT], ACT.Relu,
                                         bias=bn_shift[:, l, e * KC + hc:e * KC + hc + 1],
                                         scale=bn_scale[:, l, e * KC + hc:e * KC + hc + 1])
                ins.then_inc(kept, 1)

            def relu1(f, e):
                if e or not f.begins(1):
                    act.wait_ge(h2_done, f.n * EX + e)
                relu(f, e, 0, h1_done, h1, bankH1)

            def relu2(f, e):
                if e or not f.begins(1):
                    act.wait_ge(y_done, f.n * YS + e + (1 if e else 0))
                relu(f, e, 1, h2_done, h2, bankH2)

            def body(f, g, a):
                for s in range(EX):
                    if g is not None and s == 3:
                        root1(g, 0)
                    if f is not None:
                        relu1(f, s)
                        if s == 0:
                            keep_gate(f)
                    if g is not None:
                        if s == 0:
                            exp_logits(g)
                        if s == 4:
                            root1(g, 1)
                        if s == 5:
                            keep_x1T(g)
                        if s == 7:
                            exp_route(g)
                    if a is not None and s == 1:
                        keep_turned(a)
                    if f is not None and (s >= 1 or not f.begins(1)):
                        relu2(*before(f, s, 1))
                    if a is not None:
                        if s == 0:
                            keep_esrc(a)
                        if s in (6, 7):
                            keep_onehot(a, s - 6)

            def path():
                with act.Fori(0, TILES) as j:
                    with act.Fori(0, CH) as i:
                        act.wait_ge(sum_logit, j * CH + i + 1)
                        act.activation(gp_rows[:, D:ROW], gp_l, ACT.Exp).then_inc(sum_ex, 1)

            general(act, path)
            act.wait_ge(bn_ready, 1)
            over_stages(act, NP, body)
            relu2(Pair(0, NP - 1), EX - 1)

        @block.vector
        def _(dve):
            own = Chain(dve, dve_step)
            dve.wait_ge(consts, 9)
            own.did(dve.tensor_copy(iota[:], iota_i[:]))
            own.did(dve.tensor_copy(base[:], base_i[:]))
            own.did(dve.tensor_copy(node[:], node_i[:]))
            own.did(dve.tensor_copy(bound[:], bound_i[:]))
            own.did(dve.memset(change[:], 1.0))
            dve.wait_ge(attn_in, 48)
            for c in range(KC):
                for k in range(2):
                    own.did(dve.tensor_tensor(att_prod, wx[:, c, 0:D], att[:, k, :], ALU.mult))
                    own.settle()
                    ins = dve.tensor_reduce(wx[:, c, D + k * H:D + (k + 1) * H],
                                            att_prod.rearrange("p (h c) -> p h c", h=H), AX.X, ALU.add)
                    if c == KC - 1 and k == 1:
                        ins.then_inc(wx_ready, 1)
                    else:
                        own.did(ins)
                        own.settle()
            dve.wait_ge(p_in, 32)
            dve.tensor_copy(first_dst[0:NT, :], dst_all[0:NT, 0:1].broadcast_to([NT, J])).then_inc(p_first, 1)
            fixed = own.count

            def norm(g):
                own.start(fixed + g.n * 2)
                dve.wait_ge(t_x[g.par], (g.half + 1) * 16)
                for u in range(2):
                    ins = dve.bn_stats(stats[0:NT, u, :], xin[0:NT, g.par, u, :])
                own.did(ins)
                own.settle(alone=passed)
                for u in range(2):
                    ins = dve.bn_aggr(mv[0:NT, u, :], stats[0:NT, u, :])
                ins.then_inc(t_var, 1)
                dve.wait_ge(t_std, g.n + 1)
                own.did(dve.reciprocal(rstd[0:NT, :], std[0:NT, :]))
                own.settle()
                if not g.begins(2):
                    dve.wait_ge(t_turned, g.n - 1)
                for u in range(2):
                    dve.tensor_scalar(xnt[0:NT, g.par, u, :], xin[0:NT, g.par, u, :], mv[0:NT, u, 0:1],
                                      rstd[0:NT, u:u + 1], ALU.subtract, ALU.mult).then_inc(t_norm, 1)

            norm(Pair(0, 0))
            norm(Pair(0, 1))

            own.start(fixed + 4)
            dve.wait_ge(p_coarse, 1)
            own.did(dve.tensor_scalar(scr[0:J, 0:NT], bankH1[0:J, 0:NT], bound[0:J, :], None, ALU.is_lt, ALU.add,
                                      accum_out=coarse[0:J, :]))
            own.settle()
            own.did(dve.tensor_scalar(blkf[0:J, :], coarse[0:J, :], -1.0, 0.0, ALU.add, ALU.max))
            own.settle()
            dve.tensor_copy(blk_i[0:J, :], blkf[0:J, :]).then_inc(p_block, 1)
            fixed += own.count

            over_pairs(dve, 2, NP, norm)

            own.start(fixed + 2 * NP)
            dve.wait_ge(p_fetched, 16)
            own.did(dve.tensor_scalar(scr[0:J, :], blk[0:J, :], bound[0:J, :], None, ALU.is_lt))
            own.settle()
            own.did(dve.tensor_reduce(fine[0:J, :], scr[0:J, :], AX.X, ALU.add))
            own.did(dve.tensor_tensor(scr2[0:NT, :], dst_prev[0:NT, :], dst_all[0:NT, :], ALU.is_gt))
            own.settle()
            own.did(dve.scalar_tensor_tensor(startf[0:J, :], blkf[0:J, :], float(EB), fine[0:J, :], ALU.mult, ALU.add))
            own.did(dve.tensor_reduce(bad1[0:NT, :], scr2[0:NT, :], AX.X, ALU.max))
            own.settle()
            dve.nop().then_inc(p_row, 1)

            dve.wait_ge(bn_turned, 1)
            own.did(dve.tensor_copy(bn_cols[:].rearrange("p l k c -> p (l k c)"), bankC[:, 0:2 * 5 * EX * KC]))
            own.settle()
            dve.tensor_scalar(bn_cols[:, :, 4, :], bn_cols[:, :, 4, :], BN_EPS, None, ALU.add).then_inc(bn_sum, 1)
            dve.wait_ge(p_flag, 1)
            own.did(dve.tensor_copy(plan_f[:, 0:J], bankH2[0:1, 0:J]))
            own.did(dve.tensor_copy(plan_f[:, P:P + 1], bankH2[0:1, P:P + 1]))
            own.settle()
            own.did(dve.tensor_tensor(plan_f[:, 2 * P:2 * P + TILES], plan_f[:, 1:J], plan_f[:, 0:TILES], ALU.subtract))
            own.settle()
            own.did(dve.tensor_scalar(plan_f[:, 2 * P:2 * P + TILES], plan_f[:, 2 * P:2 * P + TILES], float(WIN), None,
                                      ALU.is_gt))
            own.settle()
            own.did(dve.tensor_reduce(plan_f[:, 3 * P:3 * P + 1], plan_f[:, 2 * P:2 * P + TILES], AX.X, ALU.add))
            own.settle()
            own.did(dve.tensor_tensor(plan_f[:, P:P + 1], plan_f[:, P:P + 1], plan_f[:, 3 * P:3 * P + 1], ALU.add))
            own.settle()
            own.did(dve.tensor_copy(plan_i[:, 0:J], plan_f[:, 0:J]))
            own.did(dve.tensor_copy(plan_i[:, P:P + 1], plan_f[:, P:P + 1]))
            own.settle()
            dve.nop().then_inc(p_ready, 1)

            dve.wait_ge(bn_root, 1)
            own.did(dve.reciprocal(bn_cols[:, :, 4, :], bn_cols[:, :, 4, :]))
            own.did(dve.tensor_tensor(bn_shift[:], bn_cols[:, :, 0, :], bn_cols[:, :, 3, :], ALU.subtract))
            own.settle()
            own.did(dve.tensor_tensor(bn_scale[:], bn_cols[:, :, 1, :], bn_cols[:, :, 4, :], ALU.mult))
            own.settle()
            own.did(dve.tensor_tensor(bn_shift[:], bn_shift[:], bn_scale[:], ALU.mult))
            own.settle()
            own.did(dve.tensor_tensor(bn_shift[:], bn_shift[:], bn_cols[:, :, 2, :], ALU.add))
            own.settle()
            dve.nop().then_inc(bn_ready, 1)

            def path():
                mine = Chain(dve, gp_dve)
                dve.sem_inc(max_free, 1)
                dve.sem_inc(sum_free, 1)
                with dve.Fori(0, TILES) as j:
                    dve.wait_ge(tile_go, j + 1)
                    tile_base = j * (CH * (MAX_STEPS + SUM_STEPS) + TILE_STEPS)
                    here = node[0:NT, bass.ds(j, 1)]
                    ed = edst[0:NT, bass.ds(j, 1), :].rearrange("n a h -> n (a h)")
                    mine.start(tile_base)
                    mine.did(dve.memset(gp_nmax[0:NT], -BIG))
                    mine.settle(alone=passed)
                    with dve.Fori(0, CH) as i:
                        mine.start(tile_base + i * MAX_STEPS + 1)
                        dve.wait_ge(max_in, i * 32 + 32)
                        mine.did(dve.tensor_scalar(gp_away[0:NT], gp_dst_row[0:NT], here, -BIG, ALU.not_equal, ALU.mult))
                        dve.wait_ge(max_spread, j * CH + i + 1)
                        mine.settle()
                        mine.did(dve.tensor_tensor(gp_val[0:NT], bankA[0:NT, 0:H * P].rearrange("n (h e) -> n h e", h=H),
                                                   gp_away[0:NT].unsqueeze(1).broadcast_to([NT, H, P]), ALU.add))
                        mine.settle()
                        mine.did(dve.tensor_reduce(gp_cmax[0:NT], gp_val[0:NT], AX.X, ALU.max))
                        mine.settle()
                        dve.tensor_tensor(gp_nmax[0:NT], gp_nmax[0:NT], gp_cmax[0:NT], ALU.max).then_inc(max_free, 1)
                        dve.wait_ge(max_free, j * CH + i + 2)
                    mine.start(tile_base + CH * MAX_STEPS + 1)
                    mine.did(dve.tensor_tensor(gp_zmax[0:NT], gp_nmax[0:NT], ed, ALU.add))
                    dve.tensor_copy(gp_edm[0:NT, 0:H], ed)
                    dve.memset(gp_acc[0:NT], 0.0)
                    mine.settle()
                    mine.did(dve.scalar_tensor_tensor(gp_edm[0:NT, H:2 * H], gp_zmax[0:NT], SLOPE, gp_zmax[0:NT], ALU.mult, ALU.max))
                    mine.settle(alone=passed)
                    with dve.Fori(0, CH) as i:
                        mine.start(tile_base + CH * MAX_STEPS + 3 + i * SUM_STEPS)
                        dve.wait_ge(sum_in, i * 64 + 64)
                        mine.did(dve.tensor_scalar(gp_rel[:], gp_dst[:], base[:, bass.ds(j, 1)], None, ALU.subtract))
                        mine.settle()
                        dve.tensor_scalar(gp_onehot[:], iota[:], gp_rel[:], None, ALU.is_equal)
                        dve.tensor_scalar(gp_onehot_t[0:NT], gp_dst_row[0:NT], here, None, ALU.is_equal).then_inc(sum_masks, 1)
                        dve.wait_ge(sum_edge, j * CH + i + 1)
                        dve.wait_ge(sum_rows, i * 16 + 16)
                        mine.did(dve.tensor_tensor(gp_z, gp_rows[:, D:ROW], bankB[:, 0:H], ALU.add))
                        mine.settle()
                        mine.did(dve.scalar_tensor_tensor(gp_l, gp_z, SLOPE, gp_z, ALU.mult, ALU.max))
                        mine.settle()
                        mine.did(dve.tensor_tensor(gp_l, gp_l, bankB[:, H:2 * H], ALU.subtract))
                        mine.settle()
                        dve.tensor_scalar(gp_l, gp_l, 0.0, None, ALU.min).then_inc(sum_logit, 1)
                        dve.wait_ge(sum_ex, j * CH + i + 1)
                        mine.did(dve.tensor_scalar(gp_w, gp_rows[:, D:ROW], gp_dist[:], None, ALU.mult))
                        mine.settle()
                        rows = gp_rows[:, 0:D].rearrange("e (h c) -> e h c", h=H)
                        dve.tensor_tensor(rows, rows, gp_w.unsqueeze(2).broadcast_to([P, H, DH]), ALU.mult).then_inc(sum_msg, 1)
                        dve.wait_ge(sum_agg, j * CH + i + 1)
                        dve.tensor_tensor(gp_acc[0:NT], gp_acc[0:NT], bankE[0][0:NT, 0:ROW], ALU.add).then_inc(sum_free, 1)
                        dve.wait_ge(sum_free, j * CH + i + 2)
                    mine.start(tile_base + CH * (MAX_STEPS + SUM_STEPS) + 3)
                    mine.did(dve.tensor_scalar(gp_den[0:NT], gp_acc[0:NT, D:ROW], TINY, None, ALU.max))
                    mine.settle()
                    mine.did(dve.reciprocal(gp_den[0:NT], gp_den[0:NT]))
                    mine.settle()
                    dve.wait_ge(res_free, j + 1)
                    dve.memset(gp_res[0:NT, D:ROW], 0.0)
                    dve.tensor_tensor(gp_res[0:NT, 0:D].rearrange("n (h c) -> n h c", h=H),
                                      gp_acc[0:NT, 0:D].rearrange("n (h c) -> n h c", h=H),
                                      gp_den[0:NT].unsqueeze(2).broadcast_to([NT, H, DH]), ALU.mult).then_inc(res_ready, 1)
                    dve.wait_ge(res_ready, j + 1)
                dve.tensor_copy(plan_i[:, 0:TILES], base_i[0:1, :]).then_inc(gp_plan, 1)

            general(dve, path)

            def shift_dst(g):
                dve.wait_ge(win_in[g.par], (g.half + 1) * PER_WIN)
                for u in range(2):
                    ins = dve.tensor_scalar(rel[:, u, :, :], dst_win[:, g.par, u, :].unsqueeze(2).broadcast_to([P, TE, H]),
                                            base[:, bass.ds(g.n * 2 + u, 1)], None,
                                            ALU.subtract)
                ins.then_inc(rel_ready, 1)

            def segments(g):
                dve.wait_ge(turn_kept, g.n + 1)
                own.did(dve.tensor_tensor(change[:, :, 1:P], turned[:, :, 1, 1:P], turned[:, :, 1, 0:P - 1], ALU.not_equal))
                own.settle()
                own.did(dve.tensor_scalar(reset[:], change[:, :, 0:P], -BIG, None, ALU.mult))
                own.settle()
                for u in range(2):
                    ins = dve.tensor_tensor_scan(scan[:, u, :], reset[:, u, :], turned[:, u, 0, :], -BIG, ALU.add, ALU.max)
                own.did(ins)
                own.settle()
                dve.tensor_tensor(scan_end[:], scan[:], change[:, :, 1:P + 1], ALU.mult).then_inc(seg_done, 1)

            def in_parts(whole, rest, parts, done):
                own.did(dve.tensor_copy(parts[0], whole))
                own.settle()
                own.did(dve.tensor_tensor(rest, whole, parts[0], ALU.subtract))
                own.settle()
                own.did(dve.tensor_copy(parts[1], rest))
                own.settle()
                dve.tensor_tensor(parts[2], rest, parts[1], ALU.subtract).then_inc(done, 1)

            def split_maxima(g):
                dve.wait_ge(back_done, g.n + 1)
                back = bankB[:, 0:4 * TH].rearrange("p (u k t h) -> p u k t h", u=2, k=2, h=H)
                dve.tensor_copy(ends[:, :, :, PARTS * H], back[:, :, 1, :, 0])
                in_parts(back[:, :, 0, :, :], ends_rest[:], [ends[:, :, :, i * H:(i + 1) * H] for i in range(PARTS)], ends_ready)

            def make_onehot(g, u):
                dve.wait_ge(rel_ready, g.n + 1)
                if not g.begins(1):
                    dve.wait_ge(onehot_kept, g.n * 2)
                dve.tensor_tensor(onehot_b[:, u, :, :], iota[:].unsqueeze(1).broadcast_to([P, TE, NT]),
                                  rel[:, u, :, 0:1].broadcast_to([P, TE, NT]), ALU.is_equal).then_inc(onehot_ready, 1)

            def make_onehot_t(g, u):
                dve.wait_ge(dst_row_in, g.n * 32 + u * 16 + 16)
                dve.tensor_scalar(onehot_t[0:NT, u, :], dst_row[0:NT, :], node[0:NT, bass.ds(g.n * 2 + u, 1)], None,
                                  ALU.is_equal).then_inc(onehotT_ready, 1)

            def node_maxima(g):
                dve.wait_ge(nodes_done, g.n + 1)
                cols = bankC[0:NT, 0:2 * TE * NCOL].rearrange("n (c k) -> n c k", k=NCOL)
                flat = nval[0:NT].rearrange("n u (t h) -> n (u t) h", h=H)
                own.did(dve.tensor_scalar(nmask[0:NT], cols[:, :, PARTS * H:NCOL], -1.0, BIG, ALU.add, ALU.mult))
                own.settle()
                own.did(dve.tensor_tensor(flat, cols[:, :, 2 * H:3 * H], nmask[0:NT].broadcast_to([NT, 2 * TE, H]), ALU.add))
                for part in (1, 0):
                    own.settle()
                    own.did(dve.tensor_tensor(flat, cols[:, :, part * H:(part + 1) * H], flat, ALU.add))
                own.settle()
                own.did(dve.tensor_reduce(nmax[0:NT], nval[0:NT].rearrange("n u (t h) -> n u h t", h=H), AX.X, ALU.max))
                own.settle()
                pair_dst = edst[0:NT, bass.ds(g.n * 2, 2), :]
                own.did(dve.tensor_tensor(zmax[0:NT], pair_dst, nmax[0:NT], ALU.add))
                dve.tensor_copy(edm[0:NT, :, 0:H], pair_dst)
                own.settle()
                own.did(dve.scalar_tensor_tensor(edm[0:NT, :, H:2 * H], zmax[0:NT], SLOPE, zmax[0:NT], ALU.mult, ALU.max))
                own.settle()
                in_parts(edm[0:NT], edm_rest[0:NT], [edm_parts[0:NT, i] for i in range(PARTS)], edm_ready)

            def logits(g):
                dve.wait_ge(edge_done, g.n + 1)
                cols = bankB[:, 0:2 * TE * 2 * H].rearrange("p (c k h) -> p c k h", k=2, h=H)
                own.did(dve.tensor_tensor(z[:], esrc[:].rearrange("p u (t h) -> p (u t) h", h=H),
                                          cols[:, :, 0, :], ALU.add))
                own.settle()
                own.did(dve.scalar_tensor_tensor(lz[:], z[:], SLOPE, z[:], ALU.mult, ALU.max))
                own.settle()
                own.did(dve.tensor_tensor(lz[:], lz[:], cols[:, :, 1, :], ALU.subtract))
                own.settle()
                dve.tensor_scalar(lz[:], lz[:], 0.0, None, ALU.min).then_inc(logit_ready, 1)

            def weigh(g):
                dve.wait_ge(ex_ready, g.n + 1)
                own.did(dve.tensor_tensor(wgt[:], gath[:, g.par, :, :, D:ROW].rearrange("p u t h -> p (u t) h"),
                                          dist_win[:, g.par, :, :].rearrange("p u t -> p (u t)").unsqueeze(2).broadcast_to([P, 2 * TE, H]), ALU.mult))
                own.settle()

            def messages(g, u, part):
                half = TE // 2
                cols = slice(part * half, (part + 1) * half)
                rows = gath[:, g.par, u, cols, 0:D].rearrange("p t (h c) -> p t h c", h=H)
                ins = dve.tensor_tensor(rows, rows, wgt[:, u * TE + part * half:u * TE + (part + 1) * half, :].unsqueeze(3
                                                        ).broadcast_to([P, half, H, DH]), ALU.mult)
                if part == 1:
                    ins.then_inc(msg_ready, 1)

            def residual(g, u):
                dve.wait_ge(agg_done, g.n * 2 + u + 1)
                dve.wait_ge(x_in[g.par], (g.half + 1) * 16)
                own.did(dve.tensor_scalar(rden[0:NT, u, :], bankE[u][0:NT, D:ROW], TINY, None, ALU.max))
                own.settle()
                own.did(dve.reciprocal(rden[0:NT, u, :], rden[0:NT, u, :]))
                own.settle()
                if not g.begins(2):
                    dve.wait_ge(out_stored[g.par], g.half * 16)
                own.did(dve.tensor_tensor(x1[0:NT, g.par, u, :].rearrange("n (h c) -> n h c", h=H),
                                          bankE[u][0:NT, 0:D].rearrange("n (h c) -> n h c", h=H),
                                          rden[0:NT, u, :].unsqueeze(2).broadcast_to([NT, H, DH]), ALU.mult))
                own.settle()
                own.did(dve.tensor_tensor(x1[0:NT, g.par, u, :], x1[0:NT, g.par, u, :], x_res[0:NT, g.par, u, :], ALU.add))
                own.settle()
                own.did(dve.bn_stats(stats[0:NT, u, :], x1[0:NT, g.par, u, :]))
                own.settle(alone=passed)
                dve.bn_aggr(mv[0:NT, u, :], stats[0:NT, u, :]).then_inc(var_ready, 1)

            def norm1(g, u):
                dve.wait_ge(std_ready, g.n * 2 + u + 1)
                own.did(dve.reciprocal(rstd[0:NT, u:u + 1], std[0:NT, u:u + 1]))
                own.settle()
                dve.tensor_scalar(xn[0:NT, u, :], x1[0:NT, g.par, u, :], mv[0:NT, u, 0:1], rstd[0:NT, u:u + 1],
                                  ALU.subtract, ALU.mult).then_inc(xn_ready, 1)

            def gates(f):
                dve.wait_ge(route_done, f.n + 1)
                r = bankE[1][0:NT, 0:2 * EX].rearrange("n (u e) -> n u e", u=2)
                own.did(dve.tensor_reduce(rmax[0:NT, :], r, AX.X, ALU.max))
                own.settle()
                dve.tensor_tensor(rsub[0:NT], r, rmax[0:NT, :].unsqueeze(2).broadcast_to([NT, 2, EX]), ALU.subtract
                                  ).then_inc(rsub_ready, 1)
                dve.wait_ge(rexp_ready, f.n + 1)
                own.did(dve.tensor_reduce(rsum[0:NT, :], rexp[0:NT], AX.X, ALU.add))
                own.settle()
                own.did(dve.reciprocal(rinv[0:NT, :], rsum[0:NT, :]))
                own.settle()
                dve.tensor_tensor(gate[0:NT, f.par], rexp[0:NT], rinv[0:NT, :].unsqueeze(2).broadcast_to([NT, 2, EX]), ALU.mult
                                  ).then_inc(gate_ready, 1)

            def add_y(f, k):
                dve.wait_ge(y_done, f.n * YS + k + 1)
                if k:
                    dve.wait_ge(y_added, f.n * YS + k)
                acc = x1[0:NT, f.par, :, :]
                if k == 0:
                    dve.wait_ge(gate_ready, f.n + 1)
                    dve.tensor_tensor(acc.rearrange("n u c -> n (u c)"), bankY[0:NT, :], acc.rearrange("n u c -> n (u c)"),
                                      ALU.add).then_inc(y_added, 1)
                    return
                for u in range(2):
                    ins = dve.scalar_tensor_tensor(acc[:, u, :], bankY[0:NT, u * D:(u + 1) * D], gate[0:NT, f.par, u, k - 1:k],
                                                   acc[:, u, :], ALU.mult, ALU.add)
                ins.then_inc(y_added, 1)

            setup_steps = own.base + own.count

            def body(f, g, a):
                if f is not None:
                    own.start(setup_steps + MAXIMA_STEPS + (f.n + 1) * (MAXIMA_STEPS + SUMS_STEPS))
                else:
                    own.start(setup_steps + (MAXIMA_STEPS if g is not None else 0))
                for s in range(EX):
                    if g is not None:
                        if s == 0:
                            logits(g)
                    if a is not None and s == 0:
                        shift_dst(a)
                    if g is not None:
                        if s == 0:
                            weigh(g)
                            messages(g, 0, 0)
                        if s == 1:
                            messages(g, 0, 1)
                            messages(g, 1, 0)
                        if s == 2:
                            messages(g, 1, 1)
                    if a is not None and s == 2:
                        make_onehot(a, 0)
                    if f is not None and s == 2:
                        add_y(f, 0)
                    if a is not None and s == 2:
                        make_onehot(a, 1)
                    if g is not None and s in (3, 4):
                        residual(g, s - 3)
                    if a is not None:
                        if s == 3:
                            segments(a)
                        if s == 4:
                            split_maxima(a)
                    if g is not None and s in (3, 4):
                        norm1(g, s - 3)
                    if a is not None:
                        if s in (3, 5):
                            make_onehot_t(a, s // 4)
                        if s == 6:
                            node_maxima(a)
                    if g is not None and s == 7:
                        gates(g)
                    if f is not None and (s >= 2 or not f.begins(1)):
                        pair, expert = before(f, s, 2)
                        add_y(pair, expert + 1)
                assert own.count == MAXIMA_STEPS * (a is not None) + SUMS_STEPS * (g is not None), own.count

            over_stages(dve, NP, body)
            add_y(Pair(0, NP - 1), EX - 1)
            add_y(Pair(0, NP - 1), EX)


INS = ["x", "src", "dst", "edge_attr3_1x1", "L0_gnn_W", "L0_gnn_w_att_src", "L0_gnn_w_att_dst", "L0_ffn_Wr", "L0_ffn_br",
       "L0_ffn_W1", "L0_ffn_b1", "L0_ffn_g1", "L0_ffn_be1", "L0_ffn_m1", "L0_ffn_v1", "L0_ffn_W2", "L0_ffn_b2",
       "L0_ffn_g2", "L0_ffn_be2", "L0_ffn_m2", "L0_ffn_v2", "L0_ffn_Wo", "L0_ffn_bo"]


def kernel(**inputs):
    import numpy as np
    import concourse.bacc as bacc
    from concourse.bass_utils import run_bass_kernel_spmd

    nc = bacc.Bacc("TRN2", target_bir_lowering=False, num_devices=1)
    arrays, args = {}, []
    for name in INS:
        a = np.ascontiguousarray(inputs[name])
        arrays[f"in_{name}"] = a
        args.append(nc.dram_tensor(f"in_{name}", a.shape, mybir.dt.from_np(a.dtype), kind="ExternalInput").ap())
    out = nc.dram_tensor("out", arrays["in_x"].shape, F32, kind="ExternalOutput").ap()
    gnn_ffn_kernel(nc, *args, out)
    return run_bass_kernel_spmd(nc, [arrays], core_ids=[0]).results[0]["out"]
```

```python
from contextlib import ExitStack

import concourse.bass as bass
from concourse import mybir

ALU = mybir.AluOpType
ACT = mybir.ActivationFunctionType
AX = mybir.AxisListType
F32 = mybir.dt.float32
I32 = mybir.dt.int32
U32 = mybir.dt.uint32
F32R = mybir.dt.float32r
BF16 = mybir.dt.bfloat16

P = 128
NT = 125
D = 256
KC = D // P
H = 4
DH = D // H
ROW = D + H
ROWX = ROW + H
TE = 18
WIN = P * TE
TH = TE * H
EX = 8
SLOPE = 0.2
LN_EPS = 1e-5
BN_EPS = 1e-3
BIG = 1e37
TINY = 1e-30
RING = 2
CHUNKS = 4
TC = TE // 2
PARTS = 3
NCOL = PARTS * H + 1
YS = EX + 1
SMALL_RUN = 6
MAXIMA_STEPS = 16
SUMS_STEPS = 16
GATE_STEPS = 3


class Pair:

    def __init__(self, k, off):
        self.k, self.off = k, off

    @property
    def n(self):
        return self.off if isinstance(self.k, int) else self.k * 2 + self.off

    @property
    def half(self):
        return self.off // 2 if isinstance(self.k, int) else self.k + self.off // 2

    @property
    def par(self):
        return self.off % 2

    def begins(self, d):
        return isinstance(self.k, int) and self.off < d

    def within(self, count):
        return not isinstance(self.k, int) or self.off < count

    def __add__(self, d):
        return Pair(self.k, self.off + d)


def over_pairs(eng, lo, hi, body, peel=0, tail=0):
    first, hi = lo, hi - tail
    for n in range(peel):
        if first < hi:
            body(Pair(0, first))
            first += 1
    turns = (hi - first) // 2
    if turns > 0:
        with eng.Fori(0, turns) as k:
            body(Pair(k, first))
            body(Pair(k, first + 1))
    for n in range(hi - (hi - first) % 2, hi + tail):
        body(Pair(0, n))


def over_stages(eng, pairs, body, tail=0):
    body(None, None, Pair(0, 0))
    body(None, Pair(0, 0), Pair(0, 1))
    over_pairs(eng, 0, pairs - 2, lambda f: body(f, f + 1, f + 2), peel=1, tail=tail)
    body(Pair(0, pairs - 2), Pair(0, pairs - 1), None)
    body(Pair(0, pairs - 1), None, None)


def before(f, s, steps):
    return (f, s - steps) if s >= steps else (f + -1, s - steps + EX)


class Chain:

    def __init__(self, eng, sem):
        self.eng, self.sem, self.base, self.count = eng, sem, 0, 0

    def start(self, base):
        self.base, self.count = base, 0

    def did(self, ins):
        ins.then_inc(self.sem, 1)
        self.count += 1

    def settle(self, alone=None):
        self.eng.wait_ge(self.sem, self.base + self.count)
        if alone is not None:
            self.eng.sem_inc(alone, 1)


def gnn_ffn_kernel(nc, x, src, dst, dist, W, att_src, att_dst, Wr, br, W1, b1, g1, be1, m1, v1, W2, b2, g2, be2,
                   m2, v2, Wo, bo, out):
    N = x.shape[0]
    E = src.shape[0]
    TILES = N // NT
    NP = TILES // 2
    EB = E // NT
    assert NP * 2 * NT == N and EB * NT == E and TILES + 1 <= P and NP >= 4
    EPAD = (-(E + WIN)) % P
    PADDED = E + WIN + EPAD

    with ExitStack() as ctx:
        def sb(name, shape, dt=F32):
            return ctx.enter_context(nc.sbuf_tensor(name, shape, dt))

        def bank(name):
            return ctx.enter_context(nc.psum_tensor(name, [P, 512], F32))

        def sem(name):
            return ctx.enter_context(nc.semaphore(name))

        table = nc.dram_tensor("table", [N, ROW], F32, kind="Internal").ap()
        src_pad = nc.dram_tensor("src_pad", [PADDED], I32, kind="Internal").ap()
        dst_pad = nc.dram_tensor("dst_pad", [PADDED + P], I32, kind="Internal").ap()
        dist_pad = nc.dram_tensor("dist_pad", [PADDED], F32, kind="Internal").ap()

        ident = sb("ident", [P, P])
        iota_i = sb("iota_i", [P, NT], I32)
        iota = sb("iota", [P, NT])
        base_i = sb("base_i", [P, TILES], I32)
        base = sb("base", [P, TILES])
        node_i = sb("node_i", [P, TILES], I32)
        node = sb("node", [P, TILES])
        ids_i = sb("ids_i", [P, TILES], I32)
        bound_i = sb("bound_i", [P, 1], I32)
        bound = sb("bound", [P, 1])
        ones = sb("ones", [P, P])
        eps_ln = sb("eps_ln", [P, 1])
        pad_fill = sb("pad_fill", [P, TE], I32)
        neg_fill = sb("neg_fill", [P, TE], I32)

        w1 = sb("w1", [P, EX * KC, D])
        w2 = sb("w2", [P, EX * KC, D])
        wo = sb("wo", [P, EX * KC, D])
        wr = sb("wr", [P, KC, EX])
        br_row = sb("br_row", [1, EX])
        bo_rows = sb("bo_rows", [EX, D])
        bn_cols = sb("bn_cols", [P, 2, 5, EX * KC])
        bn_scale = sb("bn_scale", [P, 2, EX * KC])
        bn_shift = sb("bn_shift", [P, 2, EX * KC])
        wx = sb("wx", [P, KC, ROWX])

        edst = sb("edst", [P, TILES, H])
        plan_i = sb("plan_i", [1, P + 1], I32)

        gath = sb("gath", [P, RING, 2, TE, ROW])
        onehot = sb("onehot", [P, TC, NT], F32R)
        msg_hi = sb("msg_hi", [P, TC, ROW], F32R)
        msg_lo = sb("msg_lo", [P, TC, ROW], F32R)
        onehot_b = sb("onehot_b", [P, 2, TE, NT], BF16)
        onehot_t = sb("onehot_t", [P, 2, WIN], BF16)
        dst_row = sb("dst_row", [P, WIN // 2], I32)
        src_win = sb("src_win", [P, RING, 2, TE], U32)
        dst_win = sb("dst_win", [P, RING, 2, TE], I32)
        dist_win = sb("dist_win", [P, RING, 2, TE])
        x_res = sb("x_res", [P, RING, 2, D])
        rel = sb("rel", [P, 2, TE, H])
        esrc = sb("esrc", [P, 2, TH])
        turned = sb("turned", [TH, 2, 2, P])
        change = sb("change", [TH, 2, P + 1])
        reset = sb("reset", [TH, 2, P])
        scan = sb("scan", [TH, 2, P])
        scan_end = sb("scan_end", [TH, 2, P])
        ends = sb("ends", [P, 2, TE, NCOL], BF16)
        ends_rest = sb("ends_rest", [P, 2, TE, H])
        nmask = sb("nmask", [P, 2 * TE, 1])
        nval = sb("nval", [P, 2, TH])
        nmax = sb("nmax", [P, 2, H])
        zmax = sb("zmax", [P, 2, H])
        edm = sb("edm", [P, 2, 2 * H])
        edm_rest = sb("edm_rest", [P, 2, 2 * H])
        edm_parts = sb("edm_parts", [P, PARTS, 2, 2 * H], BF16)
        z = sb("z", [P, 2 * TE, H])
        lz = sb("lz", [P, 2 * TE, H])
        wgt = sb("wgt", [P, 2 * TE, H])
        rden = sb("rden", [P, 2, H])
        stats = sb("stats", [P, 2, 6])
        mv = sb("mv", [P, 2, 2])
        std = sb("std", [P, 2])
        rstd = sb("rstd", [P, 2])
        t_mv = sb("t_mv", [P, RING, 2, 2])
        t_root = sb("t_root", [P, RING, 2])
        xn = sb("xn", [P, 2, D])
        x1 = sb("x1", [P, RING, 2, D])
        xT = sb("xT", [P, RING, KC, 2, NT])
        rsub = sb("rsub", [P, 2, EX])
        rexp = sb("rexp", [P, 2, EX])
        rmax = sb("rmax", [P, 2])
        rsum = sb("rsum", [P, 2])
        rinv = sb("rinv", [P, 2])
        gate = sb("gate", [P, RING, 2, EX])
        gate_t = sb("gate_t", [EX, 2, NT])
        h1 = sb("h1", [P, KC, 2, NT])
        h2 = sb("h2", [P, KC, 2, NT])

        bankA, bankB, bankC = bank("bankA"), bank("bankB"), bank("bankC")
        bankE = [bank("bankE0"), bank("bankE1")]
        bankH1, bankH2, bankY = bank("bankH1"), bank("bankH2"), bank("bankY")

        attn_in, small_in, pads_src = sem("attn_in"), sem("small_in"), sem("pads_src")
        weights_in = sem("weights_in")
        consts = sem("consts")
        dve_step = sem("dve_step")
        fills = sem("fills")
        wx_ready, bn_turned, bn_sum, bn_root, bn_ready = (
            sem("wx_ready"), sem("bn_turned"), sem("bn_sum"), sem("bn_root"), sem("bn_ready"))
        t_x = [sem("t_x0"), sem("t_x1")]
        t_var, t_std, t_norm, t_turned, t_xT, t_ft, t_rows = (
            sem("t_var"), sem("t_std"), sem("t_norm"), sem("t_turned"), sem("t_xT"), sem("t_ft"), sem("t_rows"))
        t_kept = sem("t_kept")
        t_stored = [sem("t_stored0"), sem("t_stored1")]
        p_all, p_in, p_first, p_coarse, p_block, p_fetched, p_row, p_flag, p_ready = (
            sem("p_all"), sem("p_in"), sem("p_first"), sem("p_coarse"), sem("p_block"), sem("p_fetched"), sem("p_row"),
            sem("p_flag"), sem("p_ready"))
        setup_done = sem("setup_done")
        passed = sem("passed")
        win_in = [sem("win_in0"), sem("win_in1")]
        x_in = [sem("x_in0"), sem("x_in1")]
        dst_row_in = sem("dst_row_in")
        rows_in = [sem("rows_in0"), sem("rows_in1")]
        esrc_kept = sem("esrc_kept")
        ends_ready, onehot_kept = sem("ends_ready"), sem("onehot_kept")
        rel_ready, turn_done, turn_kept, seg_done, back_done = (
            sem("rel_ready"), sem("turn_done"), sem("turn_kept"), sem("seg_done"), sem("back_done"))
        onehot_ready, onehotT_ready, nodes_done, edm_ready, edge_done = (
            sem("onehot_ready"), sem("onehotT_ready"), sem("nodes_done"), sem("edm_ready"), sem("edge_done"))
        logit_ready, ex_ready, msg_ready, hi_ready, lo_ready, agg_done = (
            sem("logit_ready"), sem("ex_ready"), sem("msg_ready"), sem("hi_ready"), sem("lo_ready"), sem("agg_done"))
        var_ready, std_ready, xn_ready, xT_done, xT_ready = (
            sem("var_ready"), sem("std_ready"), sem("xn_ready"), sem("xT_done"), sem("xT_ready"))
        route_done, rsub_ready, rexp_ready, gate_ready, gateT_done, gateT_kept = (
            sem("route_done"), sem("rsub_ready"), sem("rexp_ready"), sem("gate_ready"), sem("gateT_done"),
            sem("gateT_kept"))
        h1_done, h1_kept, h2_done, h2_kept, y_done, y_added = (
            sem("h1_done"), sem("h1_kept"), sem("h2_done"), sem("h2_kept"), sem("y_done"), sem("y_added"))
        out_stored = [sem("out_stored0"), sem("out_stored1")]

        table2 = nc.dram_tensor("table2", [N, ROW], F32, kind="Internal").ap()
        CH = -(-E // P)
        gp_rows = gath[:, 0, 0, 0, :]
        gp_acc = gath[:, 0, 0, 1, :]
        gp_res = gath[:, 0, 0, 2, :]
        gp_dst_row = gath[:, 0, 1, 0, 0:P].bitcast(I32)
        gp_away = gath[:, 0, 1, 1, 0:P]
        gp_val = gath[:, 0, 1, 2:4, :].rearrange("p a c -> p (a c)")[:, 0:H * P].rearrange("p (h e) -> p h e", h=H)
        gp_onehot = gath[:, 0, 1, 4, 0:NT]
        gp_onehot_t = gath[:, 0, 1, 5, 0:P]
        gp_nmax, gp_cmax, gp_zmax = (gath[:, 0, 1, 6, i * H:(i + 1) * H] for i in range(3))
        gp_edm = gath[:, 0, 1, 7, 0:2 * H]
        gp_z, gp_l, gp_w, gp_den = (gath[:, 0, 1, 8, i * H:(i + 1) * H] for i in range(4))
        gp_src = sb("gp_src", [P, 1], U32)
        gp_dst = sb("gp_dst", [P, 1], I32)
        gp_dist = sb("gp_dist", [P, 1])
        gp_rel = sb("gp_rel", [P, 1])
        table_ready = sem("table_ready")
        gp_dve = sem("gp_dve")
        max_in, max_rows, sum_in, sum_rows = sem("max_in"), sem("max_rows"), sem("sum_in"), sem("sum_rows")
        max_spread = sem("max_spread")
        max_free, sum_free, tile_go, res_free = sem("max_free"), sem("sum_free"), sem("tile_go"), sem("res_free")
        sum_masks, sum_edge, sum_logit, sum_ex, sum_msg, sum_agg = (
            sem("sum_masks"), sem("sum_edge"), sem("sum_logit"), sem("sum_ex"),
            sem("sum_msg"), sem("sum_agg"))
        res_ready, res_stored, gp_tables, gp_plan = sem("res_ready"), sem("res_stored"), sem("gp_tables"), sem("gp_plan")
        MAX_STEPS, SUM_STEPS, TILE_STEPS = 3, 5, 5

        def general(eng, path):
            eng.wait_ge(p_ready, 1)
            flag = eng.value_load(plan_i[0:1, P:P + 1], min_val=0, max_val=2 * P)
            with eng.If(flag > 0):
                path()

        xnt = x1
        setup = gath[:].rearrange("p r u t c -> p (r u t c)")
        x_first = x_res
        XALL = RING * 2 * TE * ROW - (NP - 2) * 2 * D
        x_all = setup[:, XALL:RING * 2 * TE * ROW]
        taken = 0

        def area(size):
            nonlocal taken
            taken += size
            assert taken <= XALL
            return setup[:, taken - size:taken]

        ft_rows = area(4 * ROW).rearrange("p (r u c) -> p r u c", r=2, u=2)
        dst_all, dst_prev, blk = (area(EB).bitcast(I32) for _ in range(3))
        scr, scr2 = area(EB), area(EB)
        bn_rows = area(2 * P).rearrange("p (l c) -> p l c", l=2)
        att = area(2 * D).rearrange("p (k c) -> p k c", k=2)
        att_prod = area(D)
        plan_f = area(3 * P + 1)[0:1, :]
        J = TILES + 1
        blk_i = sb("blk_i", [P, 1], I32)
        plan_cols = sb("plan_cols", [P, 5])
        coarse, fine, startf, blkf, bad1 = (plan_cols[:, i:i + 1] for i in range(5))
        first_dst = sb("first_dst", [P, J])

        x_pairs = x.rearrange("(g u p) d -> g p u d", u=2, p=NT)
        out_pairs = out.rearrange("(g u p) d -> g p u d", u=2, p=NT)
        table_pairs = table.rearrange("(g u p) d -> g p u d", u=2, p=NT)

        block = ctx.enter_context(nc.Block())

        PER_WIN = 16 * 6
        PER_ROWS = 16 * 2 * TE

        @block.sync
        def _(sp):
            sp.dma_start(wx[:, :, 0:D], W.rearrange("(c k) n -> k c n", k=P)).then_inc(attn_in, 16)
            sp.dma_start(att[:, 0, :], att_src.rearrange("a h c -> a (h c)").broadcast_to([P, D])).then_inc(attn_in, 16)
            sp.dma_start(att[:, 1, :], att_dst.rearrange("a h c -> a (h c)").broadcast_to([P, D])).then_inc(attn_in, 16)

            def load_x(g):
                if g.begins(2):
                    target = x_first[0:NT, g.par, :, :]
                else:
                    sp.wait_ge(t_x[g.par], g.half * 16)
                    sp.sem_inc(passed, 1)
                    target = x_all[0:NT, bass.ds((g.n - 2) * 2 * D, 2 * D)].rearrange("p (u d) -> p u d", u=2)
                sp.dma_start(target, x_pairs[g.n]).then_inc(t_x[g.par], 16)

            load_x(Pair(0, 0))
            load_x(Pair(0, 1))
            sp.dma_start(dst_all[0:NT, :], dst.rearrange("(a b) -> a b", a=NT)).then_inc(p_all, 16)
            load_x(Pair(0, 2))
            load_x(Pair(0, 3))

            def store_rows(g):
                sp.wait_ge(t_kept, g.n * 2 + 2)
                sp.sem_inc(passed, 1)
                sp.dma_start(table_pairs[g.n], ft_rows[0:NT, g.par, :, :]).then_inc(t_stored[g.par], 16)

            def load_and_store(g):
                load_x(g)
                store_rows(g + -4)

            over_pairs(sp, 4, NP, load_and_store)
            for n in range(NP - 4, NP):
                store_rows(Pair(0, n))

            sp.wait_ge(t_stored[0], 16 * ((NP + 1) // 2))
            sp.wait_ge(t_stored[1], 16 * (NP // 2))
            sp.nop().then_inc(table_ready, 1)

            def path():
                sp.sem_inc(res_free, 1)
                with sp.Fori(0, TILES) as j:
                    sp.wait_ge(res_ready, j + 1)
                    sp.dma_start(table2[bass.ds(j * NT, NT), :], gp_res[0:NT, :]).then_inc(res_stored, 16)
                    sp.wait_ge(res_stored, j * 16 + 16)
                    sp.sem_inc(res_free, 1)
                sp.wait_ge(sum_free, TILES * CH + 1)
                sp.dma_start(table.rearrange("(a b) c -> a (b c)", a=NT), table2.rearrange("(a b) c -> a (b c)", a=NT)).then_inc(gp_tables, 16)
                sp.dma_start(src_pad[0:N].rearrange("(p j) -> p j", p=NT), ids_i[0:NT, :]).then_inc(gp_tables, 16)
                sp.dma_start(dst_pad[1:1 + N].rearrange("(p j) -> p j", p=NT), ids_i[0:NT, :]).then_inc(gp_tables, 16)
                sp.dma_start(dst_pad[1 + N:1 + N + WIN].rearrange("(a b) -> a b", a=P), neg_fill[:, 0:TE]).then_inc(gp_tables, 16)
                sp.dma_start(dist_pad[0:N].rearrange("(p j) -> p j", p=NT), ones[0:NT, 0:TILES]).then_inc(gp_tables, 16)
                sp.wait_ge(gp_tables, 16 * 5)
                sp.wait_ge(gp_plan, 1)

            general(sp, path)
            sp.nop().then_inc(setup_done, 1)

            def load_windows(g):
                for u in range(2):
                    first = sp.value_load(plan_i[0:1, bass.ds(g.n * 2 + u, 1)], min_val=0, max_val=E)
                    for buf, dram, off in ((src_win, src_pad.bitcast(U32), 0), (dst_win, dst_pad, 1), (dist_win, dist_pad, 0)):
                        sp.dma_start(buf[:, g.par, u, :], dram[bass.ds(first + off, WIN)].rearrange("(p t) -> p t", t=TE)).then_inc(win_in[g.par], 16)

            def load_res(g):
                sp.dma_start(x_res[0:NT, g.par, :, :], x_pairs[g.n]).then_inc(x_in[g.par], 16)

            def load_dst_row(g, c):
                if not g.begins(1) or c:
                    sp.wait_ge(onehotT_ready, g.n * 4 + c)
                    sp.sem_inc(passed, 1)
                first = sp.value_load(plan_i[0:1, bass.ds(g.n * 2 + c // 2, 1)], min_val=0, max_val=E)
                sp.dma_start(dst_row[:], dst_pad[bass.ds(first + 1 + (c % 2) * (WIN // 2), WIN // 2)].rearrange("(a t) -> a t", a=1).broadcast_to([P, WIN // 2])
                             ).then_inc(dst_row_in, 16)

            def store(f):
                sp.wait_ge(y_added, f.n * YS + YS)
                sp.sem_inc(passed, 1)
                sp.dma_start(out_pairs[f.n], x1[0:NT, f.par, :, :]).then_inc(out_stored[f.par], 16)

            load_windows(Pair(0, 0))
            load_dst_row(Pair(0, 0), 0)
            load_windows(Pair(0, 1))
            load_res(Pair(0, 0))
            load_res(Pair(0, 1))

            def body(f, g, a):
                reload = g is not None and (g + 2).within(NP)
                if reload:
                    sp.wait_ge(msg_ready, g.n * CHUNKS + 1)
                    sp.sem_inc(passed, 1)
                    load_windows(g + 2)
                if f is not None and not f.begins(1):
                    store(f + -1)
                if a is not None:
                    for c in range(1, 4):
                        load_dst_row(a, c)
                if reload:
                    sp.wait_ge(xn_ready, g.n * 2 + 2)
                    sp.sem_inc(passed, 1)
                    load_res(g + 2)
                if a is not None and (a + 1).within(NP):
                    load_dst_row(a + 1, 0)

            over_stages(sp, NP, body, tail=1)
            store(Pair(0, NP - 1))
            sp.wait_ge(out_stored[0], 16 * ((NP + 1) // 2))
            sp.wait_ge(out_stored[1], 16 * (NP // 2))

        @block.gpsimd
        def _(pool):
            pool.memset(ident[:], 1.0).then_inc(consts, 1)
            pool.memset(pad_fill[:], 0).then_inc(fills, 1)
            pool.memset(neg_fill[:], -1).then_inc(fills, 1)
            pool.memset(ones[:], 1.0).then_inc(consts, 1)
            pool.memset(eps_ln[:], LN_EPS).then_inc(consts, 1)
            pool.wait_ge(consts, 3)
            pool.affine_select(out=ident[:], in_=ident[:], compare_op=ALU.is_equal, fill=0.0, base=0,
                               pattern=[[1, P]], channel_multiplier=-1).then_inc(consts, 1)
            pool.iota(iota_i[:], [[1, NT]], base=0, channel_multiplier=0).then_inc(consts, 1)
            pool.iota(base_i[:], [[NT, TILES]], base=0, channel_multiplier=0).then_inc(consts, 1)
            pool.iota(node_i[:], [[NT, TILES]], base=0, channel_multiplier=1).then_inc(consts, 1)
            pool.iota(ids_i[:], [[1, TILES]], base=0, channel_multiplier=TILES).then_inc(consts, 1)
            pool.iota(bound_i[:], [[1, 1]], base=0, channel_multiplier=NT).then_inc(consts, 1)
            pool.wait_ge(fills, 2)
            pool.dma_start(dst_pad[1:1 + E].rearrange("(a b) -> a b", a=NT), dst.rearrange("(a b) -> a b", a=NT)).then_inc(pads_src, 16)
            pool.dma_start(src_pad[0:E].rearrange("(a b) -> a b", a=NT), src.rearrange("(a b) -> a b", a=NT)).then_inc(pads_src, 16)
            pool.dma_start(dist_pad[0:E].rearrange("(a b) -> a b", a=NT),
                         dist.rearrange("(a b) c d -> a (b c d)", a=NT)).then_inc(pads_src, 16)
            pool.dma_start(src_pad[E:E + WIN].rearrange("(a b) -> a b", a=P), pad_fill[:, 0:TE]).then_inc(pads_src, 16)
            pool.dma_start(dist_pad[E:E + WIN].rearrange("(a b) -> a b", a=P).bitcast(I32), pad_fill[:, 0:TE]).then_inc(pads_src, 16)
            pool.dma_start(dst_pad[1 + E:1 + E + WIN].rearrange("(a b) -> a b", a=P), neg_fill[:, 0:TE]).then_inc(pads_src, 16)
            pool.dma_start(dst_pad[0:1].rearrange("(a b) -> a b", a=1), neg_fill[0:1, 0:1]).then_inc(pads_src, 16)
            pool.wait_ge(pads_src, 16 * 7)
            pool.dma_start(dst_prev[0:NT, :], dst_pad[0:E].rearrange("(a b) -> a b", a=NT)).then_inc(p_in, 16)
            pool.wait_ge(p_block, 1)
            pool.indirect_dma_start(blk[0:J, :], None, dst.rearrange("(a b) -> a b", a=NT),
                                    bass.IndirectOffsetOnAxis(blk_i[0:J, 0:1].bitcast(U32), 0)).then_inc(p_fetched, 16)
            def path():
                pool.wait_ge(table_ready, 1)
                pool.sem_inc(tile_go, 1)
                with pool.Fori(0, TILES) as j:
                    with pool.Fori(0, CH) as i:
                        pool.wait_ge(max_free, j * CH + i + 1)
                        pool.dma_start(gp_src[:], src_pad[bass.ds(i * P, P)].rearrange("(p a) -> p a", a=1).bitcast(U32)).then_inc(max_in, 16)
                        pool.dma_start(gp_dst_row, dst_pad[bass.ds(i * P + 1, P)].rearrange("(a e) -> a e", a=1).broadcast_to([P, P])).then_inc(max_in, 16)
                        pool.wait_ge(max_in, i * 32 + 32)
                        pool.sem_inc(passed, 1)
                        pool.indirect_dma_start(gp_rows, None, table, bass.IndirectOffsetOnAxis(gp_src[:, 0:1], 0)).then_inc(max_rows, 16)
                    pool.wait_ge(max_free, j * CH + CH + 1)
                    pool.sem_inc(passed, 1)
                    with pool.Fori(0, CH) as i:
                        pool.wait_ge(sum_free, j * CH + i + 1)
                        pool.dma_start(gp_src[:], src_pad[bass.ds(i * P, P)].rearrange("(p a) -> p a", a=1).bitcast(U32)).then_inc(sum_in, 16)
                        pool.dma_start(gp_dst[:], dst_pad[bass.ds(i * P + 1, P)].rearrange("(p a) -> p a", a=1)).then_inc(sum_in, 16)
                        pool.dma_start(gp_dist[:], dist_pad[bass.ds(i * P, P)].rearrange("(p a) -> p a", a=1)).then_inc(sum_in, 16)
                        pool.dma_start(gp_dst_row, dst_pad[bass.ds(i * P + 1, P)].rearrange("(a e) -> a e", a=1).broadcast_to([P, P])).then_inc(sum_in, 16)
                        pool.wait_ge(sum_in, i * 64 + 64)
                        pool.sem_inc(passed, 1)
                        pool.indirect_dma_start(gp_rows, None, table, bass.IndirectOffsetOnAxis(gp_src[:, 0:1], 0)).then_inc(sum_rows, 16)
                    pool.wait_ge(sum_free, j * CH + CH + 1)
                    pool.sem_inc(passed, 1)
                    pool.inc_swdge_sem([max_in, max_rows, sum_in, sum_rows], [32 * CH, 16 * CH, 64 * CH, 16 * CH], mode="sub")
                    pool.nop().then_inc(tile_go, 1)

            general(pool, path)
            pool.wait_ge(setup_done, 1)

            def gather(g):
                pool.wait_ge(win_in[g.par], (g.half + 1) * PER_WIN)
                pool.sem_inc(passed, 1)
                for u in range(2):
                    if not g.begins(2):
                        pool.wait_ge(lo_ready, g.n * CHUNKS - 6 + 2 * u)
                        pool.sem_inc(passed, 1)
                    for t in range(TE):
                        pool.indirect_dma_start(gath[:, g.par, u, t, :], None, table,
                                                bass.IndirectOffsetOnAxis(src_win[:, g.par, u, t:t + 1], 0)
                                                ).then_inc(rows_in[g.par], 16)

            over_pairs(pool, 0, NP, gather, peel=2)

        @block.tensor
        def _(pe):
            pe.wait_ge(consts, 9)
            pe.wait_ge(small_in, 16 * 13)
            for l in range(2):
                mm = pe.transpose(bankC[:, l * 80:l * 80 + 80], bn_rows[0:80, l, :], ident[0:80, 0:80])
            mm.then_inc(bn_turned, 1)

            def turn_x(g):
                pe.wait_ge(t_norm, g.n * 2 + 2)
                if not g.begins(1):
                    pe.wait_ge(t_xT, g.n)
                for u in range(2):
                    for c in range(KC):
                        mm = pe.transpose(bankA[:, (u * KC + c) * NT:(u * KC + c + 1) * NT],
                                          xnt[0:NT, g.par, u, c * P:(c + 1) * P], ident[0:NT, 0:NT])
                mm.then_inc(t_turned, 1)

            def project(g):
                pe.wait_ge(t_xT, g.n + 1)
                if not g.begins(1):
                    pe.wait_ge(t_rows, g.n * 2)
                for u in range(2):
                    for c in range(KC):
                        mm = pe.matmul(bankE[u][0:NT, 0:ROWX], xT[:, g.par, c, u, :], wx[:, c, :],
                                       start=(c == 0), stop=(c == KC - 1))
                    mm.then_inc(t_ft, 1)

            pe.wait_ge(wx_ready, 1)
            turn_x(Pair(0, 0))

            def table_turn(g):
                turn_x(g)
                project(g + -1)

            pe.wait_ge(p_first, 1)
            pe.matmul(bankH1[0:J, 0:NT], first_dst[0:NT, :], ident[0:NT, 0:NT], start=True, stop=True).then_inc(p_coarse, 1)
            over_pairs(pe, 1, NP, table_turn, peel=1)
            project(Pair(0, NP - 1))
            pe.wait_ge(p_row, 1)
            pe.matmul(bankH2[0:1, 0:J], startf[0:J, :], ident[0:J, 0:J], start=True, stop=True)
            pe.matmul(bankH2[0:1, P:P + 1], bad1[0:NT, :], ones[0:NT, 0:1], start=True, stop=True).then_inc(p_flag, 1)

            def turn_logits(g):
                pe.wait_ge(rel_ready, g.n + 1)
                pe.wait_ge(esrc_kept, g.n + 1)
                for u in range(2):
                    pe.transpose(bankA[0:TH, u * 2 * P:u * 2 * P + P], esrc[:, u, :], ident[:, :])
                    mm = pe.transpose(bankA[0:TH, u * 2 * P + P:(u + 1) * 2 * P],
                                      rel[:, u, :, :].rearrange("p t h -> p (t h)"), ident[:, :])
                mm.then_inc(turn_done, 1)

            def turn_back(g):
                pe.wait_ge(seg_done, g.n + 1)
                for u in range(2):
                    pe.transpose(bankB[:, (u * 2) * TH:(u * 2 + 1) * TH], scan_end[:, u, :], ident[0:TH, 0:TH])
                    mm = pe.transpose(bankB[:, (u * 2 + 1) * TH:(u * 2 + 2) * TH], change[:, u, 1:P + 1],
                                      ident[0:TH, 0:TH])
                mm.then_inc(back_done, 1)

            def to_nodes(g):
                pe.wait_ge(ends_ready, g.n + 1)
                for u in range(2):
                    pe.wait_ge(onehot_ready, g.n * 2 + u + 1)
                    for t in range(TE):
                        col = (u * TE + t) * NCOL
                        mm = pe.matmul(bankC[0:NT, col:col + NCOL], onehot_b[:, u, t, :], ends[:, u, t, :],
                                       start=True, stop=True)
                        if u * TE + t == 2 * TE - 1:
                            mm.then_inc(nodes_done, 1)
                        yield

            def to_edges(g):
                pe.wait_ge(onehotT_ready, g.n * 4 + 4)
                pe.wait_ge(edm_ready, g.n + 1)
                for u in range(2):
                    for t in range(TE):
                        col = (u * TE + t) * 2 * H
                        for part in range(PARTS):
                            mm = pe.matmul(bankB[:, col:col + 2 * H], onehot_t[0:NT, u, t:WIN:TE], edm_parts[0:NT, part, u, :],
                                           start=(part == 0), stop=(part == PARTS - 1))
                        if u * TE + t == 2 * TE - 1:
                            mm.then_inc(edge_done, 1)
                        yield

            def aggregate(g, c):
                pe.wait_ge(onehot_kept, g.n * CHUNKS + c + 1)
                pe.wait_ge(lo_ready, g.n * CHUNKS + c + 1)
                u, cols = c // 2, (c % 2) * TC
                for t in range(TC):
                    pe.matmul(bankE[u][0:NT, 0:ROW], onehot[:, t, :], msg_hi[:, t, :],
                              start=(cols + t == 0), stop=False)
                    mm = pe.matmul(bankE[u][0:NT, 0:ROW], onehot[:, t, :], msg_lo[:, t, :],
                                   start=False, stop=(cols + t == TE - 1))
                mm.then_inc(agg_done, 1)

            def turn_x1(g):
                pe.wait_ge(xn_ready, g.n * 2 + 2)
                for u in range(2):
                    for c in range(KC):
                        mm = pe.transpose(bankA[:, (c * 2 + u) * NT:(c * 2 + u + 1) * NT],
                                          xn[0:NT, u, c * P:(c + 1) * P], ident[0:NT, 0:NT])
                mm.then_inc(xT_done, 1)

            def route(g):
                pe.wait_ge(xT_ready, g.n + 1)
                for u in range(2):
                    o = bankE[1][0:NT, u * EX:(u + 1) * EX]
                    for c in range(KC):
                        pe.matmul(o, xT[:, g.par, c, u, :], wr[:, c, :], start=(c == 0), stop=False)
                    mm = pe.matmul(o, ones[0:1, 0:NT], br_row[0:1, :], start=False, stop=True)
                mm.then_inc(route_done, 1)

            def turn_gate(f):
                pe.wait_ge(gate_ready, f.n + 1)
                for u in range(2):
                    mm = pe.transpose(bankC[0:EX, u * NT:(u + 1) * NT], gate[0:NT, f.par, u, :], ident[0:NT, 0:NT])
                mm.then_inc(gateT_done, 1)

            def out_bias(f):
                pe.wait_ge(gateT_kept, f.n + 1)
                if not f.begins(1):
                    pe.wait_ge(y_added, f.n * YS)
                for u in range(2):
                    mm = pe.matmul(bankY[0:NT, u * D:(u + 1) * D], gate_t[:, u, :], bo_rows[:, :], start=True, stop=True)
                mm.then_inc(y_done, 1)

            def layer(weights, e, operand, target, between):
                for hc in range(KC):
                    for c in range(KC):
                        mm = pe.matmul(target[:, hc * 2 * NT:(hc + 1) * 2 * NT],
                                       weights[:, e * KC + c, hc * P:(hc + 1) * P], operand(c),
                                       start=(c == 0), stop=(c == KC - 1))
                        if hc * KC + c < KC * KC - 1:
                            between()
                return mm

            def layer1(f, e, between):
                if e or not f.begins(1):
                    pe.wait_ge(h1_kept, f.n * EX + e)
                if e == 0:
                    pe.wait_ge(xT_ready, f.n + 1)
                    if f.begins(1):
                        pe.wait_ge(weights_in, 16 * 3)
                layer(w1, e, lambda c: xT[:, f.par, c, :, :].rearrange("p u n -> p (u n)"), bankH1, between).then_inc(h1_done, 1)

            def layer2(f, e, between):
                pe.wait_ge(h1_kept, f.n * EX + e + 1)
                if e or not f.begins(1):
                    pe.wait_ge(h2_kept, f.n * EX + e)
                layer(w2, e, lambda c: h1[:, c, :, :].rearrange("p u n -> p (u n)"), bankH2, between).then_inc(h2_done, 1)

            def layer3(f, e, between):
                pe.wait_ge(h2_kept, f.n * EX + e + 1)
                pe.wait_ge(y_added, f.n * YS + e + 1)
                for u in range(2):
                    for c in range(KC):
                        mm = pe.matmul(bankY[0:NT, u * D:(u + 1) * D], h2[:, c, u, :], wo[:, e * KC + c, :],
                                       start=(c == 0), stop=(c == KC - 1))
                        if u * KC + c < 2 * KC - 1:
                            between()
                mm.then_inc(y_done, 1)

            def nothing():
                pass

            def body(f, g, a):
                for s in range(EX):
                    small = to_nodes(a) if a is not None and s == 7 else to_edges(g) if g is not None and s == 0 else iter(())

                    def between():
                        for _ in range(SMALL_RUN):
                            next(small, None)

                    if f is not None:
                        layer1(f, s, between if s == 7 else nothing)
                        if s == 0:
                            route(f)
                        if s == 1:
                            turn_gate(f)
                        if s == 2:
                            out_bias(f)
                    if a is not None:
                        if s == 2:
                            turn_logits(a)
                        if s == 4:
                            turn_back(a)
                    if f is not None and (s >= 1 or not f.begins(1)):
                        layer2(*before(f, s, 1), between)
                    if g is not None and s == 7:
                        turn_x1(g)
                    if f is not None and (s >= 2 or not f.begins(1)):
                        layer3(*before(f, s, 2), between)
                    for _ in small:
                        pass
                    if g is not None and 2 <= s < 2 + CHUNKS:
                        aggregate(g, s - 2)

            def path():
                with pe.Fori(0, TILES) as j:
                    pe.wait_ge(tile_go, j + 1)
                    pe.sem_inc(passed, 1)
                    with pe.Fori(0, CH) as i:
                        pe.wait_ge(max_rows, i * 16 + 16)
                        for h in range(H):
                            mm = pe.matmul(bankA[0:NT, h * P:(h + 1) * P], gp_rows[:, D + h:D + h + 1].broadcast_to([P, NT]),
                                           ident[:, :], start=True, stop=True)
                        mm.then_inc(max_spread, 1)
                    with pe.Fori(0, CH) as i:
                        pe.wait_ge(sum_masks, j * CH + i + 1)
                        pe.matmul(bankB[:, 0:2 * H], gp_onehot_t[0:NT, :], gp_edm[0:NT, :], start=True, stop=True).then_inc(sum_edge, 1)
                        pe.wait_ge(sum_msg, j * CH + i + 1)
                        pe.matmul(bankE[0][0:NT, 0:ROW], gp_onehot[:, :], gp_rows[:, :], start=True, stop=True).then_inc(sum_agg, 1)

            general(pe, path)

            over_stages(pe, NP, body)
            last = Pair(0, NP - 1)
            layer2(last, EX - 1, nothing)
            layer3(last, EX - 2, nothing)
            layer3(last, EX - 1, nothing)

        @block.scalar
        def _(act):
            act.dma_start(wr[:], Wr.rearrange("(c k) e -> k c e", k=P)).then_inc(small_in, 16)
            act.dma_start(br_row[:], br.rearrange("(a e) -> a e", a=1)).then_inc(small_in, 16)
            act.dma_start(bo_rows[:], bo).then_inc(small_in, 16)
            for l, params in enumerate(((b1, g1, be1, m1, v1), (b2, g2, be2, m2, v2))):
                for i, prm in enumerate(params):
                    act.dma_start(bn_rows[16 * i:16 * i + 16, l, :], prm.rearrange("e (c k) -> (e c) k", k=P)).then_inc(small_in, 16)

            act.wait_ge(consts, 3)

            def root(g):
                act.wait_ge(t_var, g.n + 1)
                act.activation(t_root[0:NT, g.par, :], t_mv[0:NT, g.par, :, 1], ACT.Sqrt, bias=eps_ln[0:NT, :]).then_inc(t_std, 1)

            def keep_xT(g):
                act.wait_ge(t_turned, g.n + 1)
                if not g.begins(2):
                    act.wait_ge(t_ft, g.n * 2 - 2)
                act.activation(xT[:, g.par, :, :, :].rearrange("p c u n -> p u c n"),
                               bankA[:, 0:2 * KC * NT].rearrange("p (u c n) -> p u c n", u=2, c=KC),
                               ACT.Copy).then_inc(t_xT, 1)

            def keep_rows(g):
                act.wait_ge(t_ft, g.n * 2 + 2)
                if not g.begins(2):
                    act.wait_ge(t_stored[g.par], g.half * 16)
                for u in range(2):
                    act.activation(ft_rows[0:NT, g.par, u, :], bankE[u][0:NT, 0:ROW], ACT.Copy).then_inc(t_kept, 1)
                    act.activation(edst[0:NT, bass.ds(g.n * 2 + u, 1), :].rearrange("p a h -> p (a h)"),
                                   bankE[u][0:NT, ROW:ROWX], ACT.Copy).then_inc(t_rows, 1)

            root(Pair(0, 0))
            root(Pair(0, 1))
            keep_xT(Pair(0, 0))

            def turn(g):
                root(g)
                keep_xT(g + -1)
                keep_rows(g + -2)

            over_pairs(act, 2, NP, turn, peel=2)
            keep_xT(Pair(0, NP - 1))
            keep_rows(Pair(0, NP - 2))
            keep_rows(Pair(0, NP - 1))
            act.wait_ge(bn_sum, 1)
            act.activation(bn_cols[:, :, 4, :], bn_cols[:, :, 4, :], ACT.Sqrt).then_inc(bn_root, 1)

            def keep_esrc(g):
                act.wait_ge(rows_in[g.par], (g.half + 1) * PER_ROWS)
                act.activation(esrc[:].rearrange("p u (t h) -> p (u t) h", h=H),
                               gath[:, g.par, :, :, D:ROW].rearrange("p u t h -> p (u t) h"), ACT.Copy).then_inc(esrc_kept, 1)

            def keep_turned(g):
                act.wait_ge(turn_done, g.n + 1)
                act.activation(turned[:].rearrange("r u k e -> r (u k e)"), bankA[0:TH, 0:4 * P], ACT.Copy).then_inc(turn_kept, 1)

            def keep_onehot(g, c):
                act.wait_ge(onehot_ready, g.n * 2 + c // 2 + 1)
                if c or not g.begins(1):
                    act.wait_ge(agg_done, g.n * CHUNKS + c)
                cols = (c % 2) * TC
                act.activation(onehot[:], onehot_b[:, c // 2, cols:cols + TC, :], ACT.Copy).then_inc(onehot_kept, 1)

            def keep_high(g, c):
                act.wait_ge(msg_ready, g.n * CHUNKS + c + 1)
                if c or not g.begins(1):
                    act.wait_ge(agg_done, g.n * CHUNKS + c)
                cols = (c % 2) * TC
                act.activation(msg_hi[:], gath[:, g.par, c // 2, cols:cols + TC, :], ACT.Copy).then_inc(hi_ready, 1)

            def exp_logits(g):
                act.wait_ge(logit_ready, g.n + 1)
                act.activation(gath[:, g.par, :, :, D:ROW].rearrange("p u t h -> p (u t) h"), lz[:, :, :], ACT.Exp).then_inc(ex_ready, 1)

            def root1(g, u):
                act.wait_ge(var_ready, g.n * 2 + u + 1)
                act.activation(std[0:NT, u:u + 1], mv[0:NT, u, 1:2], ACT.Sqrt, bias=eps_ln[0:NT, :]).then_inc(std_ready, 1)

            def keep_x1T(g):
                act.wait_ge(xT_done, g.n + 1)
                act.activation(xT[:, g.par, :, :, :].rearrange("p c u n -> p (c u n)"), bankA[:, 0:2 * KC * NT], ACT.Copy).then_inc(xT_ready, 1)

            def exp_route(f):
                act.wait_ge(rsub_ready, f.n + 1)
                act.activation(rexp[0:NT, :, :], rsub[0:NT, :, :], ACT.Exp).then_inc(rexp_ready, 1)

            def keep_gate(f):
                act.wait_ge(gateT_done, f.n + 1)
                act.activation(gate_t[:].rearrange("e u n -> e (u n)"), bankC[0:EX, 0:2 * NT], ACT.Copy).then_inc(gateT_kept, 1)

            def relu(f, e, l, done, target, source):
                act.wait_ge(done, f.n * EX + e + 1)
                kept = h1_kept if l == 0 else h2_kept
                for hc in range(KC):
                    ins = act.activation(target[:, hc, :, :].rearrange("p u n -> p (u n)"),
                                         source[:, hc * 2 * NT:(hc + 1) * 2 * NT], ACT.Relu,
                                         bias=bn_shift[:, l, e * KC + hc:e * KC + hc + 1],
                                         scale=bn_scale[:, l, e * KC + hc:e * KC + hc + 1])
                ins.then_inc(kept, 1)

            def relu1(f, e):
                if e or not f.begins(1):
                    act.wait_ge(h2_done, f.n * EX + e)
                relu(f, e, 0, h1_done, h1, bankH1)

            def relu2(f, e):
                if e or not f.begins(1):
                    act.wait_ge(y_done, f.n * YS + e + (1 if e else 0))
                relu(f, e, 1, h2_done, h2, bankH2)

            def body(f, g, a):
                for s in range(EX):
                    if g is not None and s == 6:
                        root1(g, 0)
                    if g is not None and s == 1:
                        exp_logits(g)
                    if f is not None:
                        if s == 0:
                            exp_route(f)
                        relu1(f, s)
                        if s == 1:
                            keep_gate(f)
                    if a is not None and s == 2:
                        keep_turned(a)
                    if g is not None and s == 7:
                        keep_x1T(g)
                    if f is not None and (s >= 1 or not f.begins(1)):
                        relu2(*before(f, s, 1))
                    if a is not None and s == 1:
                        keep_esrc(a)
                    if g is not None:
                        if 1 <= s < 1 + CHUNKS:
                            keep_high(g, s - 1)
                        if 2 <= s < 1 + CHUNKS:
                            keep_onehot(g, s - 1)
                        if s == 6:
                            root1(g, 1)
                    if a is not None and s == 7:
                        keep_onehot(a, 0)

            def path():
                with act.Fori(0, TILES) as j:
                    with act.Fori(0, CH) as i:
                        act.wait_ge(sum_logit, j * CH + i + 1)
                        act.activation(gp_rows[:, D:ROW], gp_l, ACT.Exp).then_inc(sum_ex, 1)

            general(act, path)
            act.wait_ge(bn_ready, 1)
            act.wait_ge(win_in[1], PER_WIN)
            act.sem_inc(passed, 1)
            for buf, dram in ((w1, W1), (w2, W2), (wo, Wo)):
                act.dma_start(buf[:], dram.rearrange("e (c k) n -> k (e c) n", k=P)).then_inc(weights_in, 16)
            over_stages(act, NP, body)
            relu2(Pair(0, NP - 1), EX - 1)

        @block.vector
        def _(dve):
            own = Chain(dve, dve_step)
            dve.wait_ge(consts, 9)
            own.did(dve.tensor_copy(iota[:], iota_i[:]))
            own.did(dve.tensor_copy(base[:], base_i[:]))
            own.did(dve.tensor_copy(node[:], node_i[:]))
            own.did(dve.tensor_copy(bound[:], bound_i[:]))
            own.did(dve.memset(change[:], 1.0))
            dve.wait_ge(attn_in, 48)
            for c in range(KC):
                for k in range(2):
                    own.did(dve.tensor_tensor(att_prod, wx[:, c, 0:D], att[:, k, :], ALU.mult))
                    own.settle()
                    ins = dve.tensor_reduce(wx[:, c, D + k * H:D + (k + 1) * H],
                                            att_prod.rearrange("p (h c) -> p h c", h=H), AX.X, ALU.add)
                    if c == KC - 1 and k == 1:
                        ins.then_inc(wx_ready, 1)
                    else:
                        own.did(ins)
                        own.settle()
            fixed = own.count

            def x_of(g, u):
                if g.begins(2):
                    return x_first[0:NT, g.par, u, :]
                return x_all[0:NT, bass.ds((g.n - 2) * 2 * D + u * D, D)]

            def moments(g):
                if not g.begins(1):
                    dve.wait_ge(t_var, g.n)
                dve.wait_ge(t_x[g.par], (g.half + 1) * 16)
                for u in range(2):
                    ins = dve.bn_stats(stats[0:NT, u, :], x_of(g, u))
                own.did(ins)
                own.settle(alone=passed)
                for u in range(2):
                    ins = dve.bn_aggr(t_mv[0:NT, g.par, u, :], stats[0:NT, u, :])
                ins.then_inc(t_var, 1)

            def norm(g):
                dve.wait_ge(t_std, g.n + 1)
                own.did(dve.reciprocal(t_root[0:NT, g.par, :], t_root[0:NT, g.par, :]))
                own.settle()
                if not g.begins(2):
                    dve.wait_ge(t_turned, g.n - 1)
                for u in range(2):
                    dve.tensor_scalar(xnt[0:NT, g.par, u, :], x_of(g, u), t_mv[0:NT, g.par, u, 0:1],
                                      t_root[0:NT, g.par, u:u + 1], ALU.subtract, ALU.mult).then_inc(t_norm, 1)

            def normalise(g):
                own.start(fixed + g.n * 2 - 1)
                moments(g)
                norm(g + -1)

            own.start(fixed)
            moments(Pair(0, 0))
            normalise(Pair(0, 1))
            dve.wait_ge(p_all, 16)
            dve.tensor_copy(first_dst[0:NT, :], dst_all[0:NT, 0:1].broadcast_to([NT, J])).then_inc(p_first, 1)

            own.start(fixed + 3)
            dve.wait_ge(p_coarse, 1)
            own.did(dve.tensor_scalar(scr[0:J, 0:NT], bankH1[0:J, 0:NT], bound[0:J, :], None, ALU.is_lt, ALU.add,
                                      accum_out=coarse[0:J, :]))
            own.settle()
            own.did(dve.tensor_scalar(blkf[0:J, :], coarse[0:J, :], -1.0, 0.0, ALU.add, ALU.max))
            own.settle()
            dve.tensor_copy(blk_i[0:J, :], blkf[0:J, :]).then_inc(p_block, 1)
            fixed += own.count

            over_pairs(dve, 2, NP, normalise, peel=1)
            own.start(fixed + 2 * NP - 1)
            norm(Pair(0, NP - 1))

            own.start(fixed + 2 * NP)
            dve.wait_ge(p_fetched, 16)
            own.did(dve.tensor_scalar(scr[0:J, :], blk[0:J, :], bound[0:J, :], None, ALU.is_lt))
            own.settle()
            own.did(dve.tensor_reduce(fine[0:J, :], scr[0:J, :], AX.X, ALU.add))
            dve.wait_ge(p_in, 16)
            own.did(dve.tensor_tensor(scr2[0:NT, :], dst_prev[0:NT, :], dst_all[0:NT, :], ALU.is_gt))
            own.settle()
            own.did(dve.scalar_tensor_tensor(startf[0:J, :], blkf[0:J, :], float(EB), fine[0:J, :], ALU.mult, ALU.add))
            own.did(dve.tensor_reduce(bad1[0:NT, :], scr2[0:NT, :], AX.X, ALU.max))
            own.settle()
            dve.nop().then_inc(p_row, 1)

            dve.wait_ge(bn_turned, 1)
            own.did(dve.tensor_copy(bn_cols[:].rearrange("p l k c -> p (l k c)"), bankC[:, 0:2 * 5 * EX * KC]))
            own.settle()
            dve.tensor_scalar(bn_cols[:, :, 4, :], bn_cols[:, :, 4, :], BN_EPS, None, ALU.add).then_inc(bn_sum, 1)
            dve.wait_ge(p_flag, 1)
            own.did(dve.tensor_copy(plan_f[:, 0:J], bankH2[0:1, 0:J]))
            own.did(dve.tensor_copy(plan_f[:, P:P + 1], bankH2[0:1, P:P + 1]))
            own.settle()
            own.did(dve.tensor_tensor(plan_f[:, 2 * P:2 * P + TILES], plan_f[:, 1:J], plan_f[:, 0:TILES], ALU.subtract))
            own.settle()
            own.did(dve.tensor_scalar(plan_f[:, 2 * P:2 * P + TILES], plan_f[:, 2 * P:2 * P + TILES], float(WIN), None,
                                      ALU.is_gt))
            own.settle()
            own.did(dve.tensor_reduce(plan_f[:, 3 * P:3 * P + 1], plan_f[:, 2 * P:2 * P + TILES], AX.X, ALU.add))
            own.settle()
            own.did(dve.tensor_tensor(plan_f[:, P:P + 1], plan_f[:, P:P + 1], plan_f[:, 3 * P:3 * P + 1], ALU.add))
            own.settle()
            own.did(dve.tensor_copy(plan_i[:, 0:J], plan_f[:, 0:J]))
            own.did(dve.tensor_copy(plan_i[:, P:P + 1], plan_f[:, P:P + 1]))
            own.settle()
            dve.nop().then_inc(p_ready, 1)

            dve.wait_ge(bn_root, 1)
            own.did(dve.reciprocal(bn_cols[:, :, 4, :], bn_cols[:, :, 4, :]))
            own.did(dve.tensor_tensor(bn_shift[:], bn_cols[:, :, 0, :], bn_cols[:, :, 3, :], ALU.subtract))
            own.settle()
            own.did(dve.tensor_tensor(bn_scale[:], bn_cols[:, :, 1, :], bn_cols[:, :, 4, :], ALU.mult))
            own.settle()
            own.did(dve.tensor_tensor(bn_shift[:], bn_shift[:], bn_scale[:], ALU.mult))
            own.settle()
            own.did(dve.tensor_tensor(bn_shift[:], bn_shift[:], bn_cols[:, :, 2, :], ALU.add))
            own.settle()
            dve.nop().then_inc(bn_ready, 1)

            def path():
                mine = Chain(dve, gp_dve)
                dve.sem_inc(max_free, 1)
                dve.sem_inc(sum_free, 1)
                with dve.Fori(0, TILES) as j:
                    dve.wait_ge(tile_go, j + 1)
                    tile_base = j * (CH * (MAX_STEPS + SUM_STEPS) + TILE_STEPS)
                    here = node[0:NT, bass.ds(j, 1)]
                    ed = edst[0:NT, bass.ds(j, 1), :].rearrange("n a h -> n (a h)")
                    mine.start(tile_base)
                    mine.did(dve.memset(gp_nmax[0:NT], -BIG))
                    mine.settle(alone=passed)
                    with dve.Fori(0, CH) as i:
                        mine.start(tile_base + i * MAX_STEPS + 1)
                        dve.wait_ge(max_in, i * 32 + 32)
                        mine.did(dve.tensor_scalar(gp_away[0:NT], gp_dst_row[0:NT], here, -BIG, ALU.not_equal, ALU.mult))
                        dve.wait_ge(max_spread, j * CH + i + 1)
                        mine.settle()
                        mine.did(dve.tensor_tensor(gp_val[0:NT], bankA[0:NT, 0:H * P].rearrange("n (h e) -> n h e", h=H),
                                                   gp_away[0:NT].unsqueeze(1).broadcast_to([NT, H, P]), ALU.add))
                        mine.settle()
                        mine.did(dve.tensor_reduce(gp_cmax[0:NT], gp_val[0:NT], AX.X, ALU.max))
                        mine.settle()
                        dve.tensor_tensor(gp_nmax[0:NT], gp_nmax[0:NT], gp_cmax[0:NT], ALU.max).then_inc(max_free, 1)
                        dve.wait_ge(max_free, j * CH + i + 2)
                    mine.start(tile_base + CH * MAX_STEPS + 1)
                    mine.did(dve.tensor_tensor(gp_zmax[0:NT], gp_nmax[0:NT], ed, ALU.add))
                    dve.tensor_copy(gp_edm[0:NT, 0:H], ed)
                    dve.memset(gp_acc[0:NT], 0.0)
                    mine.settle()
                    mine.did(dve.scalar_tensor_tensor(gp_edm[0:NT, H:2 * H], gp_zmax[0:NT], SLOPE, gp_zmax[0:NT], ALU.mult, ALU.max))
                    mine.settle(alone=passed)
                    with dve.Fori(0, CH) as i:
                        mine.start(tile_base + CH * MAX_STEPS + 3 + i * SUM_STEPS)
                        dve.wait_ge(sum_in, i * 64 + 64)
                        mine.did(dve.tensor_scalar(gp_rel[:], gp_dst[:], base[:, bass.ds(j, 1)], None, ALU.subtract))
                        mine.settle()
                        dve.tensor_scalar(gp_onehot[:], iota[:], gp_rel[:], None, ALU.is_equal)
                        dve.tensor_scalar(gp_onehot_t[0:NT], gp_dst_row[0:NT], here, None, ALU.is_equal).then_inc(sum_masks, 1)
                        dve.wait_ge(sum_edge, j * CH + i + 1)
                        dve.wait_ge(sum_rows, i * 16 + 16)
                        mine.did(dve.tensor_tensor(gp_z, gp_rows[:, D:ROW], bankB[:, 0:H], ALU.add))
                        mine.settle()
                        mine.did(dve.scalar_tensor_tensor(gp_l, gp_z, SLOPE, gp_z, ALU.mult, ALU.max))
                        mine.settle()
                        mine.did(dve.tensor_tensor(gp_l, gp_l, bankB[:, H:2 * H], ALU.subtract))
                        mine.settle()
                        dve.tensor_scalar(gp_l, gp_l, 0.0, None, ALU.min).then_inc(sum_logit, 1)
                        dve.wait_ge(sum_ex, j * CH + i + 1)
                        mine.did(dve.tensor_scalar(gp_w, gp_rows[:, D:ROW], gp_dist[:], None, ALU.mult))
                        mine.settle()
                        rows = gp_rows[:, 0:D].rearrange("e (h c) -> e h c", h=H)
                        dve.tensor_tensor(rows, rows, gp_w.unsqueeze(2).broadcast_to([P, H, DH]), ALU.mult).then_inc(sum_msg, 1)
                        dve.wait_ge(sum_agg, j * CH + i + 1)
                        dve.tensor_tensor(gp_acc[0:NT], gp_acc[0:NT], bankE[0][0:NT, 0:ROW], ALU.add).then_inc(sum_free, 1)
                        dve.wait_ge(sum_free, j * CH + i + 2)
                    mine.start(tile_base + CH * (MAX_STEPS + SUM_STEPS) + 3)
                    mine.did(dve.tensor_scalar(gp_den[0:NT], gp_acc[0:NT, D:ROW], TINY, None, ALU.max))
                    mine.settle()
                    mine.did(dve.reciprocal(gp_den[0:NT], gp_den[0:NT]))
                    mine.settle()
                    dve.wait_ge(res_free, j + 1)
                    dve.memset(gp_res[0:NT, D:ROW], 0.0)
                    dve.tensor_tensor(gp_res[0:NT, 0:D].rearrange("n (h c) -> n h c", h=H),
                                      gp_acc[0:NT, 0:D].rearrange("n (h c) -> n h c", h=H),
                                      gp_den[0:NT].unsqueeze(2).broadcast_to([NT, H, DH]), ALU.mult).then_inc(res_ready, 1)
                    dve.wait_ge(res_ready, j + 1)
                dve.tensor_copy(plan_i[:, 0:TILES], base_i[0:1, :]).then_inc(gp_plan, 1)

            general(dve, path)

            def shift_dst(g):
                dve.wait_ge(win_in[g.par], (g.half + 1) * PER_WIN)
                for u in range(2):
                    ins = dve.tensor_scalar(rel[:, u, :, :], dst_win[:, g.par, u, :].unsqueeze(2).broadcast_to([P, TE, H]),
                                            base[:, bass.ds(g.n * 2 + u, 1)], None,
                                            ALU.subtract)
                ins.then_inc(rel_ready, 1)

            def segments(g):
                dve.wait_ge(turn_kept, g.n + 1)
                own.did(dve.tensor_tensor(change[:, :, 1:P], turned[:, :, 1, 1:P], turned[:, :, 1, 0:P - 1], ALU.not_equal))
                own.settle()
                own.did(dve.tensor_scalar(reset[:], change[:, :, 0:P], -BIG, None, ALU.mult))
                own.settle()
                for u in range(2):
                    ins = dve.tensor_tensor_scan(scan[:, u, :], reset[:, u, :], turned[:, u, 0, :], -BIG, ALU.add, ALU.max)
                own.did(ins)
                own.settle()
                dve.tensor_tensor(scan_end[:], scan[:], change[:, :, 1:P + 1], ALU.mult).then_inc(seg_done, 1)

            def in_parts(whole, rest, parts, done):
                own.did(dve.tensor_copy(parts[0], whole))
                own.settle()
                own.did(dve.tensor_tensor(rest, whole, parts[0], ALU.subtract))
                own.settle()
                own.did(dve.tensor_copy(parts[1], rest))
                own.settle()
                dve.tensor_tensor(parts[2], rest, parts[1], ALU.subtract).then_inc(done, 1)

            def split_maxima(g):
                dve.wait_ge(back_done, g.n + 1)
                back = bankB[:, 0:4 * TH].rearrange("p (u k t h) -> p u k t h", u=2, k=2, h=H)
                dve.tensor_copy(ends[:, :, :, PARTS * H], back[:, :, 1, :, 0])
                in_parts(back[:, :, 0, :, :], ends_rest[:], [ends[:, :, :, i * H:(i + 1) * H] for i in range(PARTS)], ends_ready)

            def make_onehot(g, u):
                dve.wait_ge(rel_ready, g.n + 1)
                if not g.begins(1):
                    dve.wait_ge(onehot_kept, g.n * CHUNKS - 2 + 2 * u)
                dve.tensor_tensor(onehot_b[:, u, :, :], iota[:].unsqueeze(1).broadcast_to([P, TE, NT]),
                                  rel[:, u, :, 0:1].broadcast_to([P, TE, NT]), ALU.is_equal).then_inc(onehot_ready, 1)

            def make_onehot_t(g, c):
                dve.wait_ge(dst_row_in, g.n * 64 + c * 16 + 16)
                cols = (c % 2) * (WIN // 2)
                dve.tensor_scalar(onehot_t[0:NT, c // 2, cols:cols + WIN // 2], dst_row[0:NT, :],
                                  node[0:NT, bass.ds(g.n * 2 + c // 2, 1)], None, ALU.is_equal).then_inc(onehotT_ready, 1)

            def node_maxima(g):
                dve.wait_ge(nodes_done, g.n + 1)
                cols = bankC[0:NT, 0:2 * TE * NCOL].rearrange("n (c k) -> n c k", k=NCOL)
                flat = nval[0:NT].rearrange("n u (t h) -> n (u t) h", h=H)
                own.did(dve.tensor_scalar(nmask[0:NT], cols[:, :, PARTS * H:NCOL], -1.0, BIG, ALU.add, ALU.mult))
                own.settle()
                own.did(dve.tensor_tensor(flat, cols[:, :, 2 * H:3 * H], nmask[0:NT].broadcast_to([NT, 2 * TE, H]), ALU.add))
                for part in (1, 0):
                    own.settle()
                    own.did(dve.tensor_tensor(flat, cols[:, :, part * H:(part + 1) * H], flat, ALU.add))
                own.settle()
                own.did(dve.tensor_reduce(nmax[0:NT], nval[0:NT].rearrange("n u (t h) -> n u h t", h=H), AX.X, ALU.max))
                own.settle()
                pair_dst = edst[0:NT, bass.ds(g.n * 2, 2), :]
                own.did(dve.tensor_tensor(zmax[0:NT], pair_dst, nmax[0:NT], ALU.add))
                dve.tensor_copy(edm[0:NT, :, 0:H], pair_dst)
                own.settle()
                own.did(dve.scalar_tensor_tensor(edm[0:NT, :, H:2 * H], zmax[0:NT], SLOPE, zmax[0:NT], ALU.mult, ALU.max))
                own.settle()
                in_parts(edm[0:NT], edm_rest[0:NT], [edm_parts[0:NT, i] for i in range(PARTS)], edm_ready)

            def logits(g):
                dve.wait_ge(edge_done, g.n + 1)
                cols = bankB[:, 0:2 * TE * 2 * H].rearrange("p (c k h) -> p c k h", k=2, h=H)
                own.did(dve.tensor_tensor(z[:], esrc[:].rearrange("p u (t h) -> p (u t) h", h=H),
                                          cols[:, :, 0, :], ALU.add))
                own.settle()
                own.did(dve.scalar_tensor_tensor(lz[:], z[:], SLOPE, z[:], ALU.mult, ALU.max))
                own.settle()
                own.did(dve.tensor_tensor(lz[:], lz[:], cols[:, :, 1, :], ALU.subtract))
                own.settle()
                dve.tensor_scalar(lz[:], lz[:], 0.0, None, ALU.min).then_inc(logit_ready, 1)

            def weigh(g):
                dve.wait_ge(ex_ready, g.n + 1)
                own.did(dve.tensor_tensor(wgt[:], gath[:, g.par, :, :, D:ROW].rearrange("p u t h -> p (u t) h"),
                                          dist_win[:, g.par, :, :].rearrange("p u t -> p (u t)").unsqueeze(2).broadcast_to([P, 2 * TE, H]), ALU.mult))
                own.settle()

            def messages(g, c):
                u, cols = c // 2, (c % 2) * TC
                rows = gath[:, g.par, u, cols:cols + TC, 0:D].rearrange("p t (h c) -> p t h c", h=H)
                dve.tensor_tensor(rows, rows, wgt[:, u * TE + cols:u * TE + cols + TC, :].unsqueeze(3).broadcast_to([P, TC, H, DH]),
                                  ALU.mult).then_inc(msg_ready, 1)

            def low_part(g, c):
                dve.wait_ge(hi_ready, g.n * CHUNKS + c + 1)
                whole = gath[:, g.par, c // 2, (c % 2) * TC:(c % 2 + 1) * TC, :]
                dve.tensor_tensor(msg_lo[:], whole, msg_hi[:].bitcast(F32), ALU.subtract).then_inc(lo_ready, 1)

            def residual(g, u):
                dve.wait_ge(agg_done, g.n * CHUNKS + 2 * u + 2)
                dve.wait_ge(x_in[g.par], (g.half + 1) * 16)
                own.did(dve.tensor_scalar(rden[0:NT, u, :], bankE[u][0:NT, D:ROW], TINY, None, ALU.max))
                own.settle()
                own.did(dve.reciprocal(rden[0:NT, u, :], rden[0:NT, u, :]))
                own.settle()
                if not g.begins(2):
                    dve.wait_ge(out_stored[g.par], g.half * 16)
                own.did(dve.tensor_tensor(x1[0:NT, g.par, u, :].rearrange("n (h c) -> n h c", h=H),
                                          bankE[u][0:NT, 0:D].rearrange("n (h c) -> n h c", h=H),
                                          rden[0:NT, u, :].unsqueeze(2).broadcast_to([NT, H, DH]), ALU.mult))
                own.settle()
                own.did(dve.tensor_tensor(x1[0:NT, g.par, u, :], x1[0:NT, g.par, u, :], x_res[0:NT, g.par, u, :], ALU.add))
                own.settle()
                own.did(dve.bn_stats(stats[0:NT, u, :], x1[0:NT, g.par, u, :]))
                own.settle(alone=passed)
                dve.bn_aggr(mv[0:NT, u, :], stats[0:NT, u, :]).then_inc(var_ready, 1)

            def norm1(g, u):
                dve.wait_ge(std_ready, g.n * 2 + u + 1)
                own.did(dve.reciprocal(rstd[0:NT, u:u + 1], std[0:NT, u:u + 1]))
                own.settle()
                dve.tensor_scalar(xn[0:NT, u, :], x1[0:NT, g.par, u, :], mv[0:NT, u, 0:1], rstd[0:NT, u:u + 1],
                                  ALU.subtract, ALU.mult).then_inc(xn_ready, 1)

            def gates(f):
                dve.wait_ge(route_done, f.n + 1)
                r = bankE[1][0:NT, 0:2 * EX].rearrange("n (u e) -> n u e", u=2)
                own.did(dve.tensor_reduce(rmax[0:NT, :], r, AX.X, ALU.max))
                own.settle()
                dve.tensor_tensor(rsub[0:NT], r, rmax[0:NT, :].unsqueeze(2).broadcast_to([NT, 2, EX]), ALU.subtract
                                  ).then_inc(rsub_ready, 1)
                dve.wait_ge(rexp_ready, f.n + 1)
                own.did(dve.tensor_reduce(rsum[0:NT, :], rexp[0:NT], AX.X, ALU.add))
                own.settle()
                own.did(dve.reciprocal(rinv[0:NT, :], rsum[0:NT, :]))
                own.settle()
                dve.tensor_tensor(gate[0:NT, f.par], rexp[0:NT], rinv[0:NT, :].unsqueeze(2).broadcast_to([NT, 2, EX]), ALU.mult
                                  ).then_inc(gate_ready, 1)

            def add_y(f, k):
                dve.wait_ge(y_done, f.n * YS + k + 1)
                if k:
                    dve.wait_ge(y_added, f.n * YS + k)
                acc = x1[0:NT, f.par, :, :]
                if k == 0:
                    dve.wait_ge(gate_ready, f.n + 1)
                    dve.tensor_tensor(acc.rearrange("n u c -> n (u c)"), bankY[0:NT, :], acc.rearrange("n u c -> n (u c)"),
                                      ALU.add).then_inc(y_added, 1)
                    return
                for u in range(2):
                    ins = dve.scalar_tensor_tensor(acc[:, u, :], bankY[0:NT, u * D:(u + 1) * D], gate[0:NT, f.par, u, k - 1:k],
                                                   acc[:, u, :], ALU.mult, ALU.add)
                ins.then_inc(y_added, 1)

            setup_steps = own.base + own.count

            def body(f, g, a):
                if f is not None:
                    maxima = f.n + 2 if g is not None else f.n + 1
                    own.start(setup_steps + maxima * MAXIMA_STEPS + (f.n + 1) * SUMS_STEPS + f.n * GATE_STEPS)
                else:
                    own.start(setup_steps + (MAXIMA_STEPS if g is not None else 0))
                for s in range(EX):
                    if a is not None and s == 0:
                        shift_dst(a)
                    if f is not None and s == 0:
                        gates(f)
                    if g is not None:
                        if s == 1:
                            logits(g)
                            weigh(g)
                        if 1 <= s < 1 + CHUNKS:
                            messages(g, s - 1)
                    if f is not None and s == 2:
                        add_y(f, 0)
                    if g is not None and s == 5:
                        residual(g, 0)
                    if a is not None and s == 5:
                        split_maxima(a)
                    if g is not None and 2 <= s < 2 + CHUNKS:
                        low_part(g, s - 2)
                    if a is not None:
                        if s == 3:
                            segments(a)
                        if s in (3, 4):
                            make_onehot_t(a, s - 3)
                        if s in (5, 6):
                            make_onehot(a, s - 5)
                        if s == 6:
                            make_onehot_t(a, 2)
                    if g is not None:
                        if s == 6:
                            residual(g, 1)
                            norm1(g, 0)
                        if s == 7:
                            norm1(g, 1)
                    if a is not None and s == 7:
                        make_onehot_t(a, 3)
                        node_maxima(a)
                    if f is not None and (s >= 2 or not f.begins(1)):
                        pair, expert = before(f, s, 2)
                        add_y(pair, expert + 1)
                assert own.count == (MAXIMA_STEPS * (a is not None) + SUMS_STEPS * (g is not None)
                                     + GATE_STEPS * (f is not None)), own.count

            over_stages(dve, NP, body)
            add_y(Pair(0, NP - 1), EX - 1)
            add_y(Pair(0, NP - 1), EX)


INS = ["x", "src", "dst", "edge_attr3_1x1", "L0_gnn_W", "L0_gnn_w_att_src", "L0_gnn_w_att_dst", "L0_ffn_Wr", "L0_ffn_br",
       "L0_ffn_W1", "L0_ffn_b1", "L0_ffn_g1", "L0_ffn_be1", "L0_ffn_m1", "L0_ffn_v1", "L0_ffn_W2", "L0_ffn_b2",
       "L0_ffn_g2", "L0_ffn_be2", "L0_ffn_m2", "L0_ffn_v2", "L0_ffn_Wo", "L0_ffn_bo"]


def kernel(**inputs):
    import numpy as np
    import concourse.bacc as bacc
    from concourse.bass_utils import run_bass_kernel_spmd

    nc = bacc.Bacc("TRN2", target_bir_lowering=False, num_devices=1)
    arrays, args = {}, []
    for name in INS:
        a = np.ascontiguousarray(inputs[name])
        arrays[f"in_{name}"] = a
        args.append(nc.dram_tensor(f"in_{name}", a.shape, mybir.dt.from_np(a.dtype), kind="ExternalInput").ap())
    out = nc.dram_tensor("out", arrays["in_x"].shape, F32, kind="ExternalOutput").ap()
    gnn_ffn_kernel(nc, *args, out)
    return run_bass_kernel_spmd(nc, [arrays], core_ids=[0]).results[0]["out"]
```
